# Optimizing a Trainium2 kernel written in Bass

```python
import numpy as np
import jax
import jax.numpy as jnp

def _softmax(x, axis=-1):
    return jax.nn.softmax(x, axis=axis)

def _gelu(x):
    return jax.nn.gelu(x, approximate=True)

def _silu(x):
    return jax.nn.silu(x)

def _sigmoid(x):
    return jax.nn.sigmoid(x)

def _layernorm(x, axis=-1, eps=1e-05):
    m = jnp.mean(x, axis=axis, keepdims=True)
    v = jnp.var(x, axis=axis, keepdims=True)
    return (x - m) / jnp.sqrt(v + eps)

def _scatter_add(tgt, idx, src, axis=0):
    return tgt.at[idx].add(src)

def _segment_sum(src, seg, n):
    return jax.ops.segment_sum(src, seg, n)
kernel_name = 'mk_xattn_ffn_d4_seqx_r8_572ace'

def setup_inputs(seed: int=0):
    np.random.seed(seed)
    _w = jnp.asarray

    def _rec_inputs():
        import jax
        import jax.numpy as jnp
        _rk = jax.random.key(seed)
        x = -0.0005207 + 1.001 * jax.random.normal(jax.random.fold_in(_rk, 1), (4, 256, 128), jnp.float32)
        _lenS = 256 - jax.random.randint(jax.random.fold_in(_rk, 7), (4,), 0, max(1, 256 // 4) + 1, jnp.int32)
        _lenS2 = 512 - jax.random.randint(jax.random.fold_in(_rk, 8), (4,), 0, max(1, 512 // 4) + 1, jnp.int32)
        _ctx_1024P = jax.random.normal(jax.random.fold_in(_rk, 11), (4, 16, 128), jnp.float32)
        _ctx_1024c = jax.random.dirichlet(jax.random.fold_in(_rk, 511), 0.3 * jnp.ones((16,), jnp.float32), (4, 512))
        _ctx_1024t = jnp.einsum('bsk,bkd->bsd', _ctx_1024c, _ctx_1024P)
        _ctx_1024t = _ctx_1024t * jax.lax.rsqrt(jnp.mean(jnp.square(_ctx_1024t)) + 1e-12) * 0.953939
        ctx_1024 = 2.81802e-05 + 1.00001 * (_ctx_1024t + 0.3 * jax.random.normal(jax.random.fold_in(_rk, 611), (4, 512, 128), jnp.float32))
        _validS = jnp.arange(256)[None, :] < _lenS[:, None]
        _validS2 = jnp.arange(512)[None, :] < _lenS2[:, None]
        _causal = jnp.tril(jnp.ones((256, 256), dtype=bool))
        mask_Bx1x1xS2_bf1 = jnp.ones((4, 1, 1, 512), dtype=bool)
        mask_BxS2_bk0 = jnp.logical_not(jnp.broadcast_to(_validS2[:, :], (4, 512)))
        mask_SxS2_bk1 = jnp.broadcast_to(_validS2[0:1, :], (256, 512))
        return (x, ctx_1024, mask_Bx1x1xS2_bf1, mask_BxS2_bk0, mask_SxS2_bk1)
    x, ctx_1024, mask_Bx1x1xS2_bf1, mask_BxS2_bk0, mask_SxS2_bk1 = _rec_inputs()

    def _L0_xattn_setup():
        import jax, jax.numpy as jnp
        import numpy as np
        D_MODEL = 128
        N_HEADS = 16
        D_HEAD = D_MODEL // N_HEADS

        def _split_heads(x):
            B, L, D = x.shape
            return x.reshape(B, L, N_HEADS, D_HEAD).transpose(0, 2, 1, 3)
        key = jax.random.key(seed)
        ks = jax.random.split(key, 6)
        B, LQ, LK = (4, 64, 512)
        scale = 1.0 / np.sqrt(D_MODEL)
        return {'q_in': jax.random.normal(ks[0], (B, LQ, D_MODEL), dtype=jnp.float32), 'mem': jax.random.normal(ks[1], (B, LK, D_MODEL), dtype=jnp.float32), 'mem_mask': jnp.ones((B, 1, 1, LK), dtype=bool), 'Wq': jax.random.normal(ks[2], (D_MODEL, D_MODEL), dtype=jnp.float32) * scale, 'Wk': jax.random.normal(ks[3], (D_MODEL, D_MODEL), dtype=jnp.float32) * scale, 'Wv': jax.random.normal(ks[4], (D_MODEL, D_MODEL), dtype=jnp.float32) * scale, 'Wo': jax.random.normal(ks[5], (D_MODEL, D_MODEL), dtype=jnp.float32) * scale}
    _L0_xattn_all = _L0_xattn_setup()
    _L0_xattn_in = {k: v for k, v in _L0_xattn_all.items() if k in ('Wq', 'Wk', 'Wv', 'Wo')}
    del _L0_xattn_all

    def _L0_ffn_setup():
        import jax, jax.numpy as jnp
        import numpy as np
        B, S, D, E, H, K = (4, 256, 128, 8, 512, 2)
        EPS = 1e-06

        def _ln(x, scale, bias):
            m = jnp.mean(x, axis=-1, keepdims=True)
            v = jnp.mean(jnp.square(x - m), axis=-1, keepdims=True)
            return (x - m) * jax.lax.rsqrt(v + EPS) * scale + bias
        key = jax.random.key(seed)
        ks = jax.random.split(key, 4)
        s1 = 1.0 / np.sqrt(D)
        s2 = 1.0 / np.sqrt(H)
        return {'x': jax.random.normal(ks[0], (B, S, D), jnp.float32), 'router_ln_scale': jnp.ones((D,), jnp.float32), 'router_ln_bias': jnp.zeros((D,), jnp.float32), 'router_w': jax.random.normal(ks[1], (E, D), jnp.float32) * s1, 'router_b': jnp.zeros((E,), jnp.float32), 'expert_ln_scale': jnp.ones((E, D), jnp.float32), 'expert_ln_bias': jnp.zeros((E, D), jnp.float32), 'w1': jax.random.normal(ks[2], (E, H, D), jnp.float32) * s1, 'b1': jnp.zeros((E, H), jnp.float32), 'w2': jax.random.normal(ks[3], (E, D, H), jnp.float32) * s2, 'b2': jnp.zeros((E, D), jnp.float32)}
    _L0_ffn_all = _L0_ffn_setup()
    _L0_ffn_in = {k: v for k, v in _L0_ffn_all.items() if k in ('router_ln_scale', 'router_ln_bias', 'router_w', 'router_b', 'expert_ln_scale', 'expert_ln_bias', 'w1', 'b1', 'w2', 'b2')}
    del _L0_ffn_all

    def _L1_xattn_setup():
        import jax, jax.numpy as jnp
        import numpy as np
        DIM = 128
        HEADS = 16
        DS = 4
        key = jax.random.key(seed)
        ks = jax.random.split(key, 10)
        B, N, M = (2, 128, 512)
        s = 0.02
        return {'x': jax.random.normal(ks[0], (B, M, DIM), jnp.float32), 'l': jax.random.normal(ks[1], (B, N, DIM), jnp.float32), 'Wq': jax.random.normal(ks[2], (DIM, DIM), jnp.float32) * s, 'bq': jnp.zeros((DIM,), jnp.float32), 'Wk': jax.random.normal(ks[3], (DIM, DIM), jnp.float32) * s, 'bk': jnp.zeros((DIM,), jnp.float32), 'Wv': jax.random.normal(ks[4], (DIM, DIM), jnp.float32) * s, 'bv': jnp.zeros((DIM,), jnp.float32), 'Wo': jax.random.normal(ks[5], (DIM, DIM), jnp.float32) * s, 'bo': jnp.zeros((DIM,), jnp.float32)}
    _L1_xattn_all = _L1_xattn_setup()
    _L1_xattn_in = {k: v for k, v in _L1_xattn_all.items() if k in ('Wq', 'bq', 'Wk', 'bk', 'Wv', 'bv', 'Wo', 'bo')}
    del _L1_xattn_all

    def _L1_ffn_setup():
        import jax, jax.numpy as jnp
        import numpy as np
        D = 128
        F = 352
        E = 8
        TOP_K = 2
        key = jax.random.key(seed)
        ks = jax.random.split(key, 6)
        std = 0.02
        x = jax.random.normal(ks[0], (2, 256, D), dtype=jnp.float32)
        router_w = jax.random.normal(ks[1], (D, E), dtype=jnp.float32) * std
        w1 = jax.random.normal(ks[2], (E, D, F), dtype=jnp.float32) * std
        v1 = jax.random.normal(ks[3], (E, D, F), dtype=jnp.float32) * std
        w2 = jax.random.normal(ks[4], (E, F, D), dtype=jnp.float32) * std
        bias = jnp.zeros((D,), dtype=jnp.float32)
        return {'x': x, 'router_w': router_w, 'w1': w1, 'v1': v1, 'w2': w2, 'bias': bias}
    _L1_ffn_all = _L1_ffn_setup()
    _L1_ffn_in = {k: v for k, v in _L1_ffn_all.items() if k in ('router_w', 'w1', 'v1', 'w2', 'bias')}
    del _L1_ffn_all

    def _L2_xattn_setup():
        import jax, jax.numpy as jnp
        import numpy as np
        N_DIM = 128
        HEAD_NUM = 16
        HEAD_DIM = N_DIM // HEAD_NUM
        B, S = (4, 256)

        def _mha(x1, x2, x2_mask, attn_mask, Wq, Wk, Wv, Wo, bo):
            b, s1, _ = x1.shape
            s2 = x2.shape[1]
            q = (x1 @ Wq).reshape(b, s1, HEAD_NUM, HEAD_DIM)
            k = (x2 @ Wk).reshape(b, s2, HEAD_NUM, HEAD_DIM)
            v = (x2 @ Wv).reshape(b, s2, HEAD_NUM, HEAD_DIM)
            dots = jnp.einsum('bqhd,bkhd->bhqk', q, k) / np.sqrt(HEAD_DIM).astype(np.float32)
            dots = dots * (~x2_mask)[:, None, None, :].astype(dots.dtype)
            dots = jnp.where(attn_mask[None, None, :, :], -jnp.inf, dots)
            attn = jax.nn.softmax(dots, axis=-1)
            ctx = jnp.einsum('bhqk,bkhd->bqhd', attn, v).reshape(b, s1, N_DIM)
            return ctx @ Wo + bo
        key = jax.random.key(seed)
        ks = jax.random.split(key, 8)
        x1 = jax.random.normal(ks[0], (B, S, N_DIM), dtype=jnp.float32)
        x2 = jax.random.normal(ks[1], (B, S, N_DIM), dtype=jnp.float32)
        x2_mask = jax.random.randint(ks[2], (B, S), 0, 2).astype(bool)
        attn_mask = jnp.triu(jnp.ones((S, S), dtype=bool), k=1)
        sc = 1.0 / np.sqrt(N_DIM)
        Wq = jax.random.normal(ks[3], (N_DIM, N_DIM), dtype=jnp.float32) * sc
        Wk = jax.random.normal(ks[4], (N_DIM, N_DIM), dtype=jnp.float32) * sc
        Wv = jax.random.normal(ks[5], (N_DIM, N_DIM), dtype=jnp.float32) * sc
        Wo = jax.random.normal(ks[6], (N_DIM, N_DIM), dtype=jnp.float32) * sc
        bo = jnp.zeros((N_DIM,), dtype=jnp.float32)
        return {'x1': x1, 'x2': x2, 'x2_mask': x2_mask, 'attn_mask': attn_mask, 'Wq': Wq, 'Wk': Wk, 'Wv': Wv, 'Wo': Wo, 'bo': bo}
    _L2_xattn_all = _L2_xattn_setup()
    _L2_xattn_in = {k: v for k, v in _L2_xattn_all.items() if k in ('Wq', 'Wk', 'Wv', 'Wo', 'bo')}
    del _L2_xattn_all

    def _L2_ffn_setup():
        import jax, jax.numpy as jnp
        import numpy as np
        JITTER_EPS = 0.01
        NEG_INF = -jnp.inf

        def sparsemixer_eval(scores, jitter_eps):
            m1 = jnp.max(scores, axis=-1, keepdims=True)
            ind1 = jnp.argmax(scores, axis=-1)
            factor1 = jnp.maximum(jnp.abs(scores), m1)
            mask1 = jax.lax.stop_gradient((m1 - scores) / factor1 > 2.0 * jitter_eps)
            gates1 = jax.nn.softmax(jnp.where(mask1, NEG_INF, scores), axis=-1)
            mult1 = jnp.take_along_axis(gates1, ind1[:, None], axis=-1)[:, 0]
            E = scores.shape[-1]
            onehot1 = ind1[:, None] == jnp.arange(E)[None, :]
            masked_scores = jnp.where(onehot1, NEG_INF, scores)
            m2 = jnp.max(masked_scores, axis=-1, keepdims=True)
            ind2 = jnp.argmax(masked_scores, axis=-1)
            factor2 = jnp.maximum(jnp.abs(scores), m2)
            mask2 = jax.lax.stop_gradient((m2 - scores) / factor2 > 2.0 * jitter_eps)
            gates2 = jax.nn.softmax(jnp.where(mask2, NEG_INF, masked_scores), axis=-1)
            mult2 = jnp.take_along_axis(gates2, ind2[:, None], axis=-1)[:, 0]
            multiplier = jnp.stack([mult1, mult2], axis=-1)
            selected = jnp.stack([ind1, ind2], axis=-1)
            return (multiplier, selected)
        key = jax.random.key(seed)
        k0, k1, k2, k3, k4 = jax.random.split(key, 5)
        B, S, H, F, E = (2, 128, 128, 256, 8)
        scale = 0.02
        return {'hidden_states': jax.random.normal(k0, (B, S, H), dtype=jnp.float32), 'router_w': jax.random.normal(k1, (E, H), dtype=jnp.float32) * scale, 'w_gate': jax.random.normal(k2, (E, F, H), dtype=jnp.float32) * scale, 'w_up': jax.random.normal(k3, (E, F, H), dtype=jnp.float32) * scale, 'w_down': jax.random.normal(k4, (E, H, F), dtype=jnp.float32) * scale}
    _L2_ffn_all = _L2_ffn_setup()
    _L2_ffn_in = {k: v for k, v in _L2_ffn_all.items() if k in ('router_w', 'w_gate', 'w_up', 'w_down')}
    del _L2_ffn_all

    def _L3_xattn_setup():
        import jax, jax.numpy as jnp
        import numpy as np
        D_MODEL = 128
        NUM_HEADS = 16
        DEPTH = D_MODEL // NUM_HEADS
        B, S = (4, 256)

        def _split_heads(x):
            b, s, _ = x.shape
            return x.reshape(b, s, NUM_HEADS, DEPTH).transpose(0, 2, 1, 3)
        key = jax.random.key(seed)
        ks = jax.random.split(key, 11)
        scale = 1.0 / np.sqrt(D_MODEL)
        inp = {'q': jax.random.normal(ks[0], (B, S, D_MODEL), dtype=jnp.float32), 'k': jax.random.normal(ks[1], (B, S, D_MODEL), dtype=jnp.float32), 'v': jax.random.normal(ks[2], (B, S, D_MODEL), dtype=jnp.float32), 'wq_w': jax.random.normal(ks[3], (D_MODEL, D_MODEL), dtype=jnp.float32) * scale, 'wq_b': jax.random.normal(ks[4], (D_MODEL,), dtype=jnp.float32) * scale, 'wk_w': jax.random.normal(ks[5], (D_MODEL, D_MODEL), dtype=jnp.float32) * scale, 'wk_b': jax.random.normal(ks[6], (D_MODEL,), dtype=jnp.float32) * scale, 'wv_w': jax.random.normal(ks[7], (D_MODEL, D_MODEL), dtype=jnp.float32) * scale, 'wv_b': jax.random.normal(ks[8], (D_MODEL,), dtype=jnp.float32) * scale, 'proj_w': jax.random.normal(ks[9], (D_MODEL, D_MODEL), dtype=jnp.float32) * scale, 'proj_b': jax.random.normal(ks[10], (D_MODEL,), dtype=jnp.float32) * scale}
        return inp
    _L3_xattn_all = _L3_xattn_setup()
    _L3_xattn_in = {k: v for k, v in _L3_xattn_all.items() if k in ('wq_w', 'wq_b', 'wk_w', 'wk_b', 'wv_w', 'wv_b', 'proj_w', 'proj_b')}
    del _L3_xattn_all

    def _L3_ffn_setup():
        import jax, jax.numpy as jnp
        import numpy as np
        DIM, HEADS, EXPERTS, DFF = (128, 16, 8, 512)
        EPS = 1e-05

        def layernorm(x, g, b):
            mu = jnp.mean(x, -1, keepdims=True)
            var = jnp.mean(jnp.square(x - mu), -1, keepdims=True)
            return (x - mu) * jax.lax.rsqrt(var + EPS) * g + b
        key = jax.random.key(seed)
        ks = jax.random.split(key, 12)
        s = lambda d: 1.0 / np.sqrt(d)
        return {'x': jax.random.normal(ks[0], (2, 256, DIM), jnp.float32), 'conv_w': jax.random.normal(ks[1], (DIM, DIM, 3), jnp.float32) * s(DIM * 3), 'conv_b': jnp.zeros((DIM,), jnp.float32), 'wqkv': jax.random.normal(ks[2], (3 * DIM, DIM), jnp.float32) * s(DIM), 'bqkv': jnp.zeros((3 * DIM,), jnp.float32), 'wo': jax.random.normal(ks[3], (DIM, DIM), jnp.float32) * s(DIM), 'bo': jnp.zeros((DIM,), jnp.float32), 'ln1_g': jnp.ones((DIM,), jnp.float32), 'ln1_b': jnp.zeros((DIM,), jnp.float32), 'gate_w': jax.random.normal(ks[4], (DIM, EXPERTS), jnp.float32) * s(DIM), 'gate_b': jnp.zeros((EXPERTS,), jnp.float32), 'w1': jax.random.normal(ks[5], (EXPERTS, DIM, DFF), jnp.float32) * s(DIM), 'b1': jnp.zeros((EXPERTS, DFF), jnp.float32), 'w2': jax.random.normal(ks[6], (EXPERTS, DFF, DIM), jnp.float32) * s(DFF), 'b2': jnp.zeros((EXPERTS, DIM), jnp.float32), 'ln2_g': jnp.ones((DIM,), jnp.float32), 'ln2_b': jnp.zeros((DIM,), jnp.float32)}
    _L3_ffn_all = _L3_ffn_setup()
    _L3_ffn_in = {k: v for k, v in _L3_ffn_all.items() if k in ('conv_w', 'conv_b', 'wqkv', 'bqkv', 'wo', 'bo', 'ln1_g', 'ln1_b', 'gate_w', 'gate_b', 'w1', 'b1', 'w2', 'b2', 'ln2_g', 'ln2_b')}
    del _L3_ffn_all
    return {'x': x, 'ctx_1024': ctx_1024, 'mask_Bx1x1xS2_bf1': mask_Bx1x1xS2_bf1, 'mask_BxS2_bk0': mask_BxS2_bk0, 'mask_SxS2_bk1': mask_SxS2_bk1, 'L0_xattn_Wq': _L0_xattn_in['Wq'], 'L0_xattn_Wk': _L0_xattn_in['Wk'], 'L0_xattn_Wv': _L0_xattn_in['Wv'], 'L0_xattn_Wo': _L0_xattn_in['Wo'], 'L0_ffn_router_ln_scale': _L0_ffn_in['router_ln_scale'], 'L0_ffn_router_ln_bias': _L0_ffn_in['router_ln_bias'], 'L0_ffn_router_w': _L0_ffn_in['router_w'], 'L0_ffn_router_b': _L0_ffn_in['router_b'], 'L0_ffn_expert_ln_scale': _L0_ffn_in['expert_ln_scale'], 'L0_ffn_expert_ln_bias': _L0_ffn_in['expert_ln_bias'], 'L0_ffn_w1': _L0_ffn_in['w1'], 'L0_ffn_b1': _L0_ffn_in['b1'], 'L0_ffn_w2': _L0_ffn_in['w2'], 'L0_ffn_b2': _L0_ffn_in['b2'], 'L1_xattn_Wq': _L1_xattn_in['Wq'], 'L1_xattn_bq': _L1_xattn_in['bq'], 'L1_xattn_Wk': _L1_xattn_in['Wk'], 'L1_xattn_bk': _L1_xattn_in['bk'], 'L1_xattn_Wv': _L1_xattn_in['Wv'], 'L1_xattn_bv': _L1_xattn_in['bv'], 'L1_xattn_Wo': _L1_xattn_in['Wo'], 'L1_xattn_bo': _L1_xattn_in['bo'], 'L1_ffn_router_w': _L1_ffn_in['router_w'], 'L1_ffn_w1': _L1_ffn_in['w1'], 'L1_ffn_v1': _L1_ffn_in['v1'], 'L1_ffn_w2': _L1_ffn_in['w2'], 'L1_ffn_bias': _L1_ffn_in['bias'], 'L2_xattn_Wq': _L2_xattn_in['Wq'], 'L2_xattn_Wk': _L2_xattn_in['Wk'], 'L2_xattn_Wv': _L2_xattn_in['Wv'], 'L2_xattn_Wo': _L2_xattn_in['Wo'], 'L2_xattn_bo': _L2_xattn_in['bo'], 'L2_ffn_router_w': _L2_ffn_in['router_w'], 'L2_ffn_w_gate': _L2_ffn_in['w_gate'], 'L2_ffn_w_up': _L2_ffn_in['w_up'], 'L2_ffn_w_down': _L2_ffn_in['w_down'], 'L3_xattn_wq_w': _L3_xattn_in['wq_w'], 'L3_xattn_wq_b': _L3_xattn_in['wq_b'], 'L3_xattn_wk_w': _L3_xattn_in['wk_w'], 'L3_xattn_wk_b': _L3_xattn_in['wk_b'], 'L3_xattn_wv_w': _L3_xattn_in['wv_w'], 'L3_xattn_wv_b': _L3_xattn_in['wv_b'], 'L3_xattn_proj_w': _L3_xattn_in['proj_w'], 'L3_xattn_proj_b': _L3_xattn_in['proj_b'], 'L3_ffn_conv_w': _L3_ffn_in['conv_w'], 'L3_ffn_conv_b': _L3_ffn_in['conv_b'], 'L3_ffn_wqkv': _L3_ffn_in['wqkv'], 'L3_ffn_bqkv': _L3_ffn_in['bqkv'], 'L3_ffn_wo': _L3_ffn_in['wo'], 'L3_ffn_bo': _L3_ffn_in['bo'], 'L3_ffn_ln1_g': _L3_ffn_in['ln1_g'], 'L3_ffn_ln1_b': _L3_ffn_in['ln1_b'], 'L3_ffn_gate_w': _L3_ffn_in['gate_w'], 'L3_ffn_gate_b': _L3_ffn_in['gate_b'], 'L3_ffn_w1': _L3_ffn_in['w1'], 'L3_ffn_b1': _L3_ffn_in['b1'], 'L3_ffn_w2': _L3_ffn_in['w2'], 'L3_ffn_b2': _L3_ffn_in['b2'], 'L3_ffn_ln2_g': _L3_ffn_in['ln2_g'], 'L3_ffn_ln2_b': _L3_ffn_in['ln2_b']}

def reference(x, ctx_1024, mask_Bx1x1xS2_bf1, mask_BxS2_bk0, mask_SxS2_bk1, L0_xattn_Wq, L0_xattn_Wk, L0_xattn_Wv, L0_xattn_Wo, L0_ffn_router_ln_scale, L0_ffn_router_ln_bias, L0_ffn_router_w, L0_ffn_router_b, L0_ffn_expert_ln_scale, L0_ffn_expert_ln_bias, L0_ffn_w1, L0_ffn_b1, L0_ffn_w2, L0_ffn_b2, L1_xattn_Wq, L1_xattn_bq, L1_xattn_Wk, L1_xattn_bk, L1_xattn_Wv, L1_xattn_bv, L1_xattn_Wo, L1_xattn_bo, L1_ffn_router_w, L1_ffn_w1, L1_ffn_v1, L1_ffn_w2, L1_ffn_bias, L2_xattn_Wq, L2_xattn_Wk, L2_xattn_Wv, L2_xattn_Wo, L2_xattn_bo, L2_ffn_router_w, L2_ffn_w_gate, L2_ffn_w_up, L2_ffn_w_down, L3_xattn_wq_w, L3_xattn_wq_b, L3_xattn_wk_w, L3_xattn_wk_b, L3_xattn_wv_w, L3_xattn_wv_b, L3_xattn_proj_w, L3_xattn_proj_b, L3_ffn_conv_w, L3_ffn_conv_b, L3_ffn_wqkv, L3_ffn_bqkv, L3_ffn_wo, L3_ffn_bo, L3_ffn_ln1_g, L3_ffn_ln1_b, L3_ffn_gate_w, L3_ffn_gate_b, L3_ffn_w1, L3_ffn_b1, L3_ffn_w2, L3_ffn_b2, L3_ffn_ln2_g, L3_ffn_ln2_b):
    import jax
    import jax.numpy as jnp

    def _L0_xattn_ref(q_in, mem, mem_mask, Wq, Wk, Wv, Wo):
        import jax, jax.numpy as jnp
        import numpy as np
        D_MODEL = 128
        N_HEADS = 16
        D_HEAD = D_MODEL // N_HEADS

        def _split_heads(x):
            B, L, D = x.shape
            return x.reshape(B, L, N_HEADS, D_HEAD).transpose(0, 2, 1, 3)
        q = _split_heads(q_in @ Wq.T)
        k = _split_heads(mem @ Wk.T)
        v = _split_heads(mem @ Wv.T)
        scores = jnp.einsum('bhqd,bhkd->bhqk', q, k) / jnp.sqrt(jnp.float32(D_HEAD))
        scores = jnp.where(mem_mask, scores, -jnp.inf)
        attn = jax.nn.softmax(scores, axis=-1)
        out = jnp.einsum('bhqk,bhkd->bhqd', attn, v)
        B, H, LQ, Dh = out.shape
        out = out.transpose(0, 2, 1, 3).reshape(B, LQ, H * Dh)
        return out @ Wo.T

    def _L0_ffn_ref(x, router_ln_scale, router_ln_bias, router_w, router_b, expert_ln_scale, expert_ln_bias, w1, b1, w2, b2):
        import jax, jax.numpy as jnp
        import numpy as np
        B, S, D, E, H, K = (4, 256, 128, 8, 512, 2)
        EPS = 1e-06

        def _ln(x, scale, bias):
            m = jnp.mean(x, axis=-1, keepdims=True)
            v = jnp.mean(jnp.square(x - m), axis=-1, keepdims=True)
            return (x - m) * jax.lax.rsqrt(v + EPS) * scale + bias
        orig_shape = x.shape
        xf = x.reshape(-1, D)
        T = xf.shape[0]
        logits = _ln(xf, router_ln_scale, router_ln_bias) @ router_w.T + router_b
        probs = jax.nn.softmax(logits, axis=-1)
        topw, topi = jax.lax.top_k(probs, K)
        topw = topw / jnp.sum(topw, axis=-1, keepdims=True)
        gates = jnp.zeros((T, E), xf.dtype).at[jnp.arange(T)[:, None], topi].set(topw)

        def expert(ls, lb, W1, B1, W2, B2):
            h = jax.nn.gelu(_ln(xf, ls, lb) @ W1.T + B1, approximate=False)
            return h @ W2.T + B2
        ys = jax.vmap(expert)(expert_ln_scale, expert_ln_bias, w1, b1, w2, b2)
        out = jnp.einsum('te,etd->td', gates, ys)
        return out.reshape(orig_shape)

    def _L1_xattn_ref(x, l, Wq, bq, Wk, bk, Wv, bv, Wo, bo):
        import jax, jax.numpy as jnp
        import numpy as np
        DIM = 128
        HEADS = 16
        DS = 4
        B, N, _ = l.shape
        M = x.shape[1]
        d = DIM // HEADS

        def split_heads(t):
            return t.reshape(t.shape[0], t.shape[1], HEADS, d).transpose(0, 2, 1, 3)
        q = split_heads(l @ Wq.T + bq)
        k = split_heads(x @ Wk.T + bk)
        v = split_heads(x @ Wv.T + bv)
        scores = jnp.einsum('bhid,bhjd->bhij', q, k) * d ** (-0.5)
        ii = jnp.arange(N)[:, None]
        jj = jnp.arange(M)[None, :]
        allowed = jj // DS <= ii
        scores = jnp.where(allowed[None, None], scores, -jnp.inf)
        attn = jax.nn.softmax(scores, axis=-1)
        out = jnp.einsum('bhij,bhjd->bhid', attn, v)
        out = out.transpose(0, 2, 1, 3).reshape(B, N, DIM)
        return out @ Wo.T + bo

    def _L1_ffn_ref(x, router_w, w1, v1, w2, bias):
        import jax, jax.numpy as jnp
        import numpy as np
        D = 128
        F = 352
        E = 8
        TOP_K = 2
        B, S, d = x.shape
        xt = x.reshape(B * S, d)
        scores = jax.nn.softmax(xt @ router_w, axis=-1)
        expert_weights, expert_idx = jax.lax.top_k(scores, TOP_K)
        h = jax.nn.gelu(jnp.einsum('td,edf->tef', xt, w1), approximate=False) * jnp.einsum('td,edf->tef', xt, v1)
        y = jnp.einsum('tef,efd->ted', h, w2)
        yk = jnp.take_along_axis(y, expert_idx[:, :, None], axis=1)
        out = jnp.sum(expert_weights[:, :, None] * yk, axis=1) + bias
        return out.reshape(B, S, d)

    def _L2_xattn_ref(x1, x2, x2_mask, attn_mask, Wq, Wk, Wv, Wo, bo):
        import jax, jax.numpy as jnp
        import numpy as np
        N_DIM = 128
        HEAD_NUM = 16
        HEAD_DIM = N_DIM // HEAD_NUM
        B, S = (4, 256)

        def _mha(x1, x2, x2_mask, attn_mask, Wq, Wk, Wv, Wo, bo):
            b, s1, _ = x1.shape
            s2 = x2.shape[1]
            q = (x1 @ Wq).reshape(b, s1, HEAD_NUM, HEAD_DIM)
            k = (x2 @ Wk).reshape(b, s2, HEAD_NUM, HEAD_DIM)
            v = (x2 @ Wv).reshape(b, s2, HEAD_NUM, HEAD_DIM)
            dots = jnp.einsum('bqhd,bkhd->bhqk', q, k) / np.sqrt(HEAD_DIM).astype(np.float32)
            dots = dots * (~x2_mask)[:, None, None, :].astype(dots.dtype)
            dots = jnp.where(attn_mask[None, None, :, :], -jnp.inf, dots)
            attn = jax.nn.softmax(dots, axis=-1)
            ctx = jnp.einsum('bhqk,bkhd->bqhd', attn, v).reshape(b, s1, N_DIM)
            return ctx @ Wo + bo
        return _mha(x1, x2, x2_mask, attn_mask, Wq, Wk, Wv, Wo, bo)

    def _L2_ffn_ref(hidden_states, router_w, w_gate, w_up, w_down):
        import jax, jax.numpy as jnp
        import numpy as np
        JITTER_EPS = 0.01
        NEG_INF = -jnp.inf

        def sparsemixer_eval(scores, jitter_eps):
            m1 = jnp.max(scores, axis=-1, keepdims=True)
            ind1 = jnp.argmax(scores, axis=-1)
            factor1 = jnp.maximum(jnp.abs(scores), m1)
            mask1 = jax.lax.stop_gradient((m1 - scores) / factor1 > 2.0 * jitter_eps)
            gates1 = jax.nn.softmax(jnp.where(mask1, NEG_INF, scores), axis=-1)
            mult1 = jnp.take_along_axis(gates1, ind1[:, None], axis=-1)[:, 0]
            E = scores.shape[-1]
            onehot1 = ind1[:, None] == jnp.arange(E)[None, :]
            masked_scores = jnp.where(onehot1, NEG_INF, scores)
            m2 = jnp.max(masked_scores, axis=-1, keepdims=True)
            ind2 = jnp.argmax(masked_scores, axis=-1)
            factor2 = jnp.maximum(jnp.abs(scores), m2)
            mask2 = jax.lax.stop_gradient((m2 - scores) / factor2 > 2.0 * jitter_eps)
            gates2 = jax.nn.softmax(jnp.where(mask2, NEG_INF, masked_scores), axis=-1)
            mult2 = jnp.take_along_axis(gates2, ind2[:, None], axis=-1)[:, 0]
            multiplier = jnp.stack([mult1, mult2], axis=-1)
            selected = jnp.stack([ind1, ind2], axis=-1)
            return (multiplier, selected)
        B, S, H = hidden_states.shape
        E = router_w.shape[0]
        x = hidden_states.reshape(-1, H)
        T = x.shape[0]
        logits = x @ router_w.T
        routing_weights, selected = sparsemixer_eval(logits, JITTER_EPS)
        tok = jnp.arange(T)
        dense_w = jnp.zeros((T, E), dtype=x.dtype)
        dense_w = dense_w.at[tok, selected[:, 0]].add(routing_weights[:, 0])
        dense_w = dense_w.at[tok, selected[:, 1]].add(routing_weights[:, 1])
        out = jnp.zeros_like(x)
        for e in range(E):
            h = jax.nn.silu(x @ w_gate[e].T) * (x @ w_up[e].T)
            out = out + dense_w[:, e:e + 1] * (h @ w_down[e].T)
        return out.reshape(B, S, H)

    def _L3_xattn_ref(q, k, v, wq_w, wq_b, wk_w, wk_b, wv_w, wv_b, proj_w, proj_b):
        import jax, jax.numpy as jnp
        import numpy as np
        D_MODEL = 128
        NUM_HEADS = 16
        DEPTH = D_MODEL // NUM_HEADS
        B, S = (4, 256)

        def _split_heads(x):
            b, s, _ = x.shape
            return x.reshape(b, s, NUM_HEADS, DEPTH).transpose(0, 2, 1, 3)
        qh = _split_heads(q @ wq_w.T + wq_b)
        kh = _split_heads(k @ wk_w.T + wk_b)
        vh = _split_heads(v @ wv_w.T + wv_b)
        scores = jnp.einsum('bhqd,bhkd->bhqk', qh, kh) / jnp.sqrt(jnp.float32(DEPTH))
        attn = jax.nn.softmax(scores, axis=-1)
        ctx = jnp.einsum('bhqk,bhkd->bhqd', attn, vh)
        ctx = ctx.transpose(0, 2, 1, 3).reshape(q.shape[0], q.shape[1], D_MODEL)
        return ctx @ proj_w.T + proj_b

    def _L3_ffn_ref(x, conv_w, conv_b, wqkv, bqkv, wo, bo, ln1_g, ln1_b, gate_w, gate_b, w1, b1, w2, b2, ln2_g, ln2_b):
        import jax, jax.numpy as jnp
        import numpy as np
        DIM, HEADS, EXPERTS, DFF = (128, 16, 8, 512)
        EPS = 1e-05

        def layernorm(x, g, b):
            mu = jnp.mean(x, -1, keepdims=True)
            var = jnp.mean(jnp.square(x - mu), -1, keepdims=True)
            return (x - mu) * jax.lax.rsqrt(var + EPS) * g + b
        B, S, D = x.shape
        H, dh = (HEADS, D // HEADS)
        xt = jnp.transpose(x, (0, 2, 1))
        xt = jax.lax.conv_general_dilated(xt, conv_w, (1,), [(1, 1)], dimension_numbers=('NCH', 'OIH', 'NCH'))
        x = jnp.transpose(xt + conv_b[None, :, None], (0, 2, 1))
        qkv = x @ wqkv.T + bqkv
        q, k, v = jnp.split(qkv, 3, axis=-1)
        q = q.reshape(B, S, H, dh).transpose(0, 2, 1, 3)
        k = k.reshape(B, S, H, dh).transpose(0, 2, 1, 3)
        v = v.reshape(B, S, H, dh).transpose(0, 2, 1, 3)
        scores = jnp.einsum('bhqd,bhkd->bhqk', q, k) / jnp.sqrt(jnp.float32(dh))
        attn = jax.nn.softmax(scores, axis=-1)
        ctx = jnp.einsum('bhqk,bhkd->bhqd', attn, v)
        ctx = ctx.transpose(0, 2, 1, 3).reshape(B, S, D)
        attn_out = ctx @ wo.T + bo
        x = layernorm(x + attn_out, ln1_g, ln1_b)
        probs = jax.nn.softmax(x @ gate_w + gate_b, axis=-1)
        h = jax.nn.relu(jnp.einsum('bsd,edf->bsef', x, w1) + b1)
        y = jnp.einsum('bsef,efd->bsed', h, w2) + b2
        moe_out = jnp.einsum('bse,bsed->bsd', probs, y)
        x = layernorm(x + moe_out, ln2_g, ln2_b)
        return x
    x = x + _L0_xattn_ref(_layernorm(x, axis=-1), ctx_1024, mask_Bx1x1xS2_bf1, L0_xattn_Wq, L0_xattn_Wk, L0_xattn_Wv, L0_xattn_Wo)
    x = x + _L0_ffn_ref(_layernorm(x, axis=-1), L0_ffn_router_ln_scale, L0_ffn_router_ln_bias, L0_ffn_router_w, L0_ffn_router_b, L0_ffn_expert_ln_scale, L0_ffn_expert_ln_bias, L0_ffn_w1, L0_ffn_b1, L0_ffn_w2, L0_ffn_b2)
    x = x + _L1_xattn_ref(ctx_1024, _layernorm(x, axis=-1), L1_xattn_Wq, L1_xattn_bq, L1_xattn_Wk, L1_xattn_bk, L1_xattn_Wv, L1_xattn_bv, L1_xattn_Wo, L1_xattn_bo)
    x = x + _L1_ffn_ref(_layernorm(x, axis=-1), L1_ffn_router_w, L1_ffn_w1, L1_ffn_v1, L1_ffn_w2, L1_ffn_bias)
    x = x + _L2_xattn_ref(_layernorm(x, axis=-1), ctx_1024, mask_BxS2_bk0, mask_SxS2_bk1, L2_xattn_Wq, L2_xattn_Wk, L2_xattn_Wv, L2_xattn_Wo, L2_xattn_bo)
    x = x + _L2_ffn_ref(_layernorm(x, axis=-1), L2_ffn_router_w, L2_ffn_w_gate, L2_ffn_w_up, L2_ffn_w_down)
    x = x + _L3_xattn_ref(_layernorm(x, axis=-1), ctx_1024, ctx_1024, L3_xattn_wq_w, L3_xattn_wq_b, L3_xattn_wk_w, L3_xattn_wk_b, L3_xattn_wv_w, L3_xattn_wv_b, L3_xattn_proj_w, L3_xattn_proj_b)
    x = x + _L3_ffn_ref(_layernorm(x, axis=-1), L3_ffn_conv_w, L3_ffn_conv_b, L3_ffn_wqkv, L3_ffn_bqkv, L3_ffn_wo, L3_ffn_bo, L3_ffn_ln1_g, L3_ffn_ln1_b, L3_ffn_gate_w, L3_ffn_gate_b, L3_ffn_w1, L3_ffn_b1, L3_ffn_w2, L3_ffn_b2, L3_ffn_ln2_g, L3_ffn_ln2_b)
    return x

_drawn_inputs = setup_inputs


def setup_inputs(seed=0):
    import zlib

    import numpy as np

    out = dict(_drawn_inputs(seed))
    spreads = {'L0_ffn_router_ln_scale': (1.0, 0.2),
     'L0_ffn_router_ln_bias': (0.0, 0.1),
     'L0_ffn_router_b': (0.0, 0.1),
     'L0_ffn_expert_ln_scale': (1.0, 0.2),
     'L0_ffn_expert_ln_bias': (0.0, 0.1),
     'L0_ffn_b1': (0.0, 0.1),
     'L0_ffn_b2': (0.0, 0.1),
     'L1_xattn_bq': (0.0, 0.8),
     'L1_xattn_bk': (0.0, 2.0),
     'L1_xattn_bv': (0.0, 0.494),
     'L1_xattn_bo': (0.0, 0.1),
     'L1_ffn_bias': (0.0, 0.1),
     'L2_xattn_bo': (0.0, 0.1),
     'L3_ffn_conv_b': (0.0, 0.412),
     'L3_ffn_bqkv': (0.0, 0.544),
     'L3_ffn_bo': (0.0, 0.499),
     'L3_ffn_ln1_g': (1.0, 0.565),
     'L3_ffn_ln1_b': (0.0, 0.518),
     'L3_ffn_gate_b': (0.0, 2.0),
     'L3_ffn_b1': (0.0, 1.86),
     'L3_ffn_b2': (0.0, 1.28),
     'L3_ffn_ln2_g': (1.0, 0.585),
     'L3_ffn_ln2_b': (0.0, 0.57)}
    factors = {'L1_xattn_Wq': 8.0,
     'L1_xattn_Wk': 8.0,
     'L1_xattn_Wv': 2.989,
     'L1_ffn_router_w': 8.0,
     'L1_ffn_w1': 8.0,
     'L1_ffn_v1': 8.0,
     'L1_ffn_w2': 8.0,
     'L2_ffn_router_w': 8.0,
     'L2_ffn_w_gate': 7.227,
     'L2_ffn_w_up': 7.19,
     'L2_ffn_w_down': 7.15,
     'L3_xattn_wq_b': 18.724,
     'L3_xattn_wk_b': 64.0,
     'L3_xattn_wv_b': 3.989,
     'L3_xattn_proj_b': 3.865}
    for name, (base, spread) in spreads.items():
        noise = np.random.default_rng([zlib.crc32(name.encode()), seed]).standard_normal(out[name].shape)
        drawn = base * np.exp(spread * noise) if base else spread * noise
        out[name] = jnp.asarray(drawn.astype(out[name].dtype))
    for name, factor in factors.items():
        out[name] = (out[name] * factor).astype(out[name].dtype)
    return out
```

```python
from contextlib import ExitStack

import numpy as np

import concourse.bass as bass
from concourse import mybir

F32 = mybir.dt.float32
BF16 = mybir.dt.bfloat16
U8 = mybir.dt.uint8
U32 = mybir.dt.uint32
ALU = mybir.AluOpType
ACT = mybir.ActivationFunctionType
AX = mybir.AxisListType

P = 128
B, SQ, SK = 4, 256, 512
T = B * SQ
NT = T // P
TH = T // 2
TK = B * SK
HEADS, DH = 16, 8
NP = HEADS // 2
GROUP = 4
NG = HEADS // GROUP
NE = 8
SCALE = float(DH) ** -0.5
NEG = -1.0e30
EPS, EPS_IN = 1e-5, 1e-6
VW = 9 * HEADS + 24
CW = 6 * DH
MASK_ROW, SHIFT_ROW = 2 * CW, 2 * CW + 1
LOOK = 2

COLS = {}
_n = 0
for _name, _w in [(f"bq{a}", 1) for a in range(5)] + [(f"bk{a}", 1) for a in range(5)] + \
        [(f"bv{a}", 1) for a in range(5)] + \
        [("conv_b", 1), ("ffn1_bias", 1), ("rln_s", 1), ("rln_b", 1), ("eln_s", NE), ("eln_b", NE),
         ("b1_0", 4 * NE), ("b1_3", 4 * NE)]:
    COLS[_name] = (_n, _w)
    _n += _w
NCOLS = _n
ROWS = {}
_n = 0
for _name, _w in [(f"bo{a}", P) for a in range(5)] + \
        [("router_b0", NE), ("router_b3", NE), ("ln1_g", P), ("ln1_b", P), ("ln2_g", P), ("ln2_b", P)]:
    ROWS[_name] = (_n, _w)
    _n += _w
NROWS = _n
HID = [512, 352, 256, 512]
EW = [4 * P + 4 * P, 2 * 352 + 3 * P, 2 * 256 + 2 * P, 4 * P + 4 * P]


def signals(nc, phase, names, before):
    s = {n: nc.alloc_semaphore(f"{phase}_{n}") for n in names.split()}
    if before:
        nc.clear_and_free_semaphores(before.pop())
    before.append(list(s.values()))
    return s


class Chain:

    def __init__(self, eng, sem):
        self.eng, self.sem, self.n = eng, sem, 0

    def __call__(self, ins):
        self.n += 1
        ins.then_inc(self.sem, 1)
        self.eng.wait_ge(self.sem, self.n)


def build(nc, d, out):
    ctx = ExitStack()
    with ctx:
        def sb(name, shape, dt=F32):
            return ctx.enter_context(nc.sbuf_tensor(name, shape, dt))

        X = sb("X", [P, NT, P])
        XN = sb("XN", [P, NT, P])
        XNT = sb("XNT", [P, T])
        CTX = sb("CTX", [P, TK])
        KOP = sb("KOP", [P, 4, NP, 512], BF16)
        QOP = sb("QOP", [P, 2, HEADS, TH], BF16)
        V = sb("V", [P, TK // P, VW])
        SHARED = sb("SHARED", [P, 8 * 1024])
        PT = SHARED[:, :].rearrange("p (u n) -> p u n", u=8)
        GB = PT
        XPAD = SHARED[:, 0:B * (SQ + 2)].rearrange("p (b n) -> p b n", b=B)
        HI = sb("HI", [P, 2, 512], BF16)
        MID = sb("MID", [P, 2, 512], BF16)
        LO = sb("LO", [P, 2, 512], BF16)
        REST = sb("REST", [P, 2, 512])
        KEEP = sb("KEEP", [P, TK], U8)
        WA = sb("WA", [P, 5, 4, P])
        WCONV = sb("WCONV", [P, 3, P])
        WR = sb("WR", [P, 4, NE])
        B2 = sb("B2", [NE, 2, P])
        C = sb("C", [P, NCOLS])
        R = sb("R", [P, NROWS])
        W = sb("W", [P, 2, max(EW)])
        H = sb("H", [P, 3 * 1024])
        U = sb("U", [P, 2, T])
        KKEPT = H[:, 2048:3072].rearrange("p (i n) -> p i n", i=2)
        masks = U[:, 0, :].bitcast(U8)
        M0 = masks[:, 0:TK]
        M2 = masks[:, TK:TK + 2 * SK].rearrange("p (t k) -> p t k", t=2)
        M2T = masks[:, TK + 2 * SK:TK + 2 * SK + 4 * SQ].rearrange("p (t k) -> p t k", t=4)
        ACC = sb("ACC", [P, T])
        OT = sb("OT", [P, 2, 256])
        ON = sb("ON", [P, 2, 2, P])
        CT = sb("CT", [P, 2, 256])
        RC = sb("RC", [P, 2, 2, GROUP])
        NM = sb("NM", [P, 4, 2, GROUP])
        NG32 = sb("NG32", [P, 4, 2, GROUP])
        HL = sb("HL", [P, 4, 2, 2, GROUP], BF16)
        SH = sb("SH", [2 * GROUP, 2, 256], BF16)
        IDF = sb("IDF", [P, P])
        IDB = sb("IDB", [P, P], BF16)
        NEGC = sb("NEGC", [P, SK], BF16)
        STAIR = sb("STAIR", [P, 32], BF16)
        NEG2 = sb("NEG2", [P, 2, SK], BF16)
        NEG2T = sb("NEG2T", [P, 4, SQ], BF16)
        ST8 = sb("ST8", [P, NT, 6])
        MV = sb("MV", [P, NT, 2])
        VE = sb("VE", [P, NT])
        HALF = sb("HALF", [P, NT])
        RSTD = sb("RSTD", [P, NT])
        LG = sb("LG", [P, NT, NE])
        MX = sb("MX", [P, NT, NE])
        IX = sb("IX", [P, NT, NE], U32)
        IXF = sb("IXF", [P, NT, NE])
        IOTA = sb("IOTA", [P, NT, NE])
        GA = [sb(f"GA{i}", [P, NT, NE]) for i in range(8)]
        G1 = [sb(f"G1{i}", [P, NT]) for i in range(2)]
        GT = ACC[0:NE, :]

        PS = [ctx.enter_context(nc.psum_tensor(f"PS{i}", [P, 1024], F32)) for i in range(4)]

        q_parts = nc.dram_tensor("q_parts", [2, 3, P, TH], BF16).ap()
        k_parts = nc.dram_tensor("k_parts", [4, 3, P, 512], BF16).ap()
        g_rows = nc.dram_tensor("g_rows", [NE, T], F32).ap()

        def col(name, i=0, n=1, rows=P):
            a = COLS[name][0] + i
            return C[0:rows, a:a + n]

        def row(name):
            a, w = ROWS[name]
            return R[:, a:a + w]

        before = []


        def norm_vector(dve, s, src, eps, chain, n):
            for t in range(NT):
                ins = dve.bn_stats(ST8[:, t, :], src[:, t, :])
            chain(ins)
            for t in range(NT):
                ins = dve.bn_aggr(MV[:, t, :], ST8[:, t, :])
            chain(ins)
            dve.tensor_scalar(VE[:, :], MV[:, :, 1], eps, None, ALU.add).then_inc(s["var"], 1)
            dve.wait_ge(s["rstd"], n)
            for t in range(NT):
                dve.tensor_scalar(XN[:, t, :], src[:, t, :], MV[:, t, 0:1], RSTD[:, t:t + 1],
                                  ALU.subtract, ALU.mult).then_inc(s["norm_rows"], 1)
            dve.wait_ge(s["norm_rows"], NT * n)

        def norm_pool(pool, s, n):
            pool.wait_ge(s["var"], n)
            pool.tensor_tensor(RSTD[:, :], VE[:, :], HALF[:, :], ALU.pow).then_inc(s["rstd"], 1)

        def affine_rows(dve, sem, before, g, b):
            for i, (name, op) in enumerate(((g, ALU.mult), (b, ALU.add))):
                dve.tensor_tensor(XN[:, :, :], XN[:, :, :], row(name).unsqueeze(1).to_broadcast([P, NT, P]), op)\
                   .then_inc(sem, 1)
                dve.wait_ge(sem, before + i + 1)

        def turn_rows(pe, s, src, dst, name):
            for t in range(NT):
                ins = pe.transpose(dst[:, t * P:(t + 1) * P], src[:, t, :], IDF[:, :])
                if t % 4 == 3:
                    ins.then_inc(s[name], 1)

        def prep_names():
            return "k_made v_made v_kept k_kept k_hi k_rest k_mid k_lo k_stored0 k_stored1 k_placed"

        def prep_tensor(pe, s, a, src, chunks):
            for c in range(chunks):
                if c >= 2:
                    pe.wait_ge(s["k_rest"], c - 1)
                pe.matmul(PS[2][:, (c % 2) * 512:(c % 2) * 512 + 512], WA[:, a, 1, :],
                          src[:, c * 512:(c + 1) * 512], start=True, stop=True).then_inc(s["k_made"], 1)
                if c >= 2:
                    pe.wait_ge(s["v_kept"], c - 1)
                for t in range(4):
                    ins = pe.matmul(PS[3][:, (c % 2) * 512 + t * P:(c % 2) * 512 + (t + 1) * P],
                                    src[:, (4 * c + t) * P:(4 * c + t + 1) * P], WA[:, a, 2, :],
                                    start=True, stop=True)
                ins.then_inc(s["v_made"], 1)

        def prep_scalar(act, s, a, chunks):
            for c in range(chunks):
                bank = PS[2][:, (c % 2) * 512:(c % 2) * 512 + 512]
                if c >= 2:
                    act.wait_ge(s[f"k_stored{c % 2}"], 48 * (c // 2))
                if a == 2:
                    act.wait_ge(s["k_kept"], c + 1)
                    act.activation(HI[:, c % 2, :], KKEPT[:, c % 2, :], ACT.Copy).then_inc(s["k_hi"], 1)
                else:
                    act.wait_ge(s["k_made"], c + 1)
                    act.activation(HI[:, c % 2, :], bank, ACT.Identity, bias=col(f"bk{a}"))\
                       .then_inc(s["k_hi"], 1)
                act.wait_ge(s["v_made"], c + 1)
                o = V[:, 4 * c:4 * c + 4, 0:9 * HEADS].rearrange("p t (h e) -> p t h e", e=9)[:, :, :, 0:DH]
                act.activation(o, PS[3][:, (c % 2) * 512:(c % 2) * 512 + 512]
                               .rearrange("p (t h e) -> p t h e", t=4, e=DH), ACT.Copy)\
                   .then_inc(s["v_kept"], 1)

        def prep_vector(dve, s, a, chunks):
            for c in range(chunks):
                bank = PS[2][:, (c % 2) * 512:(c % 2) * 512 + 512]
                if c >= 2:
                    dve.wait_ge(s["k_lo"], c - 1)
                if a == 2:
                    dve.wait_ge(s["k_made"], c + 1)
                    dve.scalar_tensor_tensor(KKEPT[:, c % 2, :], KEEP[:, c * 512:(c + 1) * 512], 0.0, bank,
                                             ALU.is_equal, ALU.mult).then_inc(s["k_kept"], 1)
                    dve.wait_ge(s["k_hi"], c + 1)
                    dve.tensor_tensor(REST[:, c % 2, :], KKEPT[:, c % 2, :], HI[:, c % 2, :], ALU.subtract)\
                       .then_inc(s["k_rest"], 1)
                else:
                    dve.wait_ge(s["k_hi"], c + 1)
                    dve.scalar_tensor_tensor(REST[:, c % 2, :], bank, col(f"bk{a}"), HI[:, c % 2, :],
                                             ALU.add, ALU.subtract).then_inc(s["k_rest"], 1)

        def prep_pool(pool, s, a, chunks):
            for c in range(chunks):
                if c >= 2:
                    pool.wait_ge(s[f"k_stored{c % 2}"], 48 * (c // 2))
                pool.wait_ge(s["k_rest"], c + 1)
                pool.tensor_copy(MID[:, c % 2, :], REST[:, c % 2, :]).then_inc(s["k_mid"], 1)
                pool.wait_ge(s["k_mid"], c + 1)
                pool.tensor_tensor(LO[:, c % 2, :], REST[:, c % 2, :], MID[:, c % 2, :], ALU.subtract)\
                    .then_inc(s["k_lo"], 1)
            if a == 1:
                pool.wait_ge(s["k_lo"], chunks)
                pool.memset(KOP[MASK_ROW:MASK_ROW + 1, :, :, :], 0.0).then_inc(s["k_lo"], 1)
                pool.wait_ge(s["k_lo"], chunks + 1)

        def prep_sync(sp, s, a, chunks):
            for c in range(chunks):
                for r, (part, name) in enumerate(((HI, "k_hi"), (MID, "k_mid"), (LO, "k_lo"))):
                    sp.wait_ge(s[name], c + 1)
                    sp.dma_start(k_parts[c, r], part[:, c % 2, :]).then_inc(s[f"k_stored{c % 2}"], 16)
                sp.wait_ge(s[f"k_stored{c % 2}"], 48 * (c // 2 + 1))
                for m in range(2):
                    src = k_parts[c, :, m * 64:(m + 1) * 64, :].rearrange("r (d p) n -> r d (p n)", p=NP)
                    r0 = m * CW
                    sp.dma_start(KOP[r0:r0 + 24, c, :, :], src[0:3]).then_inc(s["k_placed"], 16)
                    sp.dma_start(KOP[r0 + 24:r0 + 40, c, :, :], src[0:2]).then_inc(s["k_placed"], 16)
                    sp.dma_start(KOP[r0 + 40:r0 + 48, c, :, :], src[0]).then_inc(s["k_placed"], 16)


        s = signals(nc, "load", "x ctx wk wa mask c zero idf ones k0 neg " + prep_names(), before)
        with nc.Block() as block:
            @block.sync
            def _(sp):
                sp.dma_start(CTX[:, :], d["ctxT"]).then_inc(s["ctx"], 16)
                sp.dma_start(WA[:, 0, :, :], d["wattn"][:, 0, :, :]).then_inc(s["wk"], 16)
                sp.dma_start(C[:, :], d["cols"]).then_inc(s["c"], 16)
                sp.dma_start(M0[MASK_ROW:MASK_ROW + 1, :], d["mask0"]).then_inc(s["mask"], 16)
                sp.dma_start(M2[:, :, :], d["mask2"].rearrange("(t q) k -> q t k", q=P)).then_inc(s["mask"], 16)
                sp.dma_start(M2T[:, :, :], d["mask2T"].rearrange("(t k) q -> k t q", k=P)).then_inc(s["mask"], 16)
                sp.dma_start(X[:, :, :], d["x"].rearrange("(t p) e -> p t e", p=P)).then_inc(s["x"], 16)
                prep_sync(sp, s, 0, 4)
                sp.dma_start(WA[:, 1:5, :, :], d["wattn"][:, 1:5, :, :]).then_inc(s["wa"], 16)
                sp.dma_start(WCONV[:, :, :], d["wconv"]).then_inc(s["wa"], 16)
                sp.dma_start(WR[:, :, :], d["wrouter"]).then_inc(s["wa"], 16)
                sp.dma_start(B2[:, :, :], d["b2"]).then_inc(s["wa"], 16)
                sp.dma_start(R[:, :], d["rows"].partition_broadcast(P)).then_inc(s["wa"], 16)
                sp.dma_start(KEEP[:, :], d["mask_keys"].partition_broadcast(P)).then_inc(s["wa"], 16)
                sp.wait_ge(s["wa"], 96)
                sp.wait_ge(s["k_placed"], 96 * 4)
                sp.wait_ge(s["x"], 16)

            @block.gpsimd
            def _(pool):
                pool.memset(IDF[:, :], 0.0).then_inc(s["zero"], 1)
                pool.memset(V[:, :, :], 1.0).then_inc(s["ones"], 1)
                pool.memset(HALF[:, :], -0.5)
                pool.memset(NEGC[:, :], 0.0).then_inc(s["zero"], 1)
                pool.memset(STAIR[:, :], 0.0).then_inc(s["zero"], 1)
                pool.wait_ge(s["zero"], 3)
                pool.affine_select(out=IDF[:, :], in_=IDF[:, :], compare_op=ALU.not_equal, fill=1.0, base=0,
                                   pattern=[[-1, P]], channel_multiplier=1).then_inc(s["idf"], 1)
                pool.affine_select(out=NEGC[:, :], in_=NEGC[:, :], compare_op=ALU.is_ge, fill=NEG, base=3,
                                   pattern=[[-1, SK]], channel_multiplier=4).then_inc(s["neg"], 1)
                pool.affine_select(out=STAIR[:, :], in_=STAIR[:, :], compare_op=ALU.is_ge, fill=NEG, base=3,
                                   pattern=[[4, 32]], channel_multiplier=-1).then_inc(s["neg"], 1)
                for e in range(NE):
                    pool.memset(IOTA[:, :, e], float(e))
                pool.wait_ge(s["idf"], 1)
                pool.tensor_copy(IDB[:, :], IDF[:, :]).then_inc(s["neg"], 1)
                prep_pool(pool, s, 0, 4)

            @block.vector
            def _(dve):
                dve.memset(KOP[MASK_ROW:MASK_ROW + 3, :, :, :], 1.0).then_inc(s["k0"], 1)
                prep_vector(dve, s, 0, 4)
                dve.memset(QOP[0:MASK_ROW, :, :, :], 0.0)
                dve.memset(QOP[MASK_ROW:MASK_ROW + 3, :, :, :], 1.0)
                dve.wait_ge(s["mask"], 48)
                dve.tensor_scalar(NEG2[:, :, :], M2[:, :, :], NEG, None, ALU.mult)
                dve.tensor_scalar(NEG2T[:, :, :], M2T[:, :, :], NEG, None, ALU.mult)
                dve.wait_ge(s["k0"], 1)
                for p in range(NP):
                    dve.tensor_scalar(KOP[MASK_ROW:MASK_ROW + 1, :, p, :],
                                      M0[MASK_ROW:MASK_ROW + 1, :].rearrange("o (c n) -> o c n", c=4),
                                      -NEG, NEG, ALU.mult, ALU.add).then_inc(s["k0"], 1)

            @block.scalar
            def _(act):
                act.wait_ge(s["c"], 16)
                act.wait_ge(s["ones"], 1)
                prep_scalar(act, s, 0, 4)

            @block.tensor
            def _(pe):
                pe.wait_ge(s["ctx"], 16)
                pe.wait_ge(s["wk"], 16)
                prep_tensor(pe, s, 0, CTX, 4)


        def attention(a):
            own = a == 4
            nk = SQ if own else SK
            nkt = nk // P
            stairs = a == 1
            if stairs:
                places = [(0, 0), (512, 32), (512 + 224, 64), (256, 96)]
                width, banks = 416, 2
            elif own:
                places = [(0, 0), (256, 0)]
                width, banks = 512, 1
            else:
                places = [(256 * i, 0) for i in range(4)]
                width, banks = 512, 2
            rows_out = XN if own else X
            last = B * NG

            def spot(k):
                return k // NG, k % NG // 2, 4 * (k % 2)

            def queries(k, j, lo, n, rows):
                b, m, p0 = spot(k)
                x = (b % 2) * SQ + lo
                return QOP[0:rows, b // 2, m * NP + p0 + j, x:x + n]

            def keys(k, j, lo, n, rows):
                b, m, p0 = spot(k)
                x = b * nk + lo
                return KOP[0:rows, x // 512, p0 + j, x % 512:x % 512 + n]

            def filled(t):
                return t.rearrange("p (k n) -> p k n", k=2)[:, 0:banks, 0:width]

            turn = {}
            for n in range(-LOOK, last + 2):
                if 0 <= n - 2:
                    turn["rows", n - 2] = len(turn)
                if 0 <= n + LOOK - 1 < last:
                    turn["shift", n + LOOK - 1] = len(turn)
                if n - 2 >= 0 and (n - 2) % NG == NG - 1:
                    turn["cols", (n - 2) // NG] = len(turn)
                    turn["out", (n - 2) // NG] = len(turn)

            s = signals(nc, f"attn{a}", "var rstd norm_rows chain turned kept q_made q_hi q_rest q_mid q_lo "
                        "q_stored0 q_stored1 q_placed0 q_placed1 biased scored maxed neg shift "
                        "shift_placed0 shift_placed1 scored_t exps summed o_kept x_made x_read rc", before)
            SUM = PS[3][:, 0:256]
            XB = PS[3][:, 512:1024]
            XBH = XB.bitcast(BF16)

            with nc.Block() as block:
                @block.sync
                def _(sp):
                    for h in range(2):
                        for r, (part, name) in enumerate(((HI, "q_hi"), (MID, "q_mid"), (LO, "q_lo"))):
                            sp.wait_ge(s[name], h + 1)
                            sp.dma_start(q_parts[h, r], part[:, h, :]).then_inc(s[f"q_stored{h}"], 16)
                        sp.wait_ge(s[f"q_stored{h}"], 48)
                        for m in range(2):
                            for r, (r0, n) in enumerate(((0, 3), (24, 2), (40, 1))):
                                src = q_parts[h, r, m * 64:(m + 1) * 64, :].rearrange("(d p) n -> d (p n)", p=NP)
                                if n > 1:
                                    src = src.unsqueeze(0).to_broadcast([n, DH, NP * TH])
                                sp.dma_start(QOP[m * CW + r0:m * CW + r0 + n * DH, h, m * NP:(m + 1) * NP, :],
                                             src).then_inc(s[f"q_placed{h}"], 16)
                    for k in range(last):
                        b, m, p0 = spot(k)
                        sp.wait_ge(s["x_read"], turn["shift", k] + 1)
                        for r in range(2):
                            sp.dma_start(QOP[SHIFT_ROW + r:SHIFT_ROW + r + 1, b // 2,
                                             m * NP + p0:m * NP + p0 + GROUP,
                                             (b % 2) * SQ:(b % 2) * SQ + SQ],
                                         SH[r * GROUP:(r + 1) * GROUP, k % 2, :])\
                              .then_inc(s[f"shift_placed{k % 2}"], 16)
                    for r in range(2):
                        sp.wait_ge(s[f"shift_placed{r}"], 32 * last // 2)

                @block.gpsimd
                def _(pool):
                    if not own:
                        norm_pool(pool, s, 1)
                    for h in range(2):
                        pool.wait_ge(s["q_rest"], h + 1)
                        pool.tensor_copy(MID[:, h, :], REST[:, h, :]).then_inc(s["q_mid"], 1)
                        pool.wait_ge(s["q_mid"], h + 1)
                        pool.tensor_tensor(LO[:, h, :], REST[:, h, :], MID[:, h, :], ALU.subtract)\
                            .then_inc(s["q_lo"], 1)
                    if not own:
                        pool.wait_ge(s["norm_rows"], NT)
                    if a > 0:
                        pool.tensor_tensor(rows_out[:, :, :], rows_out[:, :, :],
                                           row(f"bo{a}").unsqueeze(1).to_broadcast([P, NT, P]), ALU.add)\
                            .then_inc(s["biased"], 1)
                    for k in range(last):
                        pool.wait_ge(s["maxed"], 2 * GROUP * (k + 1))
                        if k >= 4:
                            pool.wait_ge(s["x_made"], turn["shift", k - 4] + 1)
                        pool.tensor_scalar(NG32[:, k % 4], NM[:, k % 4], -1.0, None, ALU.mult)\
                            .then_inc(s["neg"], 1)
                        pool.wait_ge(s["neg"], 2 * k + 1)
                        pool.tensor_copy(HL[:, k % 4, :, 0, :], NG32[:, k % 4]).then_inc(s["neg"], 1)
                        pool.wait_ge(s["neg"], 2 * k + 2)
                        pool.tensor_tensor(HL[:, k % 4, :, 1, :], NG32[:, k % 4], HL[:, k % 4, :, 0, :],
                                           ALU.subtract).then_inc(s["shift"], 1)

                @block.vector
                def _(dve):
                    chain = Chain(dve, s["chain"])
                    if not own:
                        norm_vector(dve, s, X, EPS, chain, 1)
                    for h in range(2):
                        dve.wait_ge(s["q_hi"], h + 1)
                        dve.scalar_tensor_tensor(REST[:, h, :], PS[1][:, h * TH:(h + 1) * TH], col(f"bq{a}"),
                                                 HI[:, h, :], ALU.add, ALU.subtract).then_inc(s["q_rest"], 1)

                    def maxima(k, j):
                        for q in range(2):
                            c = 2 * (GROUP * k + j) + q
                            dve.wait_ge(s["scored"], c + 1)
                            if k >= 4:
                                dve.wait_ge(s["shift"], k - 3)
                            dve.tensor_reduce(NM[:, k % 4, q, j:j + 1], PS[2][:, (c % 2) * 512:(c % 2) * 512 + nk],
                                              AX.X, ALU.max).then_inc(s["maxed"], 1)

                    def normalize(k):
                        b, m, p0 = spot(k)
                        dve.wait_ge(s["x_made"], turn["rows", k] + 1)
                        x = XB[:, 0:256].rearrange("p (t j e) -> p t j e", t=2, j=GROUP)
                        dve.reciprocal(RC[:, k % 2, :, :], x[:, :, :, DH]).then_inc(s["rc"], 1)
                        dve.wait_ge(s["rc"], k + 1)
                        if k % NG == 0 and b >= 2:
                            dve.wait_ge(s["x_made"], turn["cols", b - 2] + 1)
                        o = ON[:, b % 2, :, :].rearrange("p t (r m e) -> p t r m e", m=2, e=DH)
                        dve.tensor_tensor(o[:, :, p0:p0 + GROUP, m, :], x[:, :, :, 0:DH],
                                          RC[:, k % 2, :, :].unsqueeze(3).to_broadcast([P, 2, GROUP, DH]),
                                          ALU.mult).then_inc(s["x_read"], 1)

                    def add_out(b):
                        dve.wait_ge(s["x_made"], turn["out", b] + 1)
                        if a > 0:
                            dve.wait_ge(s["biased"], 1)
                        o = rows_out[:, 2 * b:2 * b + 2, :]
                        dve.tensor_tensor(o, XB[:, 0:256].rearrange("p (t e) -> p t e", t=2), o, ALU.add)\
                           .then_inc(s["x_read"], 1)

                    for n in range(-LOOK, last + 2):
                        k = n + LOOK
                        for j in range(GROUP):
                            if k < last:
                                maxima(k, j)
                            if j == 0 and n - 2 >= 0:
                                normalize(n - 2)
                            if j == 3 and n - 2 >= 0 and (n - 2) % NG == NG - 1:
                                add_out((n - 2) // NG)

                @block.scalar
                def _(act):
                    if not own:
                        for h in range(2):
                            act.wait_ge(s["turned"], h + 1)
                            act.activation(XNT[:, h * TH:(h + 1) * TH], PS[0][:, h * TH:(h + 1) * TH], ACT.Copy)\
                               .then_inc(s["kept"], 1)
                    for h in range(2):
                        act.wait_ge(s["q_made"], h + 1)
                        act.activation(HI[:, h, :], PS[1][:, h * TH:(h + 1) * TH], ACT.Identity,
                                       bias=col(f"bq{a}")).then_inc(s["q_hi"], 1)

                    def exponentials(n, j):
                        u = GROUP * n + j
                        act.wait_ge(s["scored_t"], u + 1)
                        if n >= 2:
                            act.wait_ge(s["summed"], n - 1)
                        act.activation(filled(PT[:, u % 8, :]), filled(PS[u % 2][:, :]), ACT.Exp, scale=SCALE)\
                           .then_inc(s["exps"], 1)

                    def keep_shift(k):
                        act.wait_ge(s["x_made"], turn["shift", k] + 1)
                        if k >= 2:
                            act.wait_ge(s[f"shift_placed{k % 2}"], 32 * (k // 2))
                        act.activation(SH[:, k % 2, :], XBH[0:2 * GROUP, 0:256], ACT.Copy)\
                           .then_inc(s["x_read"], 1)

                    def keep_sums(k):
                        act.wait_ge(s["summed"], k + 1)
                        if k >= 2:
                            act.wait_ge(s["x_made"], turn["rows", k - 2] + 1)
                        act.activation(OT[:, k % 2, :], SUM, ACT.Copy).then_inc(s["o_kept"], 1)

                    def keep_cols(b):
                        act.wait_ge(s["x_made"], turn["cols", b] + 1)
                        act.activation(CT[:, b % 2, :], XB[:, 0:256], ACT.Identity, bias=col(f"bv{a}"))\
                           .then_inc(s["x_read"], 1)

                    for n in range(-LOOK, last + 2):
                        for j in range(GROUP):
                            if 0 <= n < last:
                                exponentials(n, j)
                            if j == 1 and 0 <= n + LOOK - 1 < last:
                                keep_shift(n + LOOK - 1)
                            if j == 1 and 0 <= n - 1 < last:
                                keep_sums(n - 1)
                            if j == 2 and n - 2 >= 0 and (n - 2) % NG == NG - 1:
                                keep_cols((n - 2) // NG)

                @block.tensor
                def _(pe):
                    if not own:
                        for t in range(NT):
                            pe.wait_ge(s["norm_rows"], t + 1)
                            ins = pe.transpose(PS[0][:, t * P:(t + 1) * P], XN[:, t, :], IDF[:, :])
                            if t % 4 == 3:
                                ins.then_inc(s["turned"], 1)
                    for h in range(2):
                        if not own:
                            pe.wait_ge(s["kept"], h + 1)
                        pe.matmul(PS[1][:, h * TH:(h + 1) * TH], WA[:, a, 0, :], XNT[:, h * TH:(h + 1) * TH],
                                  start=True, stop=True).then_inc(s["q_made"], 1)

                    def scores(k, j):
                        b = k // NG
                        if k % (2 * NG) == 0 and j == 0:
                            pe.wait_ge(s[f"q_placed{b // 2}"], 96)
                        for q in range(2):
                            c = 2 * (GROUP * k + j) + q
                            if c >= 2:
                                pe.wait_ge(s["maxed"], c - 1)
                            o = PS[2][:, (c % 2) * 512:(c % 2) * 512 + nk]
                            masked = a == 2 or (stairs and q == 0)
                            ins = pe.matmul(o, queries(k, j, q * P, P, MASK_ROW + 1), keys(k, j, 0, nk, MASK_ROW + 1),
                                            start=True, stop=not masked)
                            if masked:
                                ins = pe.matmul(o, IDB[:, :], NEG2[:, q, :] if a == 2 else NEGC[:, :],
                                                start=False, stop=True)
                            ins.then_inc(s["scored"], 1)

                    def scores_t(n, j):
                        u = GROUP * n + j
                        if j == 0:
                            pe.wait_ge(s[f"shift_placed{n % 2}"], 32 * (n // 2 + 1))
                        if u >= 2:
                            pe.wait_ge(s["exps"], u - 1)
                        for i, (x, q0) in enumerate(places):
                            o = PS[u % 2][:, x:x + SQ - q0]
                            ins = pe.matmul(o, keys(n, j, i * P, P, SHIFT_ROW + 2),
                                            queries(n, j, q0, SQ - q0, SHIFT_ROW + 2), start=True, stop=a != 2)
                            if a == 2:
                                ins = pe.matmul(o, IDB[:, :], NEG2T[:, i, :], start=False, stop=True)
                            if stairs:
                                ins = pe.matmul(PS[u % 2][:, x:x + 32], IDB[:, :], STAIR[:, :], start=False,
                                                stop=True, skip_group_check=True)
                        ins.then_inc(s["scored_t"], 1)

                    def sums(n):
                        b, m, p0 = spot(n)
                        pe.wait_ge(s["exps"], GROUP * (n + 1))
                        if n >= 1:
                            pe.wait_ge(s["o_kept"], n)
                        for i, (x, q0) in enumerate(places):
                            for j in range(GROUP):
                                h = 2 * (p0 + j) + m
                                ins = pe.matmul(SUM[32 * j:32 * j + 32, q0:SQ], V[:, b * nkt + i, 9 * h:9 * h + 32],
                                                PT[:, (GROUP * n + j) % 8, x:x + SQ - q0], start=(i == 0),
                                                stop=(i == nkt - 1), tile_position=(0, 32 * j),
                                                skip_group_check=True)
                        ins.then_inc(s["summed"], 1)

                    def my_turn(what, k):
                        if turn[what, k]:
                            pe.wait_ge(s["x_read"], turn[what, k])

                    for n in range(-LOOK, last + 2):
                        k = n + LOOK
                        for j in range(GROUP):
                            if 0 <= n < last:
                                scores_t(n, j)
                            if k < last:
                                scores(k, j)
                            if j == 0 and n - 2 >= 0:
                                g = n - 2
                                my_turn("rows", g)
                                pe.wait_ge(s["o_kept"], g + 1)
                                for t in range(2):
                                    ins = pe.transpose(XB[:, t * P:(t + 1) * P], OT[:, g % 2, t * P:(t + 1) * P], IDF[:, :])
                                ins.then_inc(s["x_made"], 1)
                            if j == 1 and 0 <= k - 1 < last:
                                g = k - 1
                                my_turn("shift", g)
                                pe.wait_ge(s["shift"], g + 1)
                                for t in range(2):
                                    ins = pe.transpose(XBH[0:2 * GROUP, t * P:(t + 1) * P],
                                                       HL[:, g % 4, t, :, :].rearrange("p r j -> p (r j)"), IDB[:, :])
                                ins.then_inc(s["x_made"], 1)
                            if j == 1 and 0 <= n - 1 < last:
                                sums(n - 1)
                            if j == 2 and n - 2 >= 0 and (n - 2) % NG == NG - 1:
                                b = (n - 2) // NG
                                my_turn("cols", b)
                                for t in range(2):
                                    ins = pe.transpose(XB[:, t * P:(t + 1) * P], ON[:, b % 2, t, :], IDF[:, :])
                                ins.then_inc(s["x_made"], 1)
                            if j == 3 and n - 2 >= 0 and (n - 2) % NG == NG - 1:
                                b = (n - 2) // NG
                                my_turn("out", b)
                                for t in range(2):
                                    ins = pe.matmul(XB[:, t * P:(t + 1) * P], CT[:, b % 2, t * P:(t + 1) * P],
                                                    WA[:, a, 3, :], start=True, stop=True)
                                ins.then_inc(s["x_made"], 1)
    

        def experts(l):
            gated_out = l in (0, 3)
            final = l == 3
            hid = HID[l]
            sizes = [min(P, hid - P * c) for c in range(-(-hid // P))]
            nch = len(sizes)
            units = NE * nch * (1 if gated_out else 2)
            s = signals(nc, f"ffn{l}", "var rstd norm_rows chain turned kept scaled_r routed ex sub gates g_turned "
                        "g_kept g_stored " + " ".join(f"g_loaded{e}" for e in range(NE)) + " affine acc0_made acc0 w_loaded0 w_loaded1 u_made up acted h_made down "
                        "y_used added acc back chain2 stored " + (prep_names() if not final else ""), before)
            prep = l + 1 if not final else None
            HT = H[:, :].rearrange("p (u n) -> p u n", n=1024 if gated_out else 512)
            with nc.Block() as block:
                @block.sync
                def _(sp):
                    def weights(e):
                        if e >= 2:
                            sp.wait_ge(s["down"], (e - 1) * units // NE)
                        sp.dma_start(W[:, e % 2, 0:EW[l]], d[f"we{l}"][e]).then_inc(s[f"w_loaded{e % 2}"], 16)
                    weights(0)
                    weights(1)
                    if not final:
                        prep_sync(sp, s, prep, 4)
                    sp.wait_ge(s["g_kept"], 2)
                    sp.dma_start(g_rows, GT[:, :]).then_inc(s["g_stored"], 16)
                    sp.wait_ge(s["g_stored"], 16)
                    for e in range(NE):
                        sp.dma_start(GB[:, e, :], g_rows[e].partition_broadcast(P)).then_inc(s[f"g_loaded{e}"], 16)
                    for e in range(2, NE):
                        weights(e)
                    if not final:
                        sp.wait_ge(s["k_placed"], 96 * 4)
                    else:
                        sp.wait_ge(s["acc"], 1)
                        sp.dma_start(out.rearrange("(t p) e -> p t e", p=P), XN[:, :, :]).then_inc(s["stored"], 16)
                        sp.wait_ge(s["stored"], 16)

                @block.gpsimd
                def _(pool):
                    norm_pool(pool, s, 1)
                    if l == 0:
                        norm_pool(pool, s, 2)
                    if not final:
                        prep_pool(pool, s, prep, 4)
                    if gated_out:
                        for e in range(NE):
                            pool.wait_ge(s["y_used"], e + 1)
                            if e == 0:
                                pool.wait_ge(s["acc0"], 1)
                            else:
                                pool.wait_ge(s["added"], e)
                            pool.tensor_tensor(ACC[:, :], ACC[:, :], HT[:, 2, :], ALU.add)\
                                .then_inc(s["added"], 1)
                    if final:
                        norm_pool(pool, s, 2)

                @block.vector
                def _(dve):
                    chain = Chain(dve, s["chain"])
                    norm_vector(dve, s, XN if final else X, EPS, chain, 1)
                    if l == 0:
                        norm_vector(dve, s, XN, EPS_IN, chain, 2)
                    if final:
                        affine_rows(dve, s["affine"], 0, "ln1_g", "ln1_b")
                    if l == 0:
                        dve.wait_ge(s["kept"], 2)
                        dve.tensor_scalar(U[:, 0, :], XNT[:, :], col("rln_s"), col("rln_b"), ALU.mult, ALU.add)\
                           .then_inc(s["scaled_r"], 1)
                    dve.wait_ge(s["routed"], 1)
                    lg = PS[1][:, 0:NT * NE].rearrange("p (t e) -> p t e", e=NE)
                    if gated_out:
                        chain(dve.tensor_tensor(LG[:, :, :], lg,
                                                row(f"router_b{l}").unsqueeze(1).to_broadcast([P, NT, NE]), ALU.add))
                    else:
                        chain(dve.tensor_copy(LG[:, :, :], lg))
                    for t in range(NT):
                        ins = dve.max(MX[:, t, :], LG[:, t, :])
                    chain(ins)

                    def wide(v):
                        return v.to_broadcast([P, NT, NE])
                    top1, top2 = MX[:, :, 0:1], MX[:, :, 1:2]
                    D1, OH1, OH2, EX, D2, EX2, T1, T2 = [g[:, :, :] for g in GA]
                    tt = dve.tensor_tensor
                    if l != 3:
                        for t in range(NT):
                            ins = dve.max_index(IX[:, t, :], MX[:, t, :], LG[:, t, :])
                        chain(ins)
                        chain(dve.tensor_copy(IXF[:, :, :], IX[:, :, :]))
                        tt(OH1, IOTA[:, :, :], wide(IXF[:, :, 0:1]), ALU.is_equal)
                        tt(OH2, IOTA[:, :, :], wide(IXF[:, :, 1:2]), ALU.is_equal)
                    tt(D1, LG[:, :, :], wide(top1), ALU.subtract).then_inc(s["sub"], 1)
                    if l == 2:
                        chain(tt(D2, LG[:, :, :], wide(top2), ALU.subtract))
                        dve.tensor_scalar(T2, D2, 0.0, None, ALU.min).then_inc(s["sub"], 1)
                        chain(dve.tensor_scalar(T1, LG[:, :, :], -1.0, None, ALU.mult))
                        chain(tt(T1, T1, LG[:, :, :], ALU.max))
                        chain(tt(LG[:, :, :], T1, wide(top1), ALU.max))
                        chain(dve.scalar_tensor_tensor(LG[:, :, :], LG[:, :, :], 0.02, D1, ALU.mult, ALU.add))
                        chain(dve.tensor_scalar(LG[:, :, :], LG[:, :, :], 0.0, None, ALU.is_ge))
                        chain(tt(T1, T1, wide(top2), ALU.max))
                        chain(dve.scalar_tensor_tensor(T1, T1, 0.02, D2, ALU.mult, ALU.add))
                        chain(dve.tensor_scalar(T1, T1, 0.0, None, ALU.is_ge))
                        chain(dve.scalar_tensor_tensor(T1, OH1, 1.0, T1, ALU.subtract, ALU.mult))
                        dve.wait_ge(s["ex"], 2)
                        chain(tt(EX, EX, LG[:, :, :], ALU.mult))
                        chain(tt(EX2, EX2, T1, ALU.mult))
                        chain(dve.tensor_reduce(G1[0][:, :], EX, AX.X, ALU.add))
                        chain(dve.tensor_reduce(G1[1][:, :], EX2, AX.X, ALU.add))
                        chain(dve.reciprocal(G1[0][:, :], G1[0][:, :]))
                        chain(dve.reciprocal(G1[1][:, :], G1[1][:, :]))
                        chain(tt(OH1, OH1, wide(G1[0][:, :].unsqueeze(2)), ALU.mult))
                        chain(tt(OH2, OH2, wide(G1[1][:, :].unsqueeze(2)), ALU.mult))
                        tt(T1, OH1, OH2, ALU.subtract).then_inc(s["gates"], 1)
                    else:
                        if l != 3:
                            dve.wait_ge(s["sub"], 1)
                            chain(tt(OH1, OH1, OH2, ALU.add))
                        dve.wait_ge(s["ex"], 1)
                        den = EX
                        if l != 3:
                            chain(tt(EX2, EX, OH1, ALU.mult))
                            top = EX2
                        else:
                            top = EX
                        if l == 0:
                            den = EX2
                        chain(dve.tensor_reduce(G1[0][:, :], den, AX.X, ALU.add))
                        chain(dve.reciprocal(G1[0][:, :], G1[0][:, :]))
                        tt(T1, top, wide(G1[0][:, :].unsqueeze(2)), ALU.mult).then_inc(s["gates"], 1)

                    if not final:
                        prep_vector(dve, s, prep, 4)

                    if gated_out:
                        def inputs(e):
                            if l == 0:
                                if e == 0:
                                    dve.wait_ge(s["routed"], 1)
                                if e >= 2:
                                    dve.wait_ge(s["up"], nch * (e - 1))
                                dve.tensor_scalar(U[:, e % 2, :], XNT[:, :], col("eln_s", e), col("eln_b", e),
                                                  ALU.mult, ALU.add).then_inc(s["u_made"], 1)
                        inputs(0)
                        inputs(1)
                        dve.wait_ge(s["acc0_made"], 1)
                        dve.wait_ge(s["g_stored"], 16)
                        dve.tensor_copy(ACC[:, :], PS[3][:, :]).then_inc(s["acc0"], 1)
                        for e in range(NE):
                            dve.wait_ge(s["down"], nch * (e + 1))
                            dve.wait_ge(s[f"g_loaded{e}"], 16)
                            if e >= 1:
                                dve.wait_ge(s["added"], e)
                            dve.tensor_tensor(HT[:, 2, :], PS[2 + e % 2][:, :], GB[:, e, :], ALU.mult)\
                               .then_inc(s["y_used"], 1)
                            if e + 2 < NE:
                                inputs(e + 2)
                    else:
                        def inputs(e):
                            dve.wait_ge(s[f"g_loaded{e}"], 16)
                            if e >= 2:
                                dve.wait_ge(s["up"], 2 * nch * (e - 1))
                            dve.tensor_tensor(U[:, e % 2, :], XNT[:, :], GB[:, e, :], ALU.mult)\
                               .then_inc(s["u_made"], 1)
                        inputs(0)
                        for k in range(units):
                            e, c = k // (2 * nch), k % (2 * nch) // 2
                            z = sizes[c]
                            if k % (2 * nch) == 0 and e + 1 < NE:
                                inputs(e + 1)
                            dve.wait_ge(s["acted"], k + 1)
                            if k >= 3:
                                dve.wait_ge(s["down"], k - 2)
                            dve.tensor_tensor(HT[0:z, k % 3, :], PS[k % 3][0:z, 512:1024], HT[0:z, 4 + k % 2, :],
                                              ALU.mult).then_inc(s["h_made"], 1)
                        dve.wait_ge(s["down"], units)
                        if l == 1:
                            dve.tensor_scalar(ACC[:, :], PS[3][:, :], col("ffn1_bias"), None, ALU.add)\
                               .then_inc(s["acc"], 1)
                        else:
                            dve.tensor_copy(ACC[:, :], PS[3][:, :]).then_inc(s["acc"], 1)
                    dst = XN if final else X
                    dve.wait_ge(s["back"], 2)
                    chain2 = Chain(dve, s["chain2"])
                    for h in range(2):
                        o = dst[:, 4 * h:4 * h + 4, :]
                        chain2(dve.tensor_tensor(o, PS[0][:, h * TH:(h + 1) * TH].rearrange("p (t e) -> p t e", t=4),
                                                 o, ALU.add))
                    if final:
                        norm_vector(dve, s, XN, EPS, chain2, 2)
                        affine_rows(dve, s["affine"], 2, "ln2_g", "ln2_b")
                        dve.tensor_tensor(XN[:, :, :], XN[:, :, :], X[:, :, :], ALU.add).then_inc(s["acc"], 1)

                @block.scalar
                def _(act):
                    for h in range(2):
                        act.wait_ge(s["turned"], h + 1)
                        act.activation(XNT[:, h * TH:(h + 1) * TH], PS[0][:, h * TH:(h + 1) * TH], ACT.Copy)\
                           .then_inc(s["kept"], 1)
                    act.wait_ge(s["sub"], 1)
                    act.activation(GA[3][:, :, :], GA[0][:, :, :], ACT.Exp).then_inc(s["ex"], 1)
                    if l == 2:
                        act.wait_ge(s["sub"], 2)
                        act.activation(GA[5][:, :, :], GA[7][:, :, :], ACT.Exp).then_inc(s["ex"], 1)
                    if not final:
                        prep_scalar(act, s, prep, 4)
                    for h in range(2):
                        act.wait_ge(s["g_turned"], h + 1)
                        act.activation(GT[:, h * TH:(h + 1) * TH], PS[1][0:NE, h * TH:(h + 1) * TH], ACT.Copy)\
                           .then_inc(s["g_kept"], 1)
                    if gated_out:
                        for k in range(units):
                            act.wait_ge(s["up"], k + 1)
                            if k >= 2:
                                act.wait_ge(s["down"], k - 1)
                            act.activation(HT[:, k % 2, :], PS[k % 2][:, :], ACT.Gelu if l == 0 else ACT.Relu,
                                           bias=col(f"b1_{l}", k)).then_inc(s["acted"], 1)
                    else:
                        for k in range(units):
                            z = sizes[k % (2 * nch) // 2]
                            act.wait_ge(s["up"], k + 1)
                            if k >= 2:
                                act.wait_ge(s["h_made"], k - 1)
                            act.activation(HT[0:z, 4 + k % 2, :], PS[k % 3][0:z, 0:512],
                                           ACT.Gelu if l == 1 else ACT.Silu).then_inc(s["acted"], 1)

                @block.tensor
                def _(pe):
                    pe.wait_ge(s["norm_rows"], 2 * NT if l == 0 else NT)
                    if final:
                        pe.wait_ge(s["affine"], 2)
                    turn_rows(pe, s, XN, PS[0], "turned")
                    src = XNT
                    pe.wait_ge(s["kept"], 2)
                    if l == 0:
                        pe.wait_ge(s["scaled_r"], 1)
                        src = U[:, 0, :]
                    for t in range(NT):
                        ins = pe.matmul(PS[1][:, t * NE:(t + 1) * NE], src[:, t * P:(t + 1) * P], WR[:, l, :],
                                        start=True, stop=True)
                    ins.then_inc(s["routed"], 1)
                    if not final:
                        prep_tensor(pe, s, prep, CTX, 4)
                    pe.wait_ge(s["gates"], 1)
                    for t in range(NT):
                        ins = pe.transpose(PS[1][0:NE, t * P:(t + 1) * P], GA[6][:, t, :], IDF[:, :])
                        if t % 4 == 3:
                            ins.then_inc(s["g_turned"], 1)
                    if not final:
                        pe.wait_ge(s["v_kept"], 4)
                        pe.wait_ge(s["k_rest"], 4)
                    pe.wait_ge(s["g_kept"], 2)
                    if gated_out:
                        for h in range(2):
                            ins = pe.matmul(PS[3][:, h * TH:(h + 1) * TH], B2[:, l // 3, :], GT[:, h * TH:(h + 1) * TH],
                                            start=True, stop=True)
                        ins.then_inc(s["acc0_made"], 1)

                        def up(k):
                            e, c = k // nch, k % nch
                            if c == 0:
                                pe.wait_ge(s[f"w_loaded{e % 2}"], 16 * (e // 2 + 1))
                                if l == 0:
                                    pe.wait_ge(s["u_made"], e + 1)
                            if k >= 2:
                                pe.wait_ge(s["acted"], k - 1)
                            x = U[:, e % 2, :] if l == 0 else XNT[:, :]
                            for h in range(2):
                                ins = pe.matmul(PS[k % 2][:, h * TH:(h + 1) * TH], W[:, e % 2, c * P:(c + 1) * P],
                                                x[:, h * TH:(h + 1) * TH], start=True, stop=True)
                            ins.then_inc(s["up"], 1)

                        def down(k):
                            e, c = k // nch, k % nch
                            pe.wait_ge(s["acted"], k + 1)
                            if c == 0 and e == 1:
                                pe.wait_ge(s["acc0"], 1)
                            if c == 0 and e >= 2:
                                pe.wait_ge(s["y_used"], e - 1)
                            for h in range(2):
                                ins = pe.matmul(PS[2 + e % 2][:, h * TH:(h + 1) * TH],
                                                W[:, e % 2, (nch + c) * P:(nch + c + 1) * P],
                                                HT[:, k % 2, h * TH:(h + 1) * TH], start=(c == 0), stop=(c == nch - 1))
                            ins.then_inc(s["down"], 1)
                        up(0)
                        for k in range(units):
                            if k + 1 < units:
                                up(k + 1)
                            down(k)
                        pe.wait_ge(s["added"], NE)
                    else:
                        def up(k):
                            e, c, h = k // (2 * nch), k % (2 * nch) // 2, k % 2
                            z = sizes[c]
                            if k % (2 * nch) == 0:
                                pe.wait_ge(s[f"w_loaded{e % 2}"], 16 * (e // 2 + 1))
                                pe.wait_ge(s["u_made"], e + 1)
                            if k >= 3:
                                pe.wait_ge(s["h_made"], k - 2)
                            pe.matmul(PS[k % 3][0:z, 0:512], W[:, e % 2, c * P:c * P + z],
                                      XNT[:, h * TH:(h + 1) * TH], start=True, stop=True)
                            pe.matmul(PS[k % 3][0:z, 512:1024], W[:, e % 2, hid + c * P:hid + c * P + z],
                                      U[:, e % 2, h * TH:(h + 1) * TH], start=True, stop=True).then_inc(s["up"], 1)

                        def down(k):
                            e, c, h = k // (2 * nch), k % (2 * nch) // 2, k % 2
                            z = sizes[c]
                            pe.wait_ge(s["h_made"], k + 1)
                            pe.matmul(PS[3][:, h * TH:(h + 1) * TH], W[0:z, e % 2, 2 * hid + c * P:2 * hid + (c + 1) * P],
                                      HT[0:z, k % 3, :], start=(e == 0 and c == 0),
                                      stop=(e == NE - 1 and c == nch - 1)).then_inc(s["down"], 1)
                        up(0)
                        up(1)
                        for k in range(units):
                            if k + 2 < units:
                                up(k + 2)
                            down(k)
                        pe.wait_ge(s["acc"], 1)
                    for t in range(NT):
                        ins = pe.transpose(PS[0][:, t * P:(t + 1) * P], ACC[:, t * P:(t + 1) * P], IDF[:, :])
                        if t % 4 == 3:
                            ins.then_inc(s["back"], 1)
    

        def convolution():
            s = signals(nc, "conv", "var rstd norm_rows chain turned padded border made kept back rows "
                        + prep_names(), before)
            with nc.Block() as block:
                @block.sync
                def _(sp):
                    prep_sync(sp, s, 4, 2)
                    sp.wait_ge(s["k_placed"], 96 * 2)

                @block.gpsimd
                def _(pool):
                    for i in (0, SQ + 1):
                        pool.memset(XPAD[:, :, i:i + 1], 0.0).then_inc(s["border"], 1)
                    norm_pool(pool, s, 1)
                    prep_pool(pool, s, 4, 2)

                @block.vector
                def _(dve):
                    norm_vector(dve, s, X, EPS, Chain(dve, s["chain"]), 1)
                    for h in range(2):
                        dve.wait_ge(s["back"], h + 1)
                        dve.tensor_copy(XN[:, 4 * h:4 * h + 4, :],
                                        PS[0][:, h * TH:(h + 1) * TH].rearrange("p (t e) -> p t e", t=4))\
                           .then_inc(s["rows"], 1)
                    prep_vector(dve, s, 4, 2)

                @block.scalar
                def _(act):
                    for h in range(2):
                        act.wait_ge(s["turned"], h + 1)
                        act.activation(XPAD[:, 2 * h:2 * h + 2, 1:SQ + 1],
                                       PS[0][:, h * TH:(h + 1) * TH].rearrange("p (b n) -> p b n", b=2), ACT.Copy)\
                           .then_inc(s["padded"], 1)
                    for h in range(2):
                        act.wait_ge(s["made"], h + 1)
                        act.activation(XNT[:, h * TH:(h + 1) * TH], PS[1][:, h * TH:(h + 1) * TH], ACT.Identity,
                                       bias=col("conv_b")).then_inc(s["kept"], 1)
                    prep_scalar(act, s, 4, 2)

                @block.tensor
                def _(pe):
                    pe.wait_ge(s["norm_rows"], NT)
                    turn_rows(pe, s, XN, PS[0], "turned")
                    pe.wait_ge(s["border"], 2)
                    for h in range(2):
                        pe.wait_ge(s["padded"], h + 1)
                        for i in range(3):
                            ins = pe.matmul(PS[1][:, h * TH:(h + 1) * TH], WCONV[:, i, :],
                                            XPAD[:, 2 * h:2 * h + 2, i:i + SQ], start=(i == 0), stop=(i == 2))
                        ins.then_inc(s["made"], 1)
                    for h in range(2):
                        pe.wait_ge(s["kept"], h + 1)
                        for t in range(4 * h, 4 * h + 4):
                            ins = pe.transpose(PS[0][:, t * P:(t + 1) * P], XNT[:, t * P:(t + 1) * P], IDF[:, :])
                        ins.then_inc(s["back"], 1)
                    prep_tensor(pe, s, 4, XNT, 2)
    
        for l in range(4):
            attention(l)
            if l == 3:
                convolution()
                attention(4)
            experts(l)



def kernel(**inputs):
    import concourse.bacc as _bacc
    from concourse.bass_utils import run_bass_kernel_spmd as _run

    x = {k: np.asarray(v) for k, v in inputs.items()}
    f32 = np.float32
    zeros = np.zeros(P, f32)
    order = np.array([(2 * p + m) * DH + e for m in range(2) for e in range(DH) for p in range(NP)])
    wqkv, bqkv = x["L3_ffn_wqkv"], x["L3_ffn_bqkv"]
    w = [[x["L0_xattn_Wq"].T, x["L0_xattn_Wk"].T, x["L0_xattn_Wv"].T, x["L0_xattn_Wo"].T],
         [x["L1_xattn_Wq"].T, x["L1_xattn_Wk"].T, x["L1_xattn_Wv"].T, x["L1_xattn_Wo"].T],
         [x["L2_xattn_Wq"], x["L2_xattn_Wk"], x["L2_xattn_Wv"], x["L2_xattn_Wo"]],
         [x["L3_xattn_wq_w"].T, x["L3_xattn_wk_w"].T, x["L3_xattn_wv_w"].T, x["L3_xattn_proj_w"].T],
         [wqkv[0:P].T, wqkv[P:2 * P].T, wqkv[2 * P:].T, x["L3_ffn_wo"].T]]
    bq = [zeros, x["L1_xattn_bq"], zeros, x["L3_xattn_wq_b"], bqkv[0:P]]
    bk = [zeros, x["L1_xattn_bk"], zeros, x["L3_xattn_wk_b"], bqkv[P:2 * P]]
    bv = [zeros, x["L1_xattn_bv"], zeros, x["L3_xattn_wv_b"], bqkv[2 * P:]]
    bo = [zeros, x["L1_xattn_bo"], x["L2_xattn_bo"], x["L3_xattn_proj_b"], x["L3_ffn_bo"]]
    wattn = np.stack([np.stack([q[:, order], k[:, order], v, o], 1) for q, k, v, o in w], 1)
    cols = [b[order] for b in bq] + [b[order] for b in bk] + bv
    cols += [x["L3_ffn_conv_b"], x["L1_ffn_bias"], x["L0_ffn_router_ln_scale"], x["L0_ffn_router_ln_bias"]]
    cols += list(x["L0_ffn_expert_ln_scale"]) + list(x["L0_ffn_expert_ln_bias"])
    cols += list(x["L0_ffn_b1"].reshape(-1, P)) + list(x["L3_ffn_b1"].reshape(-1, P))
    rows = bo + [x["L0_ffn_router_b"], x["L3_ffn_gate_b"], x["L3_ffn_ln1_g"], x["L3_ffn_ln1_b"],
                 x["L3_ffn_ln2_g"], x["L3_ffn_ln2_b"]]

    def tiles(a):
        n = -(-a.shape[1] // P)
        full = np.zeros((a.shape[0], n * P, a.shape[2]), a.dtype)
        full[:, 0:a.shape[1]] = a
        return full.reshape(a.shape[0], n, P, -1).transpose(0, 2, 1, 3).reshape(a.shape[0], P, -1)

    t = (0, 2, 1)
    we = [np.concatenate([x["L0_ffn_w1"].transpose(t), tiles(x["L0_ffn_w2"].transpose(t))], 2),
          np.concatenate([x["L1_ffn_w1"], x["L1_ffn_v1"], tiles(x["L1_ffn_w2"])], 2),
          np.concatenate([x["L2_ffn_w_gate"].transpose(t), x["L2_ffn_w_up"].transpose(t),
                          tiles(x["L2_ffn_w_down"].transpose(t))], 2),
          np.concatenate([x["L3_ffn_w1"], tiles(x["L3_ffn_w2"])], 2)]
    data = {
        "x": x["x"].reshape(T, P),
        "ctxT": x["ctx_1024"].reshape(TK, P).T,
        "mask0": x["mask_Bx1x1xS2_bf1"].reshape(1, TK),
        "mask_keys": x["mask_BxS2_bk0"].reshape(TK),
        "mask2": x["mask_SxS2_bk1"],
        "mask2T": x["mask_SxS2_bk1"].T,
        "wattn": wattn,
        "cols": np.stack(cols, 1),
        "rows": np.concatenate(rows),
        "wconv": x["L3_ffn_conv_w"].transpose(1, 2, 0),
        "wrouter": np.stack([x["L0_ffn_router_w"].T, x["L1_ffn_router_w"], x["L2_ffn_router_w"].T,
                             x["L3_ffn_gate_w"]], 1),
        "b2": np.stack([x["L0_ffn_b2"], x["L3_ffn_b2"]], 1),
        "we0": we[0], "we1": we[1], "we2": we[2], "we3": we[3],
    }
    nc = _bacc.Bacc("TRN2", target_bir_lowering=False, num_devices=1)
    arrays, args = {}, {}
    for name, a in data.items():
        a = np.ascontiguousarray(a)
        arrays[f"in_{name}"] = a
        args[name] = nc.dram_tensor(f"in_{name}", a.shape, mybir.dt.from_np(a.dtype), kind="ExternalInput").ap()
    out = nc.dram_tensor("out", (T, P), F32, kind="ExternalOutput").ap()
    build(nc, args, out)
    r = _run(nc, [arrays], core_ids=[0])
    return r.results[0]["out"].reshape(B, SQ, P)
```

```python
from contextlib import ExitStack

import numpy as np

import concourse.bass as bass
from concourse import mybir

F32 = mybir.dt.float32
BF16 = mybir.dt.bfloat16
U8 = mybir.dt.uint8
U32 = mybir.dt.uint32
ALU = mybir.AluOpType
ACT = mybir.ActivationFunctionType
AX = mybir.AxisListType

P = 128
B, SQ, SK = 4, 256, 512
T = B * SQ
NT = T // P
TH = T // 2
TK = B * SK
HEADS, DH = 16, 8
NP = HEADS // 2
GROUP = 4
NG = HEADS // GROUP
NE = 8
SCALE = float(DH) ** -0.5
NEG = -1.0e30
EPS, EPS_IN = 1e-5, 1e-6
VW = 9 * HEADS + 24
CW = 6 * DH
MASK_ROW, SHIFT_ROW = 2 * CW, 2 * CW + 1


COLS = {}
_n = 0
for _name, _w in [(f"bq{a}", 1) for a in range(5)] + [(f"bk{a}", 1) for a in range(5)] + \
        [(f"bv{a}", 1) for a in range(5)] + \
        [("conv_b", 1), ("rln_s", 1), ("rln_b", 1), ("eln_s", NE), ("eln_b", NE),
         ("b1_0", 4 * NE), ("b1_3", 4 * NE), ("b2_0", NE), ("b2_3", NE)]:
    COLS[_name] = (_n, _w)
    _n += _w
NCOLS = _n
ROWS = {}
_n = 0
for _name, _w in [(f"bo{a}", P) for a in range(5)] + \
        [("ffn1_bias", P), ("router_b0", NE), ("router_b3", NE), ("ln1_g", P), ("ln1_b", P), ("ln2_g", P), ("ln2_b", P)]:
    ROWS[_name] = (_n, _w)
    _n += _w
NROWS = _n
HID = [512, 352, 256, 512]
EW = [4 * P + 4 * P, 2 * 352 + 3 * P, 2 * 256 + 2 * P, 4 * P + 4 * P]


def signals(nc, phase, names, before):
    s = {n: nc.alloc_semaphore(f"{phase}_{n}") for n in names.split()}
    if before:
        nc.clear_and_free_semaphores(before.pop())
    before.append(list(s.values()))
    return s


class Chain:

    def __init__(self, eng, sem):
        self.eng, self.sem, self.n = eng, sem, 0

    def __call__(self, ins):
        self.n += 1
        ins.then_inc(self.sem, 1)
        self.eng.wait_ge(self.sem, self.n)


def build(nc, d, out):
    ctx = ExitStack()
    with ctx:
        def sb(name, shape, dt=F32):
            return ctx.enter_context(nc.sbuf_tensor(name, shape, dt))

        X = sb("X", [P, NT, P])
        XN = sb("XN", [P, NT, P])
        XNT = sb("XNT", [P, T])
        CTX = sb("CTX", [P, TK])
        KOP = sb("KOP", [P, 4, NP, 512], BF16)
        QOP = sb("QOP", [P, 2, HEADS, TH], BF16)
        V = sb("V", [P, TK // P, VW])
        SHARED = sb("SHARED", [P, 8 * 1024])
        PT = SHARED[:, :].rearrange("p (u n) -> p u n", u=8)
        GB = PT
        XPAD = SHARED[:, 0:B * (SQ + 2)].rearrange("p (b n) -> p b n", b=B)
        HI = sb("HI", [P, 2, 512], BF16)
        MID = sb("MID", [P, 2, 512], BF16)
        LO = sb("LO", [P, 2, 512], BF16)
        REST = sb("REST", [P, 2, 512])
        KEEP = sb("KEEP", [P, TK], U8)
        WA = sb("WA", [P, 5, 4, P])
        WCONV = sb("WCONV", [P, 3, P])
        WR = sb("WR", [P, 4, NE])
        C = sb("C", [P, NCOLS])
        R = sb("R", [P, NROWS])
        W = sb("W", [P, 2, max(EW)])
        H = sb("H", [P, 3 * 1024])
        U = sb("U", [P, 2, T])
        KEYS = H[:, 2048:3072].rearrange("p (i n) -> p i n", i=2)
        masks = U[:, 0, :].bitcast(U8)
        M0 = masks[:, 0:TK]
        MASKS0 = U[:, 1, :].bitcast(BF16)
        M2 = masks[:, TK:TK + 2 * SK].rearrange("p (t k) -> p t k", t=2)
        M2T = masks[:, TK + 2 * SK:TK + 2 * SK + 4 * SQ].rearrange("p (t k) -> p t k", t=4)
        ACC = sb("ACC", [P, T])
        OT = sb("OT", [P, 2, 256])
        ON = sb("ON", [P, 2, 2, P])
        CT = sb("CT", [P, 2, 256])
        RC = sb("RC", [P, 2, 2, GROUP])
        NM = sb("NM", [P, 4, 2, GROUP])
        NG32 = sb("NG32", [P, 4, 2, GROUP])
        HL = sb("HL", [P, 4, 2, 2, GROUP], BF16)
        ONES = sb("ONES", [P, 512], BF16)
        SEEN = ACC[:, :].rearrange("p (i k) -> p i k", i=2)
        SH = sb("SH", [2 * GROUP, 2, 256], BF16)
        IDF = sb("IDF", [P, P])
        IDB = sb("IDB", [P, P], BF16)
        NEGC = sb("NEGC", [P, SK], BF16)
        STAIR = sb("STAIR", [P, 32], BF16)
        NEG2 = sb("NEG2", [P, 2, SK], BF16)
        NEG2T = sb("NEG2T", [P, 4, SQ], BF16)
        ST8 = sb("ST8", [P, NT, 6])
        MV = sb("MV", [P, NT, 2])
        VE = sb("VE", [P, NT])
        HALF = sb("HALF", [P, NT])
        RSTD = sb("RSTD", [P, NT])
        LG = sb("LG", [P, NT, NE])
        MX = sb("MX", [P, NT, NE])
        IX = sb("IX", [P, NT, NE], U32)
        IXF = sb("IXF", [P, NT, NE])
        IOTA = sb("IOTA", [P, NT, NE])
        GA = [sb(f"GA{i}", [P, NT, NE]) for i in range(8)]
        G1 = [sb(f"G1{i}", [P, NT]) for i in range(2)]
        GT = ACC[0:NE, :]

        PS = [ctx.enter_context(nc.psum_tensor(f"PS{i}", [P, 1024], F32)) for i in range(4)]

        q_parts = nc.dram_tensor("q_parts", [2, 3, P, TH], BF16).ap()
        k_parts = nc.dram_tensor("k_parts", [4, 3, P, 512], BF16).ap()
        g_rows = nc.dram_tensor("g_rows", [NE, T], F32).ap()

        def col(name, i=0, n=1, rows=P):
            a = COLS[name][0] + i
            return C[0:rows, a:a + n]

        def row(name):
            a, w = ROWS[name]
            return R[:, a:a + w]

        before = []


        def norm_vector(dve, s, src, eps, chain, n):
            for h in range(2):
                for t in range(4 * h, 4 * h + 4):
                    ins = dve.bn_stats(ST8[:, t, :], src[:, t, :])
                chain(ins)
                for t in range(4 * h, 4 * h + 4):
                    ins = dve.bn_aggr(MV[:, t, :], ST8[:, t, :])
                chain(ins)
                dve.tensor_scalar(VE[:, 4 * h:4 * h + 4], MV[:, 4 * h:4 * h + 4, 1], eps, None, ALU.add)\
                   .then_inc(s["var"], 1)
            for t in range(NT):
                if t % 4 == 0:
                    dve.wait_ge(s["rstd"], 2 * n - 1 + t // 4)
                dve.tensor_scalar(XN[:, t, :], src[:, t, :], MV[:, t, 0:1], RSTD[:, t:t + 1],
                                  ALU.subtract, ALU.mult).then_inc(s["norm_rows"], 1)
            dve.wait_ge(s["norm_rows"], NT * n)

        def norm_pool(pool, s, n):
            for h in range(2):
                x = slice(4 * h, 4 * h + 4)
                pool.wait_ge(s["var"], 2 * n - 1 + h)
                pool.tensor_tensor(RSTD[:, x], VE[:, x], HALF[:, x], ALU.pow).then_inc(s["rstd"], 1)

        def affine_rows(dve, sem, before, g, b):
            for i, (name, op) in enumerate(((g, ALU.mult), (b, ALU.add))):
                dve.tensor_tensor(XN[:, :, :], XN[:, :, :], row(name).unsqueeze(1).to_broadcast([P, NT, P]), op)\
                   .then_inc(sem, 1)
                dve.wait_ge(sem, before + i + 1)

        def turn_rows(pe, s, src, dst, name):
            for t in range(NT):
                ins = pe.transpose(dst[:, t * P:(t + 1) * P], src[:, t, :], IDF[:, :])
                if t % 4 == 3:
                    ins.then_inc(s[name], 1)

        PREP_NAMES = "k_made v_made v_kept k_kept k_hi k_rest k_mid k_lo k_stored0 k_stored1 " \
                     "k_placed0 k_placed1 k_placed2 k_placed3"

        def prep_tensor(pe, s, a, src, c):
            if c >= 2:
                pe.wait_ge(s["k_kept"], c - 1)
            pe.matmul(PS[2][:, (c % 2) * 512:(c % 2) * 512 + 512], WA[:, a, 1, :],
                      src[:, c * 512:(c + 1) * 512], start=True, stop=True).then_inc(s["k_made"], 1)
            if c >= 2:
                pe.wait_ge(s["v_kept"], c - 1)
            for t in range(4):
                ins = pe.matmul(PS[3][:, (c % 2) * 512 + t * P:(c % 2) * 512 + (t + 1) * P],
                                src[:, (4 * c + t) * P:(4 * c + t + 1) * P], WA[:, a, 2, :],
                                start=True, stop=True)
            ins.then_inc(s["v_made"], 1)

        def prep_scalar(act, s, a, c):
            i = c % 2
            if a != 2:
                act.wait_ge(s["k_made"], c + 1)
                if c >= 2:
                    act.wait_ge(s["k_rest"], c - 1)
                act.activation(KEYS[:, i, :], PS[2][:, i * 512:i * 512 + 512], ACT.Identity, bias=col(f"bk{a}"))\
                   .then_inc(s["k_kept"], 1)
            act.wait_ge(s["k_kept"], c + 1)
            if c >= 2:
                act.wait_ge(s[f"k_stored{i}"], 48 * (c // 2))
            act.activation(HI[:, i, :], KEYS[:, i, :], ACT.Copy).then_inc(s["k_hi"], 1)
            act.wait_ge(s["v_made"], c + 1)
            o = V[:, 4 * c:4 * c + 4, 0:9 * HEADS].rearrange("p t (h e) -> p t h e", e=9)[:, :, :, 0:DH]
            act.activation(o, PS[3][:, i * 512:i * 512 + 512].rearrange("p (t h e) -> p t h e", t=4, e=DH), ACT.Copy)\
               .then_inc(s["v_kept"], 1)

        def prep_middle(act, s, c):
            i = c % 2
            act.wait_ge(s["k_rest"], c + 1)
            act.activation(MID[:, i, :], REST[:, i, :], ACT.Copy).then_inc(s["k_mid"], 1)

        def prep_vector(dve, s, c):
            i = c % 2
            dve.wait_ge(s["k_made"], c + 1)
            if c >= 2:
                dve.wait_ge(s["k_rest"], c - 1)
            dve.scalar_tensor_tensor(KEYS[:, i, :], KEEP[:, c * 512:(c + 1) * 512], 0.0,
                                     PS[2][:, i * 512:i * 512 + 512], ALU.is_equal, ALU.mult)\
               .then_inc(s["k_kept"], 1)

        def prep_pool(pool, s, c):
            i = c % 2
            pool.wait_ge(s["k_hi"], c + 1)
            if c >= 2:
                pool.wait_ge(s["k_lo"], c - 1)
            pool.tensor_tensor(REST[:, i, :], KEYS[:, i, :], HI[:, i, :], ALU.subtract).then_inc(s["k_rest"], 1)
            pool.wait_ge(s["k_mid"], c + 1)
            if c >= 2:
                pool.wait_ge(s[f"k_stored{i}"], 48 * (c // 2))
            pool.tensor_tensor(LO[:, i, :], REST[:, i, :], MID[:, i, :], ALU.subtract).then_inc(s["k_lo"], 1)

        def prep_store(sp, s, c):
            for r, (part, name) in enumerate(((HI, "k_hi"), (MID, "k_mid"), (LO, "k_lo"))):
                sp.wait_ge(s[name], c + 1)
                sp.dma_start(k_parts[c, r], part[:, c % 2, :]).then_inc(s[f"k_stored{c % 2}"], 16)

        def prep_place(sp, s, c):
            sp.wait_ge(s[f"k_stored{c % 2}"], 48 * (c // 2 + 1))
            for m in range(2):
                src = k_parts[c, :, m * 64:(m + 1) * 64, :].rearrange("r (d p) n -> r d (p n)", p=NP)
                r0 = m * CW
                sp.dma_start(KOP[r0:r0 + 24, c, :, :], src[0:3]).then_inc(s[f"k_placed{c}"], 16)
                sp.dma_start(KOP[r0 + 24:r0 + 40, c, :, :], src[0:2]).then_inc(s[f"k_placed{c}"], 16)
                sp.dma_start(KOP[r0 + 40:r0 + 48, c, :, :], src[0]).then_inc(s[f"k_placed{c}"], 16)


        stored = nc.alloc_semaphore("stored")
        ctx_in = nc.alloc_semaphore("ctx_in")
        s = signals(nc, "load", "x wk mask c zero idf ones neg mask_row k0", before)
        with nc.Block() as block:
            @block.sync
            def _(sp):
                sp.dma_start(M0[MASK_ROW:MASK_ROW + 1, :], d["mask0"]).then_inc(s["mask"], 16)
                sp.dma_start(X[:, :, :], d["x"].rearrange("(t p) e -> p t e", p=P)).then_inc(s["x"], 16)
                sp.dma_start(WA[:, 0, :, :], d["wattn"][:, 0, :, :]).then_inc(s["wk"], 16)
                sp.dma_start(C[:, :], d["cols"]).then_inc(s["c"], 16)
                sp.wait_ge(s["ones"], 1)
                ones = ONES[MASK_ROW:MASK_ROW + 3, :].unsqueeze(1)
                sp.dma_start(QOP[MASK_ROW:MASK_ROW + 1, :, :, :].rearrange("r a b n -> r (a b) n"),
                             ones[0:1].to_broadcast([1, 32, 512])).then_inc(s["k0"], 16)
                sp.dma_start(KOP[MASK_ROW + 1:MASK_ROW + 3, :, :, :].rearrange("r a b n -> r (a b) n"),
                             ones[1:3].to_broadcast([2, 32, 512])).then_inc(s["k0"], 16)
                sp.wait_ge(s["mask_row"], 1)
                for c in range(4):
                    sp.dma_start(KOP[MASK_ROW:MASK_ROW + 1, c, :, :],
                                 MASKS0[MASK_ROW:MASK_ROW + 1, c * 512:(c + 1) * 512].unsqueeze(1)
                                 .to_broadcast([1, NP, 512])).then_inc(s["k0"], 16)
                sp.wait_ge(s["c"], 16)
                sp.wait_ge(s["wk"], 16)
                sp.wait_ge(s["x"], 16)
                sp.wait_ge(s["k0"], 96)

            @block.gpsimd
            def _(pool):
                pool.memset(IDF[:, :], 0.0).then_inc(s["zero"], 1)
                pool.memset(HALF[:, :], -0.5)
                pool.memset(NEGC[:, :], 0.0).then_inc(s["zero"], 1)
                pool.memset(STAIR[:, :], 0.0).then_inc(s["zero"], 1)
                pool.wait_ge(s["zero"], 3)
                pool.affine_select(out=IDF[:, :], in_=IDF[:, :], compare_op=ALU.not_equal, fill=1.0, base=0,
                                   pattern=[[-1, P]], channel_multiplier=1).then_inc(s["idf"], 1)
                pool.affine_select(out=NEGC[:, :], in_=NEGC[:, :], compare_op=ALU.is_ge, fill=NEG, base=3,
                                   pattern=[[-1, SK]], channel_multiplier=4).then_inc(s["neg"], 1)
                pool.affine_select(out=STAIR[:, :], in_=STAIR[:, :], compare_op=ALU.is_ge, fill=NEG, base=3,
                                   pattern=[[4, 32]], channel_multiplier=-1).then_inc(s["neg"], 1)
                for e in range(NE):
                    pool.memset(IOTA[:, :, e], float(e))
                pool.wait_ge(s["idf"], 1)
                pool.tensor_copy(IDB[:, :], IDF[:, :]).then_inc(s["neg"], 1)
                pool.memset(V[:, :, :], 1.0)
                pool.memset(QOP[0:MASK_ROW, 1, :, :].rearrange("p b n -> p (b n)").bitcast(F32), 0.0)

            @block.vector
            def _(dve):
                dve.memset(ONES[:, :], 1.0).then_inc(s["ones"], 1)
                dve.wait_ge(s["mask"], 16)
                dve.tensor_scalar(MASKS0[MASK_ROW:MASK_ROW + 1, :], M0[MASK_ROW:MASK_ROW + 1, :],
                                  -NEG, NEG, ALU.mult, ALU.add).then_inc(s["mask_row"], 1)
                dve.memset(QOP[0:MASK_ROW, 0, :, :].rearrange("p b n -> p (b n)").bitcast(F32), 0.0)

            @block.scalar
            def _(act):
                act.dma_start(CTX[:, :], d["ctxT"]).then_inc(ctx_in, 16)


        def attention(a):
            own = a == 4
            nk = SQ if own else SK
            nkt = nk // P
            stairs = a == 1
            if stairs:
                places = [(0, 0), (512, 32), (512 + 224, 64), (256, 96)]
                width, banks = 416, 2
            elif own:
                places = [(0, 0), (256, 0)]
                width, banks = 512, 1
            else:
                places = [(256 * i, 0) for i in range(4)]
                width, banks = 512, 2
            rows_out = XN if own else X
            last = B * NG
            look = 3
            chunks = {0: 4, 4: 2}.get(a, 0)
            QHI, QMID, QLO = (H[:, i * 512:(i + 1) * 512].bitcast(BF16).rearrange("p (h n) -> p h n", h=2)
                              for i in range(3))
            QREST = U[:, 1, :].rearrange("p (h n) -> p h n", h=2)

            def spot(k):
                return k // NG, k % NG // 2, 4 * (k % 2)

            def queries(k, j, lo, n, rows):
                b, m, p0 = spot(k)
                x = (b % 2) * SQ + lo
                return QOP[0:rows, b // 2, m * NP + p0 + j, x:x + n]

            def keys(k, j, lo, n, rows):
                b, m, p0 = spot(k)
                x = b * nk + lo
                return KOP[0:rows, x // 512, p0 + j, x % 512:x % 512 + n]

            def filled(t):
                return t.rearrange("p (k n) -> p k n", k=2)[:, 0:banks, 0:width]

            turn = {}
            for n in range(-look, last + 2):
                if 0 <= n - 2:
                    turn["rows", n - 2] = len(turn)
                if 0 <= n + look - 1 < last:
                    turn["shift", n + look - 1] = len(turn)
                if n - 2 >= 0 and (n - 2) % NG == NG - 1:
                    turn["cols", (n - 2) // NG] = len(turn)
                    turn["out", (n - 2) // NG] = len(turn)

            s = signals(nc, f"attn{a}", "var rstd norm_rows chain turned kept q_made q_hi q_rest q_mid q_lo "
                        "q_stored0 q_stored1 q_stored2 q_placed0 q_placed1 biased scored maxed neg shift "
                        "shift_placed0 shift_placed1 scored_t exps summed o_kept x_made x_read rc late mask "
                        + (PREP_NAMES if chunks else ""), before)
            SUM = PS[3][:, 0:256]
            XB = PS[3][:, 512:1024]
            XBH = XB.bitcast(BF16)

            with nc.Block() as block:
                @block.sync
                def _(sp):
                    parts = ((QHI, "q_hi", 0, 3), (QMID, "q_mid", 24, 2), (QLO, "q_lo", 40, 1))

                    def store(h, r):
                        part, name = parts[r][0:2]
                        sp.wait_ge(s[name], h + 1)
                        sp.dma_start(q_parts[h, r], part[:, h, :]).then_inc(s[f"q_stored{r}"], 16)

                    def place(h, r):
                        r0, n = parts[r][2:4]
                        sp.wait_ge(s[f"q_stored{r}"], 16 * (h + 1))
                        for m in range(2):
                            src = q_parts[h, r, m * 64:(m + 1) * 64, :].rearrange("(d p) n -> d (p n)", p=NP)
                            if n > 1:
                                src = src.unsqueeze(0).to_broadcast([n, DH, NP * TH])
                            sp.dma_start(QOP[m * CW + r0:m * CW + r0 + n * DH, h, m * NP:(m + 1) * NP, :],
                                         src).then_inc(s[f"q_placed{h}"], 16)
                    if a == 0:
                        sp.dma_start(M2[:, :, :], d["mask2"].rearrange("(t q) k -> q t k", q=P)).then_inc(s["mask"], 16)
                        sp.dma_start(M2T[:, :, :], d["mask2T"].rearrange("(t k) q -> k t q", k=P))\
                          .then_inc(s["mask"], 16)
                    if chunks:
                        prep_store(sp, s, 0)
                    for r in range(3):
                        store(0, r)
                    if chunks:
                        prep_place(sp, s, 0)
                        prep_store(sp, s, 1)
                    for r in range(3):
                        place(0, r)
                    for r in range(3):
                        store(1, r)
                    if chunks:
                        prep_place(sp, s, 1)
                    for r in range(3):
                        place(1, r)

                    def late_loads():
                        sp.dma_start(R[:, :], d["rows"].partition_broadcast(P)).then_inc(s["late"], 16)
                        sp.dma_start(WR[:, :, :], d["wrouter"]).then_inc(s["late"], 16)
                        sp.dma_start(WCONV[:, :, :], d["wconv"]).then_inc(s["late"], 16)
                        sp.dma_start(WA[:, 1:5, :, :], d["wattn"][:, 1:5, :, :]).then_inc(s["late"], 16)
                        sp.dma_start(KEEP[:, :], d["mask_keys"].partition_broadcast(P)).then_inc(s["late"], 16)
                    for k in range(last):
                        b, m, p0 = spot(k)
                        sp.wait_ge(s["x_read"], turn["shift", k] + 1)
                        for r in range(2):
                            sp.dma_start(QOP[SHIFT_ROW + r:SHIFT_ROW + r + 1, b // 2,
                                             m * NP + p0:m * NP + p0 + GROUP,
                                             (b % 2) * SQ:(b % 2) * SQ + SQ],
                                         SH[r * GROUP:(r + 1) * GROUP, k % 2, :])\
                              .then_inc(s[f"shift_placed{k % 2}"], 16)
                        if k + 2 < chunks:
                            prep_store(sp, s, k + 2)
                            prep_place(sp, s, k + 2)
                        if a == 0 and k == 2:
                            late_loads()
                    for r in range(2):
                        sp.wait_ge(s[f"shift_placed{r}"], 32 * last // 2)
                    if a == 0:
                        sp.wait_ge(s["late"], 80)

                @block.gpsimd
                def _(pool):
                    if not own:
                        norm_pool(pool, s, 1)
                    if not own:
                        pool.wait_ge(s["norm_rows"], NT)
                    if a > 0:
                        pool.tensor_tensor(rows_out[:, :, :], rows_out[:, :, :],
                                           row(f"bo{a}").unsqueeze(1).to_broadcast([P, NT, P]), ALU.add)\
                            .then_inc(s["biased"], 1)
                    for c in range(chunks):
                        prep_pool(pool, s, c)
                    for k in range(last):
                        pool.wait_ge(s["maxed"], 2 * GROUP * (k + 1))
                        if k >= 4:
                            pool.wait_ge(s["x_made"], turn["shift", k - 4] + 1)
                        pool.tensor_scalar(NG32[:, k % 4], NM[:, k % 4], -1.0, None, ALU.mult)\
                            .then_inc(s["neg"], 1)
                        pool.wait_ge(s["neg"], 2 * k + 1)
                        pool.tensor_copy(HL[:, k % 4, :, 0, :], NG32[:, k % 4]).then_inc(s["neg"], 1)
                        pool.wait_ge(s["neg"], 2 * k + 2)
                        pool.tensor_tensor(HL[:, k % 4, :, 1, :], NG32[:, k % 4], HL[:, k % 4, :, 0, :],
                                           ALU.subtract).then_inc(s["shift"], 1)

                @block.vector
                def _(dve):
                    chain = Chain(dve, s["chain"])
                    if not own:
                        norm_vector(dve, s, X, EPS, chain, 1)
                    for h in range(2):
                        dve.wait_ge(s["q_hi"], h + 1)
                        dve.scalar_tensor_tensor(QREST[:, h, :], PS[1][:, h * TH:(h + 1) * TH], col(f"bq{a}"),
                                                 QHI[:, h, :], ALU.add, ALU.subtract).then_inc(s["q_rest"], 1)
                        dve.wait_ge(s["q_rest"], h + 1)
                        dve.tensor_copy(QMID[:, h, :], QREST[:, h, :]).then_inc(s["q_mid"], 1)
                        dve.wait_ge(s["q_mid"], h + 1)
                        dve.tensor_tensor(QLO[:, h, :], QREST[:, h, :], QMID[:, h, :], ALU.subtract)\
                           .then_inc(s["q_lo"], 1)
                    if a == 0:
                        dve.wait_ge(s["mask"], 32)
                        dve.tensor_scalar(NEG2[:, :, :], M2[:, :, :], NEG, None, ALU.mult)
                        dve.tensor_scalar(NEG2T[:, :, :], M2T[:, :, :], NEG, None, ALU.mult)

                    def maxima(k, j):
                        for q in range(2):
                            c = 2 * (GROUP * k + j) + q
                            dve.wait_ge(s["scored"], c + 1)
                            if k >= 4:
                                dve.wait_ge(s["shift"], k - 3)
                            x = PS[2][:, (c % 2) * 512:(c % 2) * 512 + nk]
                            m = NM[:, k % 4, q, j:j + 1]
                            if a == 2 or (stairs and q == 0):
                                if c >= 2:
                                    dve.wait_ge(s["maxed"], c - 1)
                                dve.tensor_tensor_reduce(SEEN[:, c % 2, :], x, NEG2[:, q, :] if a == 2 else NEGC[:, :],
                                                         1.0, NEG * 4, ALU.add, ALU.max, m).then_inc(s["maxed"], 1)
                            else:
                                dve.tensor_reduce(m, x, AX.X, ALU.max).then_inc(s["maxed"], 1)

                    def normalize(k):
                        b, m, p0 = spot(k)
                        dve.wait_ge(s["x_made"], turn["rows", k] + 1)
                        x = XB[:, 0:256].rearrange("p (t j e) -> p t j e", t=2, j=GROUP)
                        dve.reciprocal(RC[:, k % 2, :, :], x[:, :, :, DH]).then_inc(s["rc"], 1)
                        dve.wait_ge(s["rc"], k + 1)
                        if k % NG == 0 and b >= 2:
                            dve.wait_ge(s["x_made"], turn["cols", b - 2] + 1)
                        o = ON[:, b % 2, :, :].rearrange("p t (r m e) -> p t r m e", m=2, e=DH)
                        dve.tensor_tensor(o[:, :, p0:p0 + GROUP, m, :], x[:, :, :, 0:DH],
                                          RC[:, k % 2, :, :].unsqueeze(3).to_broadcast([P, 2, GROUP, DH]),
                                          ALU.mult).then_inc(s["x_read"], 1)

                    def add_out(b):
                        dve.wait_ge(s["x_made"], turn["out", b] + 1)
                        if a > 0:
                            dve.wait_ge(s["biased"], 1)
                        o = rows_out[:, 2 * b:2 * b + 2, :]
                        dve.tensor_tensor(o, XB[:, 0:256].rearrange("p (t e) -> p t e", t=2), o, ALU.add)\
                           .then_inc(s["x_read"], 1)

                    for n in range(-look, last + 2):
                        k = n + look
                        for j in range(GROUP):
                            if k < last:
                                maxima(k, j)
                            if j == 0 and n - 2 >= 0:
                                normalize(n - 2)
                            if j == 3 and n - 2 >= 0 and (n - 2) % NG == NG - 1:
                                add_out((n - 2) // NG)

                @block.scalar
                def _(act):
                    if not own:
                        for h in range(2):
                            act.wait_ge(s["turned"], h + 1)
                            act.activation(XNT[:, h * TH:(h + 1) * TH], PS[0][:, h * TH:(h + 1) * TH], ACT.Copy)\
                               .then_inc(s["kept"], 1)
                    if chunks:
                        prep_scalar(act, s, a, 0)
                        prep_middle(act, s, 0)
                    for h in range(2):
                        act.wait_ge(s["q_made"], h + 1)
                        act.activation(QHI[:, h, :], PS[1][:, h * TH:(h + 1) * TH], ACT.Identity,
                                       bias=col(f"bq{a}")).then_inc(s["q_hi"], 1)
                    for c in range(1, chunks):
                        prep_scalar(act, s, a, c)
                        prep_middle(act, s, c)

                    def exponentials(n, j):
                        u = GROUP * n + j
                        act.wait_ge(s["scored_t"], u + 1)
                        if n >= 2:
                            act.wait_ge(s["summed"], n - 1)
                        act.activation(filled(PT[:, u % 8, :]), filled(PS[u % 2][:, :]), ACT.Exp, scale=SCALE)\
                           .then_inc(s["exps"], 1)

                    def keep_shift(k):
                        act.wait_ge(s["x_made"], turn["shift", k] + 1)
                        if k >= 2:
                            act.wait_ge(s[f"shift_placed{k % 2}"], 32 * (k // 2))
                        act.activation(SH[:, k % 2, :], XBH[0:2 * GROUP, 0:256], ACT.Copy)\
                           .then_inc(s["x_read"], 1)

                    def keep_sums(k):
                        act.wait_ge(s["summed"], k + 1)
                        if k >= 2:
                            act.wait_ge(s["x_made"], turn["rows", k - 2] + 1)
                        act.activation(OT[:, k % 2, :], SUM, ACT.Copy).then_inc(s["o_kept"], 1)

                    def keep_cols(b):
                        act.wait_ge(s["x_made"], turn["cols", b] + 1)
                        act.activation(CT[:, b % 2, :], XB[:, 0:256], ACT.Identity, bias=col(f"bv{a}"))\
                           .then_inc(s["x_read"], 1)

                    for n in range(-look, last + 2):
                        for j in range(GROUP):
                            if 0 <= n < last:
                                exponentials(n, j)
                            if j == 1 and 0 <= n + look - 1 < last:
                                keep_shift(n + look - 1)
                            if j == nkt - 1 and 0 <= n - 1 < last:
                                keep_sums(n - 1)
                            if j == 2 and n - 2 >= 0 and (n - 2) % NG == NG - 1:
                                keep_cols((n - 2) // NG)

                @block.tensor
                def _(pe):
                    if a == 0:
                        pe.wait_ge(ctx_in, 16)
                    if chunks:
                        prep_tensor(pe, s, a, XNT if own else CTX, 0)
                    if not own:
                        for t in range(NT):
                            pe.wait_ge(s["norm_rows"], t + 1)
                            ins = pe.transpose(PS[0][:, t * P:(t + 1) * P], XN[:, t, :], IDF[:, :])
                            if t % 4 == 3:
                                ins.then_inc(s["turned"], 1)
                    for h in range(2):
                        if not own:
                            pe.wait_ge(s["kept"], h + 1)
                        pe.matmul(PS[1][:, h * TH:(h + 1) * TH], WA[:, a, 0, :], XNT[:, h * TH:(h + 1) * TH],
                                  start=True, stop=True).then_inc(s["q_made"], 1)
                    for c in range(1, chunks):
                        prep_tensor(pe, s, a, XNT if own else CTX, c)
                    if chunks:
                        pe.wait_ge(s["k_kept"], chunks)
                        pe.wait_ge(s["v_kept"], chunks)

                    def scores(k, j):
                        b = k // NG
                        if k % (2 * NG) == 0 and j == 0:
                            pe.wait_ge(s[f"q_placed{b // 2}"], 96)
                        if chunks and (k * nk // NG) % 512 == 0 and j == 0:
                            pe.wait_ge(s[f"k_placed{b * nk // 512}"], 96)
                        for q in range(2):
                            c = 2 * (GROUP * k + j) + q
                            if c >= 2:
                                pe.wait_ge(s["maxed"], c - 1)
                            o = PS[2][:, (c % 2) * 512:(c % 2) * 512 + nk]
                            pe.matmul(o, queries(k, j, q * P, P, MASK_ROW + 1), keys(k, j, 0, nk, MASK_ROW + 1),
                                      start=True, stop=True).then_inc(s["scored"], 1)

                    def scores_t(n, j):
                        u = GROUP * n + j
                        if j == 0:
                            pe.wait_ge(s[f"shift_placed{n % 2}"], 32 * (n // 2 + 1))
                        if u >= 2:
                            pe.wait_ge(s["exps"], u - 1)
                        for i, (x, q0) in enumerate(places):
                            o = PS[u % 2][:, x:x + SQ - q0]
                            ins = pe.matmul(o, keys(n, j, i * P, P, SHIFT_ROW + 2),
                                            queries(n, j, q0, SQ - q0, SHIFT_ROW + 2), start=True, stop=a != 2)
                            if a == 2:
                                ins = pe.matmul(o, IDB[:, :], NEG2T[:, i, :], start=False, stop=True)
                            if stairs:
                                ins = pe.matmul(PS[u % 2][:, x:x + 32], IDB[:, :], STAIR[:, :], start=False,
                                                stop=True, skip_group_check=True)
                        ins.then_inc(s["scored_t"], 1)

                    def sums(n, i):
                        b, m, p0 = spot(n)
                        if i == 0:
                            pe.wait_ge(s["exps"], GROUP * (n + 1))
                            if n >= 1:
                                pe.wait_ge(s["o_kept"], n)
                        x, q0 = places[i]
                        for j in range(GROUP):
                                h = 2 * (p0 + j) + m
                                ins = pe.matmul(SUM[32 * j:32 * j + 32, q0:SQ], V[:, b * nkt + i, 9 * h:9 * h + 32],
                                                PT[:, (GROUP * n + j) % 8, x:x + SQ - q0], start=(i == 0),
                                                stop=(i == nkt - 1), tile_position=(0, 32 * j),
                                                skip_group_check=True)
                        if i == nkt - 1:
                            ins.then_inc(s["summed"], 1)

                    def my_turn(what, k):
                        if turn[what, k]:
                            pe.wait_ge(s["x_read"], turn[what, k])

                    for n in range(-look, last + 2):
                        k = n + look
                        for j in range(GROUP):
                            if 0 <= n < last:
                                scores_t(n, j)
                            if k < last:
                                scores(k, j)
                            if 0 <= n - 1 < last and j < nkt:
                                sums(n - 1, j)
                            if j == 0 and n - 2 >= 0:
                                g = n - 2
                                my_turn("rows", g)
                                pe.wait_ge(s["o_kept"], g + 1)
                                for t in range(2):
                                    ins = pe.transpose(XB[:, t * P:(t + 1) * P], OT[:, g % 2, t * P:(t + 1) * P], IDF[:, :])
                                ins.then_inc(s["x_made"], 1)
                            if j == 1 and 0 <= k - 1 < last:
                                g = k - 1
                                my_turn("shift", g)
                                pe.wait_ge(s["shift"], g + 1)
                                for t in range(2):
                                    ins = pe.transpose(XBH[0:2 * GROUP, t * P:(t + 1) * P],
                                                       HL[:, g % 4, t, :, :].rearrange("p r j -> p (r j)"), IDB[:, :])
                                ins.then_inc(s["x_made"], 1)
                            if j == 2 and n - 2 >= 0 and (n - 2) % NG == NG - 1:
                                b = (n - 2) // NG
                                my_turn("cols", b)
                                for t in range(2):
                                    ins = pe.transpose(XB[:, t * P:(t + 1) * P], ON[:, b % 2, t, :], IDF[:, :])
                                ins.then_inc(s["x_made"], 1)
                            if j == 3 and n - 2 >= 0 and (n - 2) % NG == NG - 1:
                                b = (n - 2) // NG
                                my_turn("out", b)
                                for t in range(2):
                                    ins = pe.matmul(XB[:, t * P:(t + 1) * P], CT[:, b % 2, t * P:(t + 1) * P],
                                                    WA[:, a, 3, :], start=True, stop=True)
                                ins.then_inc(s["x_made"], 1)
    

        def experts(l):
            gated_out = l in (0, 3)
            final = l == 3
            hid = HID[l]
            sizes = [min(P, hid - P * c) for c in range(-(-hid // P))]
            nch = len(sizes)
            units = NE * nch * (1 if gated_out else 2)
            s = signals(nc, f"ffn{l}", "var rstd norm_rows chain turned kept scaled_r routed ex sub gates g_turned "
                        "g_kept g_stored " + " ".join(f"g_loaded{e}" for e in range(NE)) + " affine w_loaded0 w_loaded1 u_made up acted h_made down "
                        "y_used added acc biased back no_mask lg_read chain2 " + (PREP_NAMES if not final else ""), before)
            prep = l + 1 if not final else None
            YG = H[:, 2 * T:3 * T] if gated_out else U[:, 0, :]
            HT = H[:, :].rearrange("p (u n) -> p u n", n=1024 if gated_out else 512)
            GBANK = PS[3] if gated_out else PS[2]
            with nc.Block() as block:
                @block.sync
                def _(sp):
                    def weights(e):
                        if e >= 2:
                            sp.wait_ge(s["down"], (e - 1) * units // NE)
                        sp.dma_start(W[:, e % 2, 0:EW[l]], d[f"we{l}"][e]).then_inc(s[f"w_loaded{e % 2}"], 16)
                    weights(0)
                    weights(1)
                    if not final:
                        for c in range(3):
                            prep_store(sp, s, c)
                            prep_place(sp, s, c)
                        prep_store(sp, s, 3)
                    sp.wait_ge(s["g_kept"], 2)
                    sp.dma_start(g_rows, GT[:, :]).then_inc(s["g_stored"], 16)
                    if not final:
                        prep_place(sp, s, 3)
                        if l == 0:
                            sp.wait_ge(s["no_mask"], 1)
                            sp.dma_start(KOP[MASK_ROW:MASK_ROW + 1, :, :, :].rearrange("r a b n -> r (a b) n"),
                                         ONES[0:1, :].unsqueeze(1).to_broadcast([1, 32, 512]))\
                              .then_inc(s["k_placed0"], 16)
                    sp.wait_ge(s["g_stored"], 16)
                    for e in range(NE):
                        sp.dma_start(GB[:, e, :], g_rows[e].partition_broadcast(P)).then_inc(s[f"g_loaded{e}"], 16)
                    for e in range(2, NE):
                        weights(e)
                    if not final:
                        for c in range(4):
                            sp.wait_ge(s[f"k_placed{c}"], 112 if l == 0 and c == 0 else 96)
                    else:
                        sp.wait_ge(s["acc"], 1)
                        sp.dma_start(out.rearrange("(t p) e -> p t e", p=P), XN[:, :, :]).then_inc(stored, 16)
                        sp.wait_ge(stored, 16)

                @block.gpsimd
                def _(pool):
                    norm_pool(pool, s, 1)
                    if l == 0:
                        prep_pool(pool, s, 0)
                        norm_pool(pool, s, 2)
                        pool.memset(ONES[0:1, :], 0.0).then_inc(s["no_mask"], 1)
                    if not final:
                        for c in range(1 if l == 0 else 0, 4):
                            prep_pool(pool, s, c)
                    if l == 1:
                        pool.wait_ge(s["norm_rows"], NT)
                        pool.tensor_tensor(X[:, :, :], X[:, :, :],
                                           row("ffn1_bias").unsqueeze(1).to_broadcast([P, NT, P]), ALU.add)\
                            .then_inc(s["biased"], 1)
                    for e in range(1, NE):
                        for h in range(2):
                            x = slice(h * TH, (h + 1) * TH)
                            pool.wait_ge(s["y_used"], 2 * e + h + 1)
                            pool.tensor_tensor(ACC[:, x], ACC[:, x], YG[:, x], ALU.add).then_inc(s["added"], 1)
                    if final:
                        norm_pool(pool, s, 2)

                @block.vector
                def _(dve):
                    chain = Chain(dve, s["chain"])
                    if prep == 2:
                        prep_vector(dve, s, 0)
                        prep_vector(dve, s, 1)
                    norm_vector(dve, s, XN if final else X, EPS, chain, 1)
                    if prep == 2:
                        prep_vector(dve, s, 2)
                        prep_vector(dve, s, 3)
                    if l == 0:
                        norm_vector(dve, s, XN, EPS_IN, chain, 2)
                    if final:
                        affine_rows(dve, s["affine"], 0, "ln1_g", "ln1_b")
                    if l == 0:
                        dve.wait_ge(s["kept"], 2)
                        dve.tensor_scalar(U[:, 0, :], XNT[:, :], col("rln_s"), col("rln_b"), ALU.mult, ALU.add)\
                           .then_inc(s["scaled_r"], 1)

                    def inputs(e):
                        if e == 1:
                            dve.wait_ge(s["routed"], 1)
                        if e >= 2:
                            dve.wait_ge(s["up"], nch * (e - 1))
                        dve.tensor_scalar(U[:, (e + 1) % 2, :], XNT[:, :], col("eln_s", e), col("eln_b", e),
                                          ALU.mult, ALU.add).then_inc(s["u_made"], 1)
                    if l == 0:
                        inputs(0)
                    dve.wait_ge(s["routed"], 1)
                    lg = PS[1][:, 0:NT * NE].rearrange("p (t e) -> p t e", e=NE)
                    if gated_out:
                        dve.tensor_tensor(LG[:, :, :], lg, row(f"router_b{l}").unsqueeze(1).to_broadcast([P, NT, NE]),
                                          ALU.add).then_inc(s["lg_read"], 1)
                    else:
                        dve.tensor_copy(LG[:, :, :], lg).then_inc(s["lg_read"], 1)
                    dve.wait_ge(s["lg_read"], 1)
                    for t in range(NT):
                        ins = dve.max(MX[:, t, :], LG[:, t, :])
                    chain(ins)

                    def wide(v):
                        return v.to_broadcast([P, NT, NE])
                    top1, top2 = MX[:, :, 0:1], MX[:, :, 1:2]
                    D1, OH1, OH2, EX, D2, EX2, T1, T2 = [g[:, :, :] for g in GA]
                    tt = dve.tensor_tensor
                    if l != 3:
                        for t in range(NT):
                            ins = dve.max_index(IX[:, t, :], MX[:, t, :], LG[:, t, :])
                        chain(ins)
                        chain(dve.tensor_copy(IXF[:, :, :], IX[:, :, :]))
                        tt(OH1, IOTA[:, :, :], wide(IXF[:, :, 0:1]), ALU.is_equal)
                        tt(OH2, IOTA[:, :, :], wide(IXF[:, :, 1:2]), ALU.is_equal)
                    tt(D1, LG[:, :, :], wide(top1), ALU.subtract).then_inc(s["sub"], 1)
                    if l == 2:
                        chain(tt(D2, LG[:, :, :], wide(top2), ALU.subtract))
                        dve.tensor_scalar(T2, D2, 0.0, None, ALU.min).then_inc(s["sub"], 1)
                        chain(dve.tensor_scalar(T1, LG[:, :, :], -1.0, None, ALU.mult))
                        chain(tt(T1, T1, LG[:, :, :], ALU.max))
                        chain(tt(LG[:, :, :], T1, wide(top1), ALU.max))
                        chain(dve.scalar_tensor_tensor(LG[:, :, :], LG[:, :, :], 0.02, D1, ALU.mult, ALU.add))
                        chain(dve.tensor_scalar(LG[:, :, :], LG[:, :, :], 0.0, None, ALU.is_ge))
                        chain(tt(T1, T1, wide(top2), ALU.max))
                        chain(dve.scalar_tensor_tensor(T1, T1, 0.02, D2, ALU.mult, ALU.add))
                        chain(dve.tensor_scalar(T1, T1, 0.0, None, ALU.is_ge))
                        chain(dve.scalar_tensor_tensor(T1, OH1, 1.0, T1, ALU.subtract, ALU.mult))
                        dve.wait_ge(s["ex"], 2)
                        chain(tt(EX, EX, LG[:, :, :], ALU.mult))
                        chain(tt(EX2, EX2, T1, ALU.mult))
                        chain(dve.tensor_reduce(G1[0][:, :], EX, AX.X, ALU.add))
                        chain(dve.tensor_reduce(G1[1][:, :], EX2, AX.X, ALU.add))
                        chain(dve.reciprocal(G1[0][:, :], G1[0][:, :]))
                        chain(dve.reciprocal(G1[1][:, :], G1[1][:, :]))
                        chain(tt(OH1, OH1, wide(G1[0][:, :].unsqueeze(2)), ALU.mult))
                        chain(tt(OH2, OH2, wide(G1[1][:, :].unsqueeze(2)), ALU.mult))
                        tt(T1, OH1, OH2, ALU.subtract).then_inc(s["gates"], 1)
                    else:
                        if l != 3:
                            dve.wait_ge(s["sub"], 1)
                            chain(tt(OH1, OH1, OH2, ALU.add))
                        dve.wait_ge(s["ex"], 1)
                        den = EX
                        if l != 3:
                            chain(tt(EX2, EX, OH1, ALU.mult))
                            top = EX2
                        else:
                            top = EX
                        if l == 0:
                            den = EX2
                        chain(dve.tensor_reduce(G1[0][:, :], den, AX.X, ALU.add))
                        chain(dve.reciprocal(G1[0][:, :], G1[0][:, :]))
                        tt(T1, top, wide(G1[0][:, :].unsqueeze(2)), ALU.mult).then_inc(s["gates"], 1)

                    def gate(e):
                        for h in range(2):
                            x = slice(h * TH, (h + 1) * TH)
                            dve.wait_ge(s["down"], dpe * (e + 1) if gated_out else dpe * (e + 1) - 1 + h)
                            if h == 0:
                                dve.wait_ge(s[f"g_loaded{e}"], 16)
                            if e >= 2:
                                dve.wait_ge(s["added"], 2 * (e - 2) + h + 1)
                            if e == 0:
                                dve.wait_ge(s["g_stored"], 16)
                            y = (PS[2 + e % 2] if gated_out else PS[3])[:, x]
                            o = (YG if e else ACC)[:, x]
                            if gated_out:
                                dve.scalar_tensor_tensor(o, y, col(f"b2_{l}", e), GB[:, e, x], ALU.add, ALU.mult)\
                                   .then_inc(s["y_used"], 1)
                            else:
                                dve.tensor_tensor(o, y, GB[:, e, x], ALU.mult).then_inc(s["y_used"], 1)

                    dpe = units // NE
                    if gated_out:
                        if l == 0:
                            inputs(1)
                        for e in range(NE):
                            gate(e)
                            if l == 0 and e + 2 < NE:
                                inputs(e + 2)
                    else:
                        for k in range(units):
                            z = sizes[k % dpe // 2]
                            dve.wait_ge(s["acted"], k + 1)
                            if k >= 3:
                                dve.wait_ge(s["down"], k - 2)
                            dve.tensor_tensor(HT[0:z, k % 3, :], PS[k % 3][0:z, 512:1024], HT[0:z, 4 + k % 2, :],
                                              ALU.mult).then_inc(s["h_made"], 1)
                            if k % dpe == 1 and k > dpe:
                                gate(k // dpe - 1)
                        gate(NE - 1)
                    dst = XN if final else X
                    if l == 1:
                        dve.wait_ge(s["biased"], 1)
                    chain2 = Chain(dve, s["chain2"])
                    for h in range(2):
                        dve.wait_ge(s["back"], h + 1)
                        o = dst[:, 4 * h:4 * h + 4, :]
                        chain2(dve.tensor_tensor(o, PS[0][:, h * TH:(h + 1) * TH].rearrange("p (t e) -> p t e", t=4),
                                                 o, ALU.add))
                    if final:
                        norm_vector(dve, s, XN, EPS, chain2, 2)
                        affine_rows(dve, s["affine"], 2, "ln2_g", "ln2_b")
                        dve.tensor_tensor(XN[:, :, :], XN[:, :, :], X[:, :, :], ALU.add).then_inc(s["acc"], 1)

                @block.scalar
                def _(act):
                    if not final:
                        prep_scalar(act, s, prep, 0)
                        prep_scalar(act, s, prep, 1)
                        prep_middle(act, s, 0)
                        prep_middle(act, s, 1)
                    for h in range(2):
                        act.wait_ge(s["turned"], h + 1)
                        act.activation(XNT[:, h * TH:(h + 1) * TH], PS[0][:, h * TH:(h + 1) * TH], ACT.Copy)\
                           .then_inc(s["kept"], 1)
                    if not final:
                        prep_scalar(act, s, prep, 2)
                        prep_middle(act, s, 2)
                        prep_scalar(act, s, prep, 3)
                    act.wait_ge(s["sub"], 1)
                    act.activation(GA[3][:, :, :], GA[0][:, :, :], ACT.Exp).then_inc(s["ex"], 1)
                    if l == 2:
                        act.wait_ge(s["sub"], 2)
                        act.activation(GA[5][:, :, :], GA[7][:, :, :], ACT.Exp).then_inc(s["ex"], 1)
                    if not final:
                        prep_middle(act, s, 3)

                    def keep_gates():
                        for h in range(2):
                            act.wait_ge(s["g_turned"], h + 1)
                            act.activation(GT[:, h * TH:(h + 1) * TH], GBANK[0:NE, h * TH:(h + 1) * TH], ACT.Copy)\
                               .then_inc(s["g_kept"], 1)
                    if gated_out:
                        for k in range(units):
                            if k == 2:
                                keep_gates()
                            act.wait_ge(s["up"], k + 1)
                            if k >= 2:
                                act.wait_ge(s["down"], k - 1)
                            act.activation(HT[:, k % 2, :], PS[k % 2][:, :], ACT.Gelu if l == 0 else ACT.Relu,
                                           bias=col(f"b1_{l}", k)).then_inc(s["acted"], 1)
                    else:
                        for k in range(units):
                            z = sizes[k % (2 * nch) // 2]
                            if k == 5:
                                keep_gates()
                            act.wait_ge(s["up"], k + 1)
                            if k >= 2:
                                act.wait_ge(s["h_made"], k - 1)
                            act.activation(HT[0:z, 4 + k % 2, :], PS[k % 3][0:z, 0:512],
                                           ACT.Gelu if l == 1 else ACT.Silu).then_inc(s["acted"], 1)

                @block.tensor
                def _(pe):
                    if not final:
                        for c in range(3):
                            prep_tensor(pe, s, prep, CTX, c)
                    pe.wait_ge(s["norm_rows"], 2 * NT if l == 0 else NT)
                    if final:
                        pe.wait_ge(s["affine"], 2)
                    turn_rows(pe, s, XN, PS[0], "turned")
                    if not final:
                        prep_tensor(pe, s, prep, CTX, 3)
                    src = XNT
                    pe.wait_ge(s["kept"], 2)
                    if l == 0:
                        pe.wait_ge(s["scaled_r"], 1)
                        src = U[:, 0, :]
                    for t in range(NT):
                        ins = pe.matmul(PS[1][:, t * NE:(t + 1) * NE], src[:, t * P:(t + 1) * P], WR[:, l, :],
                                        start=True, stop=True)
                    ins.then_inc(s["routed"], 1)

                    def turn_gates():
                        pe.wait_ge(s["gates"], 1)
                        for t in range(NT):
                            ins = pe.transpose(GBANK[0:NE, t * P:(t + 1) * P], GA[6][:, t, :], IDF[:, :])
                            if t % 4 == 3:
                                ins.then_inc(s["g_turned"], 1)

                    if gated_out:
                        def up(k):
                            e, c = k // nch, k % nch
                            if c == 0:
                                pe.wait_ge(s[f"w_loaded{e % 2}"], 16 * (e // 2 + 1))
                                if l == 0:
                                    pe.wait_ge(s["u_made"], e + 1)
                            if k == 1:
                                pe.wait_ge(s["lg_read"], 1)
                            if k >= 2:
                                pe.wait_ge(s["acted"], k - 1)
                            x = U[:, (e + 1) % 2, :] if l == 0 else XNT[:, :]
                            for h in range(2):
                                ins = pe.matmul(PS[k % 2][:, h * TH:(h + 1) * TH], W[:, e % 2, c * P:(c + 1) * P],
                                                x[:, h * TH:(h + 1) * TH], start=True, stop=True)
                            ins.then_inc(s["up"], 1)

                        def down(k):
                            e, c = k // nch, k % nch
                            pe.wait_ge(s["acted"], k + 1)
                            if k == 0 and not final:
                                pe.wait_ge(s["k_kept"], 4)
                                pe.wait_ge(s["v_kept"], 4)
                            if c == 0 and e == 1:
                                pe.wait_ge(s["g_kept"], 2)
                            if c == 0 and e >= 2:
                                pe.wait_ge(s["y_used"], 2 * (e - 1))
                            for h in range(2):
                                ins = pe.matmul(PS[2 + e % 2][:, h * TH:(h + 1) * TH],
                                                W[:, e % 2, (nch + c) * P:(nch + c + 1) * P],
                                                HT[:, k % 2, h * TH:(h + 1) * TH], start=(c == 0), stop=(c == nch - 1))
                            ins.then_inc(s["down"], 1)
                        up(0)
                        for k in range(units):
                            if k + 1 < units:
                                up(k + 1)
                            down(k)
                            if k == 0:
                                turn_gates()
                    else:
                        def up(k):
                            e, c, h = k // (2 * nch), k % (2 * nch) // 2, k % 2
                            z = sizes[c]
                            if k % (2 * nch) == 0:
                                pe.wait_ge(s[f"w_loaded{e % 2}"], 16 * (e // 2 + 1))
                            if k == 1:
                                pe.wait_ge(s["lg_read"], 1)
                            if k == 2:
                                pe.wait_ge(s["k_kept"], 4)
                                pe.wait_ge(s["v_kept"], 4)
                            if k == 5:
                                pe.wait_ge(s["g_kept"], 2)
                            if k >= 3:
                                pe.wait_ge(s["h_made"], k - 2)
                            pe.matmul(PS[k % 3][0:z, 0:512], W[:, e % 2, c * P:c * P + z],
                                      XNT[:, h * TH:(h + 1) * TH], start=True, stop=True)
                            pe.matmul(PS[k % 3][0:z, 512:1024], W[:, e % 2, hid + c * P:hid + c * P + z],
                                      XNT[:, h * TH:(h + 1) * TH], start=True, stop=True).then_inc(s["up"], 1)

                        def down(k):
                            e, c, h = k // (2 * nch), k % (2 * nch) // 2, k % 2
                            z = sizes[c]
                            pe.wait_ge(s["h_made"], k + 1)
                            if c == 0 and e >= 1:
                                pe.wait_ge(s["y_used"], 2 * (e - 1) + h + 1)
                            pe.matmul(PS[3][:, h * TH:(h + 1) * TH], W[0:z, e % 2, 2 * hid + c * P:2 * hid + (c + 1) * P],
                                      HT[0:z, k % 3, :], start=(c == 0),
                                      stop=(c == nch - 1)).then_inc(s["down"], 1)
                        up(0)
                        up(1)
                        for k in range(units):
                            if k == 3:
                                pe.wait_ge(s["h_made"], 3)
                                turn_gates()
                            if k + 2 < units:
                                up(k + 2)
                            down(k)
                    for t in range(NT):
                        if t % 4 == 0:
                            pe.wait_ge(s["added"], 2 * (NE - 2) + t // 4 + 1)
                        ins = pe.transpose(PS[0][:, t * P:(t + 1) * P], ACC[:, t * P:(t + 1) * P], IDF[:, :])
                        if t % 4 == 3:
                            ins.then_inc(s["back"], 1)
    

        def convolution():
            s = signals(nc, "conv", "var rstd norm_rows chain turned padded border made kept back rows", before)
            with nc.Block() as block:
                @block.gpsimd
                def _(pool):
                    for i in (0, SQ + 1):
                        pool.memset(XPAD[:, :, i:i + 1], 0.0).then_inc(s["border"], 1)
                    norm_pool(pool, s, 1)

                @block.vector
                def _(dve):
                    norm_vector(dve, s, X, EPS, Chain(dve, s["chain"]), 1)
                    for h in range(2):
                        dve.wait_ge(s["back"], h + 1)
                        dve.tensor_copy(XN[:, 4 * h:4 * h + 4, :],
                                        PS[0][:, h * TH:(h + 1) * TH].rearrange("p (t e) -> p t e", t=4))\
                           .then_inc(s["rows"], 1)

                @block.scalar
                def _(act):
                    for h in range(2):
                        act.wait_ge(s["turned"], h + 1)
                        act.activation(XPAD[:, 2 * h:2 * h + 2, 1:SQ + 1],
                                       PS[0][:, h * TH:(h + 1) * TH].rearrange("p (b n) -> p b n", b=2), ACT.Copy)\
                           .then_inc(s["padded"], 1)
                    for h in range(2):
                        act.wait_ge(s["made"], h + 1)
                        act.activation(XNT[:, h * TH:(h + 1) * TH], PS[1][:, h * TH:(h + 1) * TH], ACT.Identity,
                                       bias=col("conv_b")).then_inc(s["kept"], 1)

                @block.tensor
                def _(pe):
                    pe.wait_ge(s["norm_rows"], NT)
                    turn_rows(pe, s, XN, PS[0], "turned")
                    pe.wait_ge(s["border"], 2)
                    for h in range(2):
                        pe.wait_ge(s["padded"], h + 1)
                        for i in range(3):
                            ins = pe.matmul(PS[1][:, h * TH:(h + 1) * TH], WCONV[:, i, :],
                                            XPAD[:, 2 * h:2 * h + 2, i:i + SQ], start=(i == 0), stop=(i == 2))
                        ins.then_inc(s["made"], 1)
                    for h in range(2):
                        pe.wait_ge(s["kept"], h + 1)
                        for t in range(4 * h, 4 * h + 4):
                            ins = pe.transpose(PS[0][:, t * P:(t + 1) * P], XNT[:, t * P:(t + 1) * P], IDF[:, :])
                        ins.then_inc(s["back"], 1)
    
        for l in range(4):
            attention(l)
            if l == 3:
                convolution()
                attention(4)
            experts(l)



def kernel(**inputs):
    import concourse.bacc as _bacc
    from concourse.bass_utils import run_bass_kernel_spmd as _run

    x = {k: np.asarray(v) for k, v in inputs.items()}
    f32 = np.float32
    zeros = np.zeros(P, f32)
    order = np.array([(2 * p + m) * DH + e for m in range(2) for e in range(DH) for p in range(NP)])
    wqkv, bqkv = x["L3_ffn_wqkv"], x["L3_ffn_bqkv"]
    w = [[x["L0_xattn_Wq"].T, x["L0_xattn_Wk"].T, x["L0_xattn_Wv"].T, x["L0_xattn_Wo"].T],
         [x["L1_xattn_Wq"].T, x["L1_xattn_Wk"].T, x["L1_xattn_Wv"].T, x["L1_xattn_Wo"].T],
         [x["L2_xattn_Wq"], x["L2_xattn_Wk"], x["L2_xattn_Wv"], x["L2_xattn_Wo"]],
         [x["L3_xattn_wq_w"].T, x["L3_xattn_wk_w"].T, x["L3_xattn_wv_w"].T, x["L3_xattn_proj_w"].T],
         [wqkv[0:P].T, wqkv[P:2 * P].T, wqkv[2 * P:].T, x["L3_ffn_wo"].T]]
    bq = [zeros, x["L1_xattn_bq"], zeros, x["L3_xattn_wq_b"], bqkv[0:P]]
    bk = [zeros, x["L1_xattn_bk"], zeros, x["L3_xattn_wk_b"], bqkv[P:2 * P]]
    bv = [zeros, x["L1_xattn_bv"], zeros, x["L3_xattn_wv_b"], bqkv[2 * P:]]
    bo = [zeros, x["L1_xattn_bo"], x["L2_xattn_bo"], x["L3_xattn_proj_b"], x["L3_ffn_bo"]]
    wattn = np.stack([np.stack([q[:, order], k[:, order], v, o], 1) for q, k, v, o in w], 1)
    cols = [b[order] for b in bq] + [b[order] for b in bk] + bv
    cols += [x["L3_ffn_conv_b"], x["L0_ffn_router_ln_scale"], x["L0_ffn_router_ln_bias"]]
    cols += list(x["L0_ffn_expert_ln_scale"]) + list(x["L0_ffn_expert_ln_bias"])
    cols += list(x["L0_ffn_b1"].reshape(-1, P)) + list(x["L3_ffn_b1"].reshape(-1, P))
    cols += list(x["L0_ffn_b2"]) + list(x["L3_ffn_b2"])
    rows = bo + [x["L1_ffn_bias"], x["L0_ffn_router_b"], x["L3_ffn_gate_b"], x["L3_ffn_ln1_g"], x["L3_ffn_ln1_b"],
                 x["L3_ffn_ln2_g"], x["L3_ffn_ln2_b"]]

    def tiles(a):
        n = -(-a.shape[1] // P)
        full = np.zeros((a.shape[0], n * P, a.shape[2]), a.dtype)
        full[:, 0:a.shape[1]] = a
        return full.reshape(a.shape[0], n, P, -1).transpose(0, 2, 1, 3).reshape(a.shape[0], P, -1)

    t = (0, 2, 1)
    we = [np.concatenate([x["L0_ffn_w1"].transpose(t), tiles(x["L0_ffn_w2"].transpose(t))], 2),
          np.concatenate([x["L1_ffn_w1"], x["L1_ffn_v1"], tiles(x["L1_ffn_w2"])], 2),
          np.concatenate([x["L2_ffn_w_gate"].transpose(t), x["L2_ffn_w_up"].transpose(t),
                          tiles(x["L2_ffn_w_down"].transpose(t))], 2),
          np.concatenate([x["L3_ffn_w1"], tiles(x["L3_ffn_w2"])], 2)]
    data = {
        "x": x["x"].reshape(T, P),
        "ctxT": x["ctx_1024"].reshape(TK, P).T,
        "mask0": x["mask_Bx1x1xS2_bf1"].reshape(1, TK),
        "mask_keys": x["mask_BxS2_bk0"].reshape(TK),
        "mask2": x["mask_SxS2_bk1"],
        "mask2T": x["mask_SxS2_bk1"].T,
        "wattn": wattn,
        "cols": np.stack(cols, 1),
        "rows": np.concatenate(rows),
        "wconv": x["L3_ffn_conv_w"].transpose(1, 2, 0),
        "wrouter": np.stack([x["L0_ffn_router_w"].T, x["L1_ffn_router_w"], x["L2_ffn_router_w"].T,
                             x["L3_ffn_gate_w"]], 1),
        "we0": we[0], "we1": we[1], "we2": we[2], "we3": we[3],
    }
    nc = _bacc.Bacc("TRN2", target_bir_lowering=False, num_devices=1)
    arrays, args = {}, {}
    for name, a in data.items():
        a = np.ascontiguousarray(a)
        arrays[f"in_{name}"] = a
        args[name] = nc.dram_tensor(f"in_{name}", a.shape, mybir.dt.from_np(a.dtype), kind="ExternalInput").ap()
    out = nc.dram_tensor("out", (T, P), F32, kind="ExternalOutput").ap()
    build(nc, args, out)
    r = _run(nc, [arrays], core_ids=[0])
    return r.results[0]["out"].reshape(B, SQ, P)
```

```python
from contextlib import ExitStack

import numpy as np

import concourse.bass as bass
from concourse import mybir

F32 = mybir.dt.float32
F32R = mybir.dt.float32r
BF16 = mybir.dt.bfloat16
U8 = mybir.dt.uint8
U32 = mybir.dt.uint32
ALU = mybir.AluOpType
ACT = mybir.ActivationFunctionType
AX = mybir.AxisListType

P = 128
B, SQ, SK = 4, 256, 512
T = B * SQ
NT = T // P
TH = T // 2
TK = B * SK
HEADS, DH = 16, 8
NP = HEADS // 2
GROUP = 4
NG = HEADS // GROUP
NE = 8
SCALE = float(DH) ** -0.5
NEG = -1.0e30
EPS, EPS_IN = 1e-5, 1e-6
VW = 9 * HEADS + 24
CW = 6 * DH
MASK_ROW, SHIFT_ROW = 2 * CW, 2 * CW + 1

COLS = {}
_n = 0
for _name, _w in [(f"bq{a}", 1) for a in range(5)] + [(f"bk{a}", 1) for a in range(5)] + \
        [(f"bv{a}", 1) for a in range(5)] + \
        [("conv_b", 1), ("rln_s", 1), ("rln_b", 1), ("eln_s", NE), ("eln_b", NE),
         ("b1_0", 4 * NE), ("b1_3", 4 * NE), ("b2_0", NE), ("b2_3", NE)]:
    COLS[_name] = (_n, _w)
    _n += _w
NCOLS = _n
ROWS = {}
_n = 0
for _name, _w in [(f"bo{a}", P) for a in range(5)] + \
        [("ffn1_bias", P), ("router_b0", NE), ("router_b3", NE),
         ("ln1_g", P), ("ln1_b", P), ("ln2_g", P), ("ln2_b", P)]:
    ROWS[_name] = (_n, _w)
    _n += _w
NROWS = _n
HID = [512, 352, 256, 512]
EW = [4 * P + 4 * P, 2 * 352 + 3 * P, 2 * 256 + 2 * P, 4 * P + 4 * P]


def signals(nc, phase, names, before):
    s = {n: nc.alloc_semaphore(f"{phase}_{n}") for n in names.split()}
    if before:
        nc.clear_and_free_semaphores(before.pop())
    before.append(list(s.values()))
    return s


class Chain:

    def __init__(self, eng, sem):
        self.eng, self.sem, self.n = eng, sem, 0

    def __call__(self, ins):
        self.n += 1
        ins.then_inc(self.sem, 1)
        self.eng.wait_ge(self.sem, self.n)


def build(nc, d, out):
    ctx = ExitStack()
    with ctx:
        def sb(name, shape, dt=F32):
            return ctx.enter_context(nc.sbuf_tensor(name, shape, dt))

        X = sb("X", [P, NT, P])
        XN = sb("XN", [P, NT, P])
        XNT = sb("XNT", [P, T])
        CTX = sb("CTX", [P, TK])
        KOP = sb("KOP", [P, 4, NP, 512], BF16)
        V = sb("V", [P, TK // P, VW])
        HI = sb("HI", [P, 2, 512], BF16)
        MID = sb("MID", [P, 2, 512], BF16)
        LO = sb("LO", [P, 2, 512], BF16)
        REST = sb("REST", [P, 2, 512])
        KEEP = sb("KEEP", [P, TK], U8)
        WA = sb("WA", [P, 5, 4, P])
        WCONV = sb("WCONV", [P, 3, P])
        WR = sb("WR", [P, 4, NE])
        C = sb("C", [P, NCOLS])
        R = sb("R", [P, NROWS])
        W = sb("W", [P, 2, max(EW)])
        ACC = sb("ACC", [P, T])
        OT = sb("OT", [P, 2, 256])
        ON = sb("ON", [P, 2, 2, P])
        CT = sb("CT", [P, 2, 256])
        RC = sb("RC", [P, 2, 2, GROUP])
        NM = sb("NM", [P, 4, 2, GROUP])
        NG32 = sb("NG32", [P, 4, 2, GROUP])
        HL = sb("HL", [P, 4, 2, 2, GROUP], BF16)
        ONES = sb("ONES", [P, 512], BF16)
        SEEN = ACC[:, :].rearrange("p (i k) -> p i k", i=2)
        SH = sb("SH", [2 * GROUP, 2, 256], BF16)
        IDF = sb("IDF", [P, P])
        IDB = sb("IDB", [P, P], BF16)
        NEGC = sb("NEGC", [P, SK], BF16)
        STAIR = sb("STAIR", [P, 32], BF16)
        NEG2 = sb("NEG2", [P, 2, SK], BF16)
        NEG2T = sb("NEG2T", [P, 4, SQ], BF16)
        ST8 = sb("ST8", [P, NT, 6])
        MV = sb("MV", [P, NT, 2])
        VE = sb("VE", [P, NT])
        HALF = sb("HALF", [P, NT])
        RSTD = sb("RSTD", [P, NT])
        LG = sb("LG", [P, NT, NE])
        MX = sb("MX", [P, NT, NE])
        IX = sb("IX", [P, NT, NE], U32)
        IXF = sb("IXF", [P, NT, NE])
        IOTA = sb("IOTA", [P, NT, NE])
        GA = [sb(f"GA{i}", [P, NT, NE]) for i in range(8)]
        G1 = [sb(f"G1{i}", [P, NT]) for i in range(2)]
        GT = ACC[0:NE, :]

        PS = [ctx.enter_context(nc.psum_tensor(f"PS{i}", [P, 1024], F32)) for i in range(4)]

        q_parts = nc.dram_tensor("q_parts", [2, 3, P, TH], BF16).ap()
        k_parts = nc.dram_tensor("k_parts", [4, 3, P, 512], BF16).ap()
        g_rows = nc.dram_tensor("g_rows", [NE, T], F32).ap()


        def f32r(t):
            return t.bitcast(F32R)

        def product(pe, o, w_hi, w_lo, x_hi, x_lo, start, stop):
            pe.matmul(o, f32r(w_hi), f32r(x_hi), start=start, stop=False)
            pe.matmul(o, f32r(w_hi), f32r(x_lo), start=False, stop=False)
            return pe.matmul(o, f32r(w_lo), f32r(x_hi), start=False, stop=stop)

        def col(name, i=0, n=1, rows=P):
            a = COLS[name][0] + i
            return C[0:rows, a:a + n]

        def row(name):
            a, w = ROWS[name]
            return R[:, a:a + w]

        before = []

        def phase_memory(phase):
            mem = ExitStack()

            def own(name, shape, dt=F32):
                return mem.enter_context(nc.sbuf_tensor(f"{name}_{phase}", shape, dt))
            return own, mem



        def norm_stats(dve, s, src, eps, tiles, chain):
            for t in tiles:
                ins = dve.bn_stats(ST8[:, t, :], src[:, t, :])
            chain(ins)
            for t in tiles:
                ins = dve.bn_aggr(MV[:, t, :], ST8[:, t, :])
            chain(ins)
            x = slice(tiles[0], tiles[-1] + 1)
            dve.tensor_scalar(VE[:, x], MV[:, x, 1], eps, None, ALU.add).then_inc(s["var"], 1)

        def norm_root(pool, s, tiles, part):
            x = slice(tiles[0], tiles[-1] + 1)
            pool.wait_ge(s["var"], part + 1)
            pool.tensor_tensor(RSTD[:, x], VE[:, x], HALF[:, x], ALU.pow).then_inc(s["rstd"], 1)

        def norm_scale(dve, s, src, tiles, part):
            dve.wait_ge(s["rstd"], part + 1)
            for t in tiles:
                dve.tensor_scalar(XN[:, t, :], src[:, t, :], MV[:, t, 0:1], RSTD[:, t:t + 1],
                                  ALU.subtract, ALU.mult).then_inc(s["norm_rows"], 1)

        def kv_banks(c):
            return PS[2][:, (c % 2) * 512:(c % 2) * 512 + 512], PS[3][:, (c % 2) * 512:(c % 2) * 512 + 512]

        HALVES = (range(0, 4), range(4, 8))

        def norm_vector(dve, s, src, eps, chain):
            for tiles in HALVES:
                norm_stats(dve, s, src, eps, tiles, chain)
            for part, tiles in enumerate(HALVES):
                norm_scale(dve, s, src, tiles, part)

        def norm_pool(pool, s):
            for part, tiles in enumerate(HALVES):
                norm_root(pool, s, tiles, part)

        def affine_rows(dve, sem, g, b):
            for h in range(2):
                x = XN[:, 4 * h:4 * h + 4, :]
                for i, (name, op) in enumerate(((g, ALU.mult), (b, ALU.add))):
                    dve.tensor_tensor(x, x, row(name).unsqueeze(1).to_broadcast([P, 4, P]), op).then_inc(sem, 1)
                    dve.wait_ge(sem, 2 * h + i + 1)

        def turn_rows(pe, s, src, dst, name, affine=None):
            for t in range(NT):
                if affine and t % 4 == 0:
                    pe.wait_ge(affine, t // 2 + 2)
                ins = pe.transpose(dst[:, t * P:(t + 1) * P], src[:, t, :], IDF[:, :])
                if t % 4 == 3:
                    ins.then_inc(s[name], 1)

        PREP_NAMES = "k_made v_made v_kept k_kept k_hi k_rest k_mid k_lo " \
                     "k_stored0 k_stored1 k_stored2 k_stored3 k_placed0 k_placed1 k_placed2 k_placed3"

        def prep_tensor(pe, s, a, src, c, k_bank, v_bank):
            pe.matmul(k_bank, WA[:, a, 1, :], src[:, c * 512:(c + 1) * 512], start=True, stop=True)\
              .then_inc(s["k_made"], 1)
            for t in range(4):
                ins = pe.matmul(v_bank[:, t * P:(t + 1) * P], src[:, (4 * c + t) * P:(4 * c + t + 1) * P],
                                WA[:, a, 2, :], start=True, stop=True)
            ins.then_inc(s["v_made"], 1)

        def prep_scalar(act, s, a, c, k_bank, v_bank, bufs):
            keys, hi = bufs[0][:, c % 2, :], bufs[1]
            if a != 2:
                act.wait_ge(s["k_made"], c + 1)
                if c >= 2:
                    act.wait_ge(s["k_rest"], c - 1)
                act.activation(keys, k_bank, ACT.Identity, bias=col(f"bk{a}")).then_inc(s["k_kept"], 1)
            act.wait_ge(s["k_kept"], c + 1)
            n = hi.shape[1]
            if c >= n:
                act.wait_ge(s[f"k_stored{c - n}"], 48)
            act.activation(hi[:, c % n, :], keys, ACT.Copy).then_inc(s["k_hi"], 1)
            act.wait_ge(s["v_made"], c + 1)
            o = V[:, 4 * c:4 * c + 4, 0:9 * HEADS].rearrange("p t (h e) -> p t h e", e=9)[:, :, :, 0:DH]
            act.activation(o, v_bank.rearrange("p (t h e) -> p t h e", t=4, e=DH), ACT.Copy).then_inc(s["v_kept"], 1)

        def prep_middle(act, s, c, bufs):
            mid = bufs[2]
            act.wait_ge(s["k_rest"], c + 1)
            act.activation(mid[:, c % mid.shape[1], :], REST[:, c % 2, :], ACT.Copy).then_inc(s["k_mid"], 1)

        def prep_vector(dve, s, c, k_bank, bufs):
            dve.wait_ge(s["k_made"], c + 1)
            if c >= 2:
                dve.wait_ge(s["k_rest"], c - 1)
            dve.scalar_tensor_tensor(bufs[0][:, c % 2, :], KEEP[:, c * 512:(c + 1) * 512], 0.0, k_bank,
                                     ALU.is_equal, ALU.mult).then_inc(s["k_kept"], 1)

        def prep_pool(pool, s, c, bufs):
            keys, hi, mid, lo = bufs
            n = hi.shape[1]
            pool.wait_ge(s["k_hi"], c + 1)
            if c >= 2:
                pool.wait_ge(s["k_lo"], c - 1)
            pool.tensor_tensor(REST[:, c % 2, :], keys[:, c % 2, :], hi[:, c % n, :], ALU.subtract)\
                .then_inc(s["k_rest"], 1)
            pool.wait_ge(s["k_mid"], c + 1)
            if c >= n:
                pool.wait_ge(s[f"k_stored{c - n}"], 48)
            pool.tensor_tensor(lo[:, c % n, :], REST[:, c % 2, :], mid[:, c % n, :], ALU.subtract)\
                .then_inc(s["k_lo"], 1)

        def prep_store(sp, s, c, bufs):
            for r, (part, name) in enumerate(zip(bufs[1:], ("k_hi", "k_mid", "k_lo"))):
                sp.wait_ge(s[name], c + 1)
                sp.dma_start(k_parts[c, r], part[:, c % part.shape[1], :]).then_inc(s[f"k_stored{c}"], 16)

        def prep_place(sp, s, c):
            sp.wait_ge(s[f"k_stored{c}"], 48)
            for m in range(2):
                src = k_parts[c, :, m * 64:(m + 1) * 64, :].rearrange("r (d p) n -> r d (p n)", p=NP)
                r0 = m * CW
                sp.dma_start(KOP[r0:r0 + 24, c, :, :], src[0:3]).then_inc(s[f"k_placed{c}"], 16)
                sp.dma_start(KOP[r0 + 24:r0 + 40, c, :, :], src[0:2]).then_inc(s[f"k_placed{c}"], 16)
                sp.dma_start(KOP[r0 + 40:r0 + 48, c, :, :], src[0]).then_inc(s[f"k_placed{c}"], 16)


        stored = nc.alloc_semaphore("stored")
        LOAD_NAMES = "x ctx wk mask0 c zero idf ones consts mask_row k0 half v1 first_var first_rstd first_rows"

        def load_sync(sp, s, M0, MASKS0):
            sp.dma_start(M0[MASK_ROW:MASK_ROW + 1, :], d["mask0"]).then_inc(s["mask0"], 16)
            sp.dma_start(X[:, :, :], d["x"].rearrange("(t p) e -> p t e", p=P)).then_inc(s["x"], 16)
            sp.dma_start(WA[:, 0, :, :], d["wattn"][:, 0, :, :]).then_inc(s["wk"], 16)
            sp.dma_start(C[:, :], d["cols"]).then_inc(s["c"], 16)
            sp.dma_start(CTX[:, :], d["ctxT"]).then_inc(s["ctx"], 16)
            sp.wait_ge(s["ones"], 1)
            ones = ONES[MASK_ROW:MASK_ROW + 3, :].unsqueeze(1)
            sp.dma_start(KOP[MASK_ROW + 1:MASK_ROW + 3, :, :, :].rearrange("r a b n -> r (a b) n"),
                         ones[1:3].to_broadcast([2, 32, 512])).then_inc(s["k0"], 16)
            sp.wait_ge(s["mask_row"], 1)
            for c in range(4):
                sp.dma_start(KOP[MASK_ROW:MASK_ROW + 1, c, :, :],
                             MASKS0[MASK_ROW:MASK_ROW + 1, c * 512:(c + 1) * 512].unsqueeze(1)
                             .to_broadcast([1, NP, 512])).then_inc(s["k0"], 16)

        def load_pool(pool, s, first):
            pool.memset(IDF[:, :], 0.0).then_inc(s["zero"], 1)
            pool.memset(HALF[:, :], -0.5).then_inc(s["half"], 1)
            pool.memset(NEGC[:, :], 0.0).then_inc(s["zero"], 1)
            pool.memset(STAIR[:, :], 0.0).then_inc(s["zero"], 1)
            pool.wait_ge(s["zero"], 3)
            pool.affine_select(out=IDF[:, :], in_=IDF[:, :], compare_op=ALU.not_equal, fill=1.0, base=0,
                               pattern=[[-1, P]], channel_multiplier=1).then_inc(s["idf"], 1)
            pool.affine_select(out=NEGC[:, :], in_=NEGC[:, :], compare_op=ALU.is_ge, fill=NEG, base=3,
                               pattern=[[-1, SK]], channel_multiplier=4).then_inc(s["consts"], 1)
            pool.affine_select(out=STAIR[:, :], in_=STAIR[:, :], compare_op=ALU.is_ge, fill=NEG, base=3,
                               pattern=[[4, 32]], channel_multiplier=-1).then_inc(s["consts"], 1)
            for e in range(NE):
                pool.memset(IOTA[:, :, e], float(e))
            pool.wait_ge(s["idf"], 1)
            pool.tensor_copy(IDB[:, :], IDF[:, :]).then_inc(s["consts"], 1)
            pool.memset(V[:, :, :], 1.0).then_inc(s["v1"], 1)
            pool.wait_ge(s["half"], 1)
            norm_pool(pool, first)

        def load_vector(dve, s, first, M0, MASKS0):
            dve.memset(ONES[:, :], 1.0).then_inc(s["ones"], 1)
            dve.wait_ge(s["mask0"], 16)
            dve.tensor_scalar(MASKS0[MASK_ROW:MASK_ROW + 1, :], M0[MASK_ROW:MASK_ROW + 1, :],
                              -NEG, NEG, ALU.mult, ALU.add).then_inc(s["mask_row"], 1)
            dve.wait_ge(s["x"], 16)
            norm_vector(dve, first, X, EPS, Chain(dve, s["chain"]))


        def attention(a):
            own = a == 4
            nk = SQ if own else SK
            nkt = nk // P
            stairs = a == 1
            if stairs:
                places = [(0, 0), (512, 32), (512 + 224, 64), (256, 96)]
                width, banks = 416, 2
            elif own:
                places = [(0, 0), (256, 0)]
                width, banks = 512, 1
            else:
                places = [(256 * i, 0) for i in range(4)]
                width, banks = 512, 2
            rows_out = XN if own else X
            last = B * NG
            look = 3
            chunks = {0: 4, 4: 2}.get(a, 0)
            norms = 2 if a == 0 else 1

            def cleared(h):
                return QOP[0:MASK_ROW, h, :, :].rearrange("p b n -> p (b n)").bitcast(F32)
            own_tensor, mem = phase_memory(f"attn{a}")
            QOP = own_tensor("QOP", [P, 2, HEADS, TH], BF16)
            PT = own_tensor("PT", [P, 8, 1024])
            QHI, QMID, QLO = (own_tensor(n, [P, 2, TH], BF16) for n in ("QHI", "QMID", "QLO"))
            QREST = own_tensor("QREST", [P, 2, TH])
            parts_of_keys = (own_tensor("KEYS", [P, 2, 512]), HI, MID, LO) if chunks else None
            if a == 0:
                masks = own_tensor("MASKS", [P, T], F32).bitcast(U8)
                M0 = masks[:, 0:TK]
                M2 = masks[:, TK:TK + 2 * SK].rearrange("p (t k) -> p t k", t=2)
                M2T = masks[:, TK + 2 * SK:TK + 2 * SK + 4 * SQ].rearrange("p (t k) -> p t k", t=4)
                MASKS0 = QREST[:, :, :].rearrange("p h n -> p (h n)").bitcast(BF16)

            def spot(k):
                return k // NG, k % NG // 2, 4 * (k % 2)

            def queries(k, j, lo, n, rows):
                b, m, p0 = spot(k)
                x = (b % 2) * SQ + lo
                return QOP[0:rows, b // 2, m * NP + p0 + j, x:x + n]

            def keys(k, j, lo, n, rows):
                b, m, p0 = spot(k)
                x = b * nk + lo
                return KOP[0:rows, x // 512, p0 + j, x % 512:x % 512 + n]

            ahead = 2 * GROUP * (look - 1)

            def score_bank(c):
                i = c % 4 if c < ahead else c % 2
                return PS[0 if i >= 2 else 2][:, (c % 2) * 512:(c % 2) * 512 + nk]

            def filled(t):
                return t.rearrange("p (k n) -> p k n", k=2)[:, 0:banks, 0:width]

            turn = {}
            for n in range(-look, last + 2):
                if 0 <= n - 2:
                    turn["rows", n - 2] = len(turn)
                if 0 <= n + look - 1 < last:
                    turn["shift", n + look - 1] = len(turn)
                if n - 2 >= 0 and (n - 2) % NG == NG - 1:
                    turn["cols", (n - 2) // NG] = len(turn)
                    turn["out", (n - 2) // NG] = len(turn)

            s = signals(nc, f"attn{a}", "var rstd norm_rows chain turned kept q_made q_hi q_rest q_mid q_lo "
                        "q_stored0 q_stored1 q_stored2 q_placed00 q_placed01 q_placed10 q_placed11 biased scored "
                        "maxed neg shift shift_placed0 shift_placed1 scored_t exps summed o_kept x_made x_read rc "
                        "late mask cleared0 cleared1 rows_chain q_ones w_early "
                        + (PREP_NAMES if chunks else "") + " " + (LOAD_NAMES if a == 0 else ""), before)
            if a == 0:
                first = {n: s[f"first_{m}"] for n, m in (("var", "var"), ("rstd", "rstd"), ("norm_rows", "rows"))}
            SUM = PS[3][:, 0:256]
            XB = PS[3][:, 512:1024]
            XBH = XB.bitcast(BF16)

            with nc.Block() as block:
                @block.sync
                def _(sp):
                    parts = ((QHI, "q_hi", 0, 3), (QMID, "q_mid", 24, 2), (QLO, "q_lo", 40, 1))

                    def ones_row():
                        sp.dma_start(QOP[MASK_ROW:MASK_ROW + 1, :, :, :].rearrange("r a b n -> r (a b) n"),
                                     ONES[MASK_ROW:MASK_ROW + 1, :].unsqueeze(1).to_broadcast([1, 32, 512]))\
                          .then_inc(s["q_ones"], 16)

                    def store(h, r):
                        part, name = parts[r][0:2]
                        sp.wait_ge(s[name], h + 1)
                        sp.dma_start(q_parts[h, r], part[:, h, :]).then_inc(s[f"q_stored{r}"], 16)

                    def place(h):
                        for m in range(2):
                            for r, (_, _, r0, n) in enumerate(parts):
                                sp.wait_ge(s[f"q_stored{r}"], 16 * (h + 1))
                                if r == 0 and m == 0:
                                    sp.wait_ge(s[f"cleared{h}"], 1)
                                src = q_parts[h, r, m * 64:(m + 1) * 64, :].rearrange("(d p) n -> d (p n)", p=NP)
                                if n > 1:
                                    src = src.unsqueeze(0).to_broadcast([n, DH, NP * TH])
                                sp.dma_start(QOP[m * CW + r0:m * CW + r0 + n * DH, h, m * NP:(m + 1) * NP, :],
                                             src).then_inc(s[f"q_placed{h}{m}"], 16)

                    if a == 0:
                        load_sync(sp, s, M0, MASKS0)
                        sp.dma_start(M2[:, :, :], d["mask2"].rearrange("(t q) k -> q t k", q=P)).then_inc(s["mask"], 16)
                        sp.dma_start(M2T[:, :, :], d["mask2T"].rearrange("(t k) q -> k t q", k=P))\
                          .then_inc(s["mask"], 16)
                    ones_row()
                    if chunks:
                        prep_store(sp, s, 0, parts_of_keys)
                    for r in range(3):
                        store(0, r)
                    if chunks:
                        prep_place(sp, s, 0)
                    place(0)
                    if chunks:
                        prep_store(sp, s, 1, parts_of_keys)
                    for r in range(3):
                        store(1, r)
                    if not own:
                        place(1)

                    def late_loads():
                        sp.dma_start(R[:, :], d["rows"].partition_broadcast(P)).then_inc(s["late"], 16)
                        sp.dma_start(WR[:, :, :], d["wrouter"]).then_inc(s["late"], 16)
                        sp.dma_start(WCONV[:, :, :], d["wconv"]).then_inc(s["late"], 16)
                        sp.dma_start(WA[:, 1:5, :, :], d["wattn"][:, 1:5, :, :]).then_inc(s["late"], 16)
                        sp.dma_start(KEEP[:, :], d["mask_keys"].partition_broadcast(P)).then_inc(s["late"], 16)
                    for k in range(last):
                        b, m, p0 = spot(k)
                        sp.wait_ge(s["x_read"], turn["shift", k] + 1)
                        for r in range(2):
                            sp.dma_start(QOP[SHIFT_ROW + r:SHIFT_ROW + r + 1, b // 2,
                                             m * NP + p0:m * NP + p0 + GROUP,
                                             (b % 2) * SQ:(b % 2) * SQ + SQ],
                                         SH[r * GROUP:(r + 1) * GROUP, k % 2, :])\
                              .then_inc(s[f"shift_placed{k % 2}"], 16)
                        if k + 1 < chunks:
                            if k > 0:
                                prep_store(sp, s, k + 1, parts_of_keys)
                            prep_place(sp, s, k + 1)
                        if k == 1 and own:
                            place(1)
                        if a == 0 and k == 3:
                            late_loads()
                        if k == 4 and a != 3:
                            w = d[f"we{min(a, 3)}"]
                            for e in range(2):
                                sp.dma_start(W[:, e, 0:EW[min(a, 3)]], w[e]).then_inc(s["w_early"], 16)
                    for r in range(2):
                        sp.wait_ge(s[f"shift_placed{r}"], 32 * last // 2)
                    if a == 0:
                        sp.wait_ge(s["late"], 80)
                    if a != 3:
                        sp.wait_ge(s["w_early"], 32)

                @block.gpsimd
                def _(pool):
                    if a == 0:
                        load_pool(pool, s, first)
                    if own:
                        for c in range(chunks):
                            prep_pool(pool, s, c, parts_of_keys)
                    pool.memset(cleared(1), 0.0).then_inc(s["cleared1"], 1)
                    if a > 0:
                        pool.tensor_tensor(rows_out[:, :, :], rows_out[:, :, :],
                                           row(f"bo{a}").unsqueeze(1).to_broadcast([P, NT, P]), ALU.add)\
                            .then_inc(s["biased"], 1)
                    if a == 0:
                        for c in range(chunks):
                            prep_pool(pool, s, c, parts_of_keys)

                    def roots(b):
                        for i in range(norms):
                            norm_root(pool, s, range(2 * b, 2 * b + 2), norms * b + i)
                    for k in range(last):
                        b = (k - look - 6) // NG
                        if b >= 0 and k - look == NG * b + 6:
                            roots(b)
                            rooted = b + 1
                        pool.wait_ge(s["maxed"], 2 * GROUP * (k + 1))
                        if k >= 4:
                            pool.wait_ge(s["x_made"], turn["shift", k - 4] + 1)
                        pool.tensor_scalar(NG32[:, k % 4], NM[:, k % 4], -1.0, None, ALU.mult)\
                            .then_inc(s["neg"], 1)
                        pool.wait_ge(s["neg"], 2 * k + 1)
                        pool.tensor_copy(HL[:, k % 4, :, 0, :], NG32[:, k % 4]).then_inc(s["neg"], 1)
                        pool.wait_ge(s["neg"], 2 * k + 2)
                        pool.tensor_tensor(HL[:, k % 4, :, 1, :], NG32[:, k % 4], HL[:, k % 4, :, 0, :],
                                           ALU.subtract).then_inc(s["shift"], 1)
                    for b in range(rooted, B):
                        roots(b)

                @block.vector
                def _(dve):
                    if a == 0:
                        load_vector(dve, s, first, M0, MASKS0)
                    chain = Chain(dve, s["rows_chain"])
                    if a == 0:
                        dve.wait_ge(s["c"], 16)
                        dve.wait_ge(s["k0"], 80)
                    dve.memset(cleared(0), 0.0).then_inc(s["cleared0"], 1)
                    for h in range(2):
                        dve.wait_ge(s["q_hi"], h + 1)
                        dve.scalar_tensor_tensor(QREST[:, h, :], PS[1][:, h * TH:(h + 1) * TH], col(f"bq{a}"),
                                                 QHI[:, h, :], ALU.add, ALU.subtract).then_inc(s["q_rest"], 1)
                        dve.wait_ge(s["q_rest"], h + 1)
                        dve.tensor_copy(QMID[:, h, :], QREST[:, h, :]).then_inc(s["q_mid"], 1)
                        dve.wait_ge(s["q_mid"], h + 1)
                        dve.tensor_tensor(QLO[:, h, :], QREST[:, h, :], QMID[:, h, :], ALU.subtract)\
                           .then_inc(s["q_lo"], 1)
                    if a == 0:
                        dve.wait_ge(s["mask"], 32)
                        dve.tensor_scalar(NEG2[:, :, :], M2[:, :, :], NEG, None, ALU.mult)
                        dve.tensor_scalar(NEG2T[:, :, :], M2T[:, :, :], NEG, None, ALU.mult)

                    def maxima(k, j):
                        for q in range(2):
                            c = 2 * (GROUP * k + j) + q
                            dve.wait_ge(s["scored"], c + 1)
                            if k >= 4:
                                dve.wait_ge(s["shift"], k - 3)
                            x = score_bank(c)
                            m = NM[:, k % 4, q, j:j + 1]
                            if a == 2 or (stairs and q == 0):
                                if c >= 2:
                                    dve.wait_ge(s["maxed"], c - 1)
                                dve.tensor_tensor_reduce(SEEN[:, c % 2, :], x, NEG2[:, q, :] if a == 2 else NEGC[:, :],
                                                         1.0, NEG * 4, ALU.add, ALU.max, m).then_inc(s["maxed"], 1)
                            else:
                                dve.tensor_reduce(m, x, AX.X, ALU.max).then_inc(s["maxed"], 1)

                    def normalize(k):
                        b, m, p0 = spot(k)
                        dve.wait_ge(s["x_made"], turn["rows", k] + 1)
                        x = XB[:, 0:256].rearrange("p (t j e) -> p t j e", t=2, j=GROUP)
                        dve.reciprocal(RC[:, k % 2, :, :], x[:, :, :, DH]).then_inc(s["rc"], 1)
                        dve.wait_ge(s["rc"], k + 1)
                        if k % NG == 0 and b >= 2:
                            dve.wait_ge(s["x_made"], turn["cols", b - 2] + 1)
                        o = ON[:, b % 2, :, :].rearrange("p t (r m e) -> p t r m e", m=2, e=DH)
                        dve.tensor_tensor(o[:, :, p0:p0 + GROUP, m, :], x[:, :, :, 0:DH],
                                          RC[:, k % 2, :, :].unsqueeze(3).to_broadcast([P, 2, GROUP, DH]),
                                          ALU.mult).then_inc(s["x_read"], 1)

                    def add_out(b):
                        dve.wait_ge(s["x_made"], turn["out", b] + 1)
                        if a > 0:
                            dve.wait_ge(s["biased"], 1)
                        o = rows_out[:, 2 * b:2 * b + 2, :]
                        dve.tensor_tensor(o, XB[:, 0:256].rearrange("p (t e) -> p t e", t=2), o, ALU.add)\
                           .then_inc(s["x_read"], 1)

                    def norm_step(b, j):
                        tiles = range(2 * b, 2 * b + 2)
                        if j == 0:
                            dve.wait_ge(s["x_read"], turn["out", b] + 1)
                            norm_stats(dve, s, rows_out, EPS, tiles, chain)
                        elif j == 1:
                            norm_scale(dve, s, rows_out, tiles, norms * b)
                        elif j == 2 and norms == 2:
                            dve.wait_ge(s["norm_rows"], 4 * b + 2)
                            norm_stats(dve, s, XN, EPS_IN, tiles, chain)
                        elif j == 3 and norms == 2:
                            norm_scale(dve, s, XN, tiles, norms * b + 1)

                    for n in range(-look, last + 2):
                        k = n + look
                        for j in range(GROUP):
                            if k < last:
                                maxima(k, j)
                            if n >= NG + 2 and (n - 2) % NG == 0:
                                norm_step((n - 2) // NG - 1, j)
                            if j == 0 and n - 2 >= 0:
                                normalize(n - 2)
                            if j == 3 and n - 2 >= 0 and (n - 2) % NG == NG - 1:
                                add_out((n - 2) // NG)
                    for j in range(GROUP):
                        norm_step(B - 1, j)

                @block.scalar
                def _(act):
                    if a == 0:
                        act.wait_ge(s["c"], 16)
                        act.wait_ge(s["v1"], 1)
                    if chunks:
                        prep_scalar(act, s, a, 0, *kv_banks(0), parts_of_keys)
                    if a == 0:
                        prep_middle(act, s, 0, parts_of_keys)
                    if not own:
                        for h in range(2):
                            act.wait_ge(s["turned"], h + 1)
                            act.activation(XNT[:, h * TH:(h + 1) * TH], PS[0][:, h * TH:(h + 1) * TH], ACT.Copy)\
                               .then_inc(s["kept"], 1)
                    for h in range(2):
                        act.wait_ge(s["q_made"], h + 1)
                        act.activation(QHI[:, h, :], PS[1][:, h * TH:(h + 1) * TH], ACT.Identity,
                                       bias=col(f"bq{a}")).then_inc(s["q_hi"], 1)
                    if own:
                        prep_middle(act, s, 0, parts_of_keys)
                    for c in range(1, chunks):
                        prep_scalar(act, s, a, c, *kv_banks(c), parts_of_keys)
                        prep_middle(act, s, c, parts_of_keys)

                    def exponentials(n, j):
                        u = GROUP * n + j
                        act.wait_ge(s["scored_t"], u + 1)
                        if n >= 2:
                            act.wait_ge(s["summed"], n - 1)
                        act.activation(filled(PT[:, u % 8, :]), filled(PS[u % 2][:, :]), ACT.Exp, scale=SCALE)\
                           .then_inc(s["exps"], 1)

                    def keep_shift(k):
                        act.wait_ge(s["x_made"], turn["shift", k] + 1)
                        if k >= 2:
                            act.wait_ge(s[f"shift_placed{k % 2}"], 32 * (k // 2))
                        act.activation(SH[:, k % 2, :], XBH[0:2 * GROUP, 0:256], ACT.Copy)\
                           .then_inc(s["x_read"], 1)

                    def keep_sums(k):
                        act.wait_ge(s["summed"], k + 1)
                        if k >= 2:
                            act.wait_ge(s["x_made"], turn["rows", k - 2] + 1)
                        act.activation(OT[:, k % 2, :], SUM, ACT.Copy).then_inc(s["o_kept"], 1)

                    def keep_cols(b):
                        act.wait_ge(s["x_made"], turn["cols", b] + 1)
                        act.activation(CT[:, b % 2, :], XB[:, 0:256], ACT.Identity, bias=col(f"bv{a}"))\
                           .then_inc(s["x_read"], 1)

                    for n in range(-look, last + 2):
                        for j in range(GROUP):
                            if 0 <= n < last:
                                exponentials(n, j)
                            if j == 1 and 0 <= n + look - 1 < last:
                                keep_shift(n + look - 1)
                            if j == nkt - 1 and 0 <= n - 1 < last:
                                keep_sums(n - 1)
                            if j == 2 and n - 2 >= 0 and (n - 2) % NG == NG - 1:
                                keep_cols((n - 2) // NG)

                @block.tensor
                def _(pe):
                    if a == 0:
                        pe.wait_ge(s["ctx"], 16)
                        pe.wait_ge(s["wk"], 16)
                    if chunks:
                        prep_tensor(pe, s, a, XNT if own else CTX, 0, *kv_banks(0))
                    if a == 0:
                        pe.wait_ge(s["idf"], 1)
                        pe.wait_ge(s["first_rows"], NT)
                    if not own:
                        turn_rows(pe, s, XN, PS[0], "turned")
                    for h in range(2):
                        if not own:
                            pe.wait_ge(s["kept"], h + 1)
                        pe.matmul(PS[1][:, h * TH:(h + 1) * TH], WA[:, a, 0, :], XNT[:, h * TH:(h + 1) * TH],
                                  start=True, stop=True).then_inc(s["q_made"], 1)
                    for c in range(1, chunks):
                        if c >= 2:
                            pe.wait_ge(s["k_kept"], c - 1)
                            pe.wait_ge(s["v_kept"], c - 1)
                        prep_tensor(pe, s, a, XNT if own else CTX, c, *kv_banks(c))
                    if chunks:
                        pe.wait_ge(s["k_kept"], chunks)

                    pe.wait_ge(s["q_ones"], 16)
                    if a == 0:
                        pe.wait_ge(s["consts"], 3)
                        pe.wait_ge(s["k0"], 80)

                    def scores(k, j):
                        b = k // NG
                        if k % (2 * NG) in (0, 2) and j == 0:
                            pe.wait_ge(s[f"q_placed{b // 2}{k % NG // 2}"], 48)
                        if chunks and (k * nk // NG) % 512 == 0 and j == 0:
                            pe.wait_ge(s[f"k_placed{b * nk // 512}"], 96)
                        for q in range(2):
                            c = 2 * (GROUP * k + j) + q
                            back = 4 if c < ahead else 2
                            if c >= back:
                                pe.wait_ge(s["maxed"], c - back + 1)
                            o = score_bank(c)
                            pe.matmul(o, queries(k, j, q * P, P, MASK_ROW + 1), keys(k, j, 0, nk, MASK_ROW + 1),
                                      start=True, stop=True).then_inc(s["scored"], 1)

                    def scores_t(n, j):
                        u = GROUP * n + j
                        if j == 0:
                            pe.wait_ge(s[f"shift_placed{n % 2}"], 32 * (n // 2 + 1))
                        if u == 0:
                            pe.wait_ge(s["maxed"], ahead)
                        if u >= 2:
                            pe.wait_ge(s["exps"], u - 1)
                        for i, (x, q0) in enumerate(places):
                            o = PS[u % 2][:, x:x + SQ - q0]
                            ins = pe.matmul(o, keys(n, j, i * P, P, SHIFT_ROW + 2),
                                            queries(n, j, q0, SQ - q0, SHIFT_ROW + 2), start=True, stop=a != 2)
                            if a == 2:
                                ins = pe.matmul(o, IDB[:, :], NEG2T[:, i, :], start=False, stop=True)
                            if stairs:
                                ins = pe.matmul(PS[u % 2][:, x:x + 32], IDB[:, :], STAIR[:, :], start=False,
                                                stop=True, skip_group_check=True)
                        ins.then_inc(s["scored_t"], 1)

                    def sums(n, i):
                        b, m, p0 = spot(n)
                        if i == 0:
                            pe.wait_ge(s["exps"], GROUP * (n + 1))
                            if n >= 1:
                                pe.wait_ge(s["o_kept"], n)
                        x, q0 = places[i]
                        for j in range(GROUP):
                            h = 2 * (p0 + j) + m
                            ins = pe.matmul(SUM[32 * j:32 * j + 32, q0:SQ], V[:, b * nkt + i, 9 * h:9 * h + 32],
                                            PT[:, (GROUP * n + j) % 8, x:x + SQ - q0], start=(i == 0),
                                            stop=(i == nkt - 1), tile_position=(0, 32 * j),
                                            skip_group_check=True)
                        if i == nkt - 1:
                            ins.then_inc(s["summed"], 1)

                    def my_turn(what, k):
                        if turn[what, k]:
                            pe.wait_ge(s["x_read"], turn[what, k])

                    for n in range(-look, last + 2):
                        k = n + look
                        if k == 1 and chunks:
                            pe.wait_ge(s["v_kept"], chunks)
                        for j in range(GROUP):
                            if 0 <= n < last:
                                scores_t(n, j)
                            if k < last:
                                scores(k, j)
                            if 0 <= n - 1 < last and j < nkt:
                                sums(n - 1, j)
                            if j == 0 and n - 2 >= 0:
                                g = n - 2
                                my_turn("rows", g)
                                pe.wait_ge(s["o_kept"], g + 1)
                                for t in range(2):
                                    ins = pe.transpose(XB[:, t * P:(t + 1) * P], OT[:, g % 2, t * P:(t + 1) * P],
                                                       IDF[:, :])
                                ins.then_inc(s["x_made"], 1)
                            if j == 1 and 0 <= k - 1 < last:
                                g = k - 1
                                my_turn("shift", g)
                                pe.wait_ge(s["shift"], g + 1)
                                for t in range(2):
                                    ins = pe.transpose(XBH[0:2 * GROUP, t * P:(t + 1) * P],
                                                       HL[:, g % 4, t, :, :].rearrange("p r j -> p (r j)"), IDB[:, :])
                                ins.then_inc(s["x_made"], 1)
                            if j == 2 and n - 2 >= 0 and (n - 2) % NG == NG - 1:
                                b = (n - 2) // NG
                                my_turn("cols", b)
                                for t in range(2):
                                    ins = pe.transpose(XB[:, t * P:(t + 1) * P], ON[:, b % 2, t, :], IDF[:, :])
                                ins.then_inc(s["x_made"], 1)
                            if j == 3 and n - 2 >= 0 and (n - 2) % NG == NG - 1:
                                b = (n - 2) // NG
                                my_turn("out", b)
                                for t in range(2):
                                    ins = pe.matmul(XB[:, t * P:(t + 1) * P], CT[:, b % 2, t * P:(t + 1) * P],
                                                    WA[:, a, 3, :], start=True, stop=True)
                                ins.then_inc(s["x_made"], 1)
            mem.close()


        def experts(l):
            gated_out = l in (0, 3)
            final = l == 3
            hid = HID[l]
            sizes = [min(P, hid - P * c) for c in range(-(-hid // P))]
            nch = len(sizes)
            units = NE * nch * (1 if gated_out else 2)
            s = signals(nc, f"ffn{l}", "var rstd norm_rows chain turned kept scaled_r routed ex sub gates g_turned "
                        "g_kept g_stored " + " ".join(f"g_loaded{e}" for e in range(NE)) + " affine w_loaded0 w_loaded1 up "
                        "acted h_made down y_used added acc biased back no_mask lg_read summed h_hi h_full u_full w_first_hi w_first w_hi "
                        "w_made x_hi x_made " + (PREP_NAMES if not final else ""), before)
            prep = l + 1 if not final else None
            dpe = units // NE
            ew = EW[l]
            own_tensor, mem = phase_memory(f"ffn{l}")
            WHI, WLO = (own_tensor(n, [P, 3, ew]) for n in ("WHI", "WLO"))
            XHI, XLO = (own_tensor(n, [P, 2 if l == 0 else 1, T]) for n in ("XHI", "XLO"))
            nh = 4 if gated_out else 3
            HF, HHI, HLO = (own_tensor(n, [P, nh, TH]) for n in ("HF", "HHI", "HLO"))
            if not gated_out:
                HG = own_tensor("HG", [P, 2, TH])
            YG = own_tensor("YG", [P, T])
            GB = own_tensor("GB", [P, 2, T])
            if l == 0:
                UF = own_tensor("UF", [P, T])
            parts_of_keys = (own_tensor("KEYS", [P, 2, 512]), HI, MID, LO) if not final else None

            def inputs_lo(eng, e):
                eng.wait_ge(s["u_full"], 2 * (e + 1))
                eng.tensor_tensor(f32r(XLO[:, e % 2, :]), UF[:, :], XHI[:, e % 2, :], ALU.subtract)\
                   .then_inc(s["x_made"], 1)

            def weights_hi(copy, eng, e):
                if e >= 2:
                    eng.wait_ge(s[f"w_loaded{e % 2}"], 16 * (e // 2))
                if e >= 3:
                    eng.wait_ge(s["down"], dpe * (e - 2))
                copy(f32r(WHI[:, e % 3, :]), W[:, e % 2, 0:ew]).then_inc(s["w_hi" if e else "w_first_hi"], 1)

            def weights_lo(eng, e):
                eng.wait_ge(s["w_hi" if e else "w_first_hi"], max(e, 1))
                eng.tensor_tensor(f32r(WLO[:, e % 3, :]), W[:, e % 2, 0:ew], WHI[:, e % 3, :], ALU.subtract)\
                   .then_inc(s["w_made" if e else "w_first"], 1)

            PREP_UNITS = (3, 4) if gated_out else (3, 7)

            def banks(c):
                b = PS[3] if gated_out else PS[PREP_UNITS[c - 2] % 3]
                return kv_banks(c) if c < 2 else (b[:, 0:512], b[:, 512:1024])

            GBANK = PS[3] if gated_out else PS[2]
            with nc.Block() as block:
                @block.sync
                def _(sp):
                    if not final:
                        for c in range(4):
                            prep_store(sp, s, c, parts_of_keys)
                            prep_place(sp, s, c)
                    if l == 0:
                        sp.wait_ge(s["no_mask"], 1)
                        sp.dma_start(KOP[MASK_ROW:MASK_ROW + 1, :, :, :].rearrange("r a b n -> r (a b) n"),
                                     ONES[0:1, :].unsqueeze(1).to_broadcast([1, 32, 512])).then_inc(s["k_placed0"], 16)
                    if not final:
                        for c in range(4):
                            sp.wait_ge(s[f"k_placed{c}"], 112 if l == 0 and c == 0 else 96)
                    else:
                        for h in range(2):
                            x = slice(4 * h, 4 * h + 4)
                            sp.wait_ge(s["acc"], h + 1)
                            sp.dma_start(out.rearrange("(t p) e -> p t e", p=P)[:, x, :], XN[:, x, :])\
                              .then_inc(stored, 16)
                        sp.wait_ge(stored, 32)

                @block.gpsimd
                def _(pool):
                    if l == 0:
                        pool.memset(ONES[0:1, :], 0.0).then_inc(s["no_mask"], 1)
                    if not final:
                        for c in range(2):
                            prep_pool(pool, s, c, parts_of_keys)
                    weights_lo(pool, 1)
                    if not final:
                        for c in range(2, 4):
                            prep_pool(pool, s, c, parts_of_keys)
                    if final:
                        pool.tensor_tensor(X[:, :, :], X[:, :, :],
                                           row("ln2_b").unsqueeze(1).to_broadcast([P, NT, P]), ALU.add)\
                            .then_inc(s["biased"], 1)
                    if l == 1:
                        pool.tensor_tensor(X[:, :, :], X[:, :, :],
                                           row("ffn1_bias").unsqueeze(1).to_broadcast([P, NT, P]), ALU.add)\
                            .then_inc(s["biased"], 1)
                    for e in range(1, NE - 1):
                        weights_lo(pool, e + 1)
                        if l == 0:
                            inputs_lo(pool, e + 1)
                        for h in range(2):
                            x = slice(h * TH, (h + 1) * TH)
                            pool.wait_ge(s["y_used"], 2 * e + h + 1)
                            pool.tensor_tensor(ACC[:, x], ACC[:, x], YG[:, x], ALU.add).then_inc(s["added"], 1)
                    norm_pool(pool, s)

                @block.vector
                def _(dve):
                    chain = Chain(dve, s["chain"])
                    if final:
                        affine_rows(dve, s["affine"], "ln1_g", "ln1_b")
                    weights_hi(dve.tensor_copy, dve, 0)
                    weights_lo(dve, 0)
                    if prep == 2:
                        prep_vector(dve, s, 0, banks(0)[0], parts_of_keys)
                        prep_vector(dve, s, 1, banks(1)[0], parts_of_keys)
                    if l == 0:
                        dve.wait_ge(s["kept"], 2)
                        dve.tensor_scalar(YG[:, :], XNT[:, :], col("rln_s"), col("rln_b"), ALU.mult, ALU.add)\
                           .then_inc(s["scaled_r"], 1)

                    if l > 0:
                        dve.wait_ge(s["kept"], 2)
                        dve.tensor_copy(f32r(XHI[:, 0, :]), XNT[:, :]).then_inc(s["x_hi"], 1)
                        dve.wait_ge(s["x_hi"], 1)
                        dve.tensor_tensor(f32r(XLO[:, 0, :]), XNT[:, :], XHI[:, 0, :], ALU.subtract)\
                           .then_inc(s["x_made"], 1)

                    def inputs(e):
                        if e >= 1:
                            dve.wait_ge(s["x_made"], e)
                        if e >= 2:
                            dve.wait_ge(s["up"], 2 * nch * (e - 1))
                        for o in (f32r(XHI[:, e % 2, :]), UF[:, :]):
                            dve.tensor_scalar(o, XNT[:, :], col("eln_s", e), col("eln_b", e), ALU.mult, ALU.add)\
                               .then_inc(s["u_full"], 1)
                        if e < 2:
                            inputs_lo(dve, e)
                    if l == 0:
                        inputs(0)
                    dve.wait_ge(s["routed"], 1)
                    lg = PS[1][:, 0:NT * NE].rearrange("p (t e) -> p t e", e=NE)
                    if gated_out:
                        dve.tensor_tensor(LG[:, :, :], lg, row(f"router_b{l}").unsqueeze(1).to_broadcast([P, NT, NE]),
                                          ALU.add).then_inc(s["lg_read"], 1)
                    else:
                        dve.tensor_copy(LG[:, :, :], lg).then_inc(s["lg_read"], 1)
                    dve.wait_ge(s["lg_read"], 1)
                    for t in range(NT):
                        ins = dve.max(MX[:, t, :], LG[:, t, :])
                    chain(ins)

                    def wide(v):
                        return v.to_broadcast([P, NT, NE])
                    top1, top2 = MX[:, :, 0:1], MX[:, :, 1:2]
                    D1, OH1, OH2, EX, D2, EX2, T1, T2 = [g[:, :, :] for g in GA]
                    tt = dve.tensor_tensor
                    if l != 3:
                        for t in range(NT):
                            ins = dve.max_index(IX[:, t, :], MX[:, t, :], LG[:, t, :])
                        chain(ins)
                        chain(dve.tensor_copy(IXF[:, :, :], IX[:, :, :]))
                        tt(OH1, IOTA[:, :, :], wide(IXF[:, :, 0:1]), ALU.is_equal)
                        tt(OH2, IOTA[:, :, :], wide(IXF[:, :, 1:2]), ALU.is_equal)
                    tt(D1, LG[:, :, :], wide(top1), ALU.subtract).then_inc(s["sub"], 1)
                    if l == 2:
                        chain(tt(D2, LG[:, :, :], wide(top2), ALU.subtract))
                        dve.tensor_scalar(T2, D2, 0.0, None, ALU.min).then_inc(s["sub"], 1)
                        chain(dve.tensor_scalar(T1, LG[:, :, :], -1.0, None, ALU.mult))
                        chain(tt(T1, T1, LG[:, :, :], ALU.max))
                        chain(tt(LG[:, :, :], T1, wide(top1), ALU.max))
                        chain(dve.scalar_tensor_tensor(LG[:, :, :], LG[:, :, :], 0.02, D1, ALU.mult, ALU.add))
                        chain(dve.tensor_scalar(LG[:, :, :], LG[:, :, :], 0.0, None, ALU.is_ge))
                        chain(tt(T1, T1, wide(top2), ALU.max))
                        chain(dve.scalar_tensor_tensor(T1, T1, 0.02, D2, ALU.mult, ALU.add))
                        chain(dve.tensor_scalar(T1, T1, 0.0, None, ALU.is_ge))
                        chain(dve.scalar_tensor_tensor(T1, OH1, 1.0, T1, ALU.subtract, ALU.mult))
                        dve.wait_ge(s["ex"], 2)
                        chain(tt(EX, EX, LG[:, :, :], ALU.mult))
                        chain(tt(EX2, EX2, T1, ALU.mult))
                        chain(dve.tensor_reduce(G1[0][:, :], EX, AX.X, ALU.add))
                        chain(dve.tensor_reduce(G1[1][:, :], EX2, AX.X, ALU.add))
                        chain(dve.reciprocal(G1[0][:, :], G1[0][:, :]))
                        chain(dve.reciprocal(G1[1][:, :], G1[1][:, :]))
                        chain(tt(OH1, OH1, wide(G1[0][:, :].unsqueeze(2)), ALU.mult))
                        chain(tt(OH2, OH2, wide(G1[1][:, :].unsqueeze(2)), ALU.mult))
                        tt(T1, OH1, OH2, ALU.subtract).then_inc(s["gates"], 1)
                    else:
                        if l != 3:
                            dve.wait_ge(s["sub"], 1)
                            chain(tt(OH1, OH1, OH2, ALU.add))
                        dve.wait_ge(s["ex"], 1)
                        den = EX
                        if l != 3:
                            chain(tt(EX2, EX, OH1, ALU.mult))
                            top = EX2
                        else:
                            top = EX
                        if l == 0:
                            den = EX2
                        chain(dve.tensor_reduce(G1[0][:, :], den, AX.X, ALU.add))
                        chain(dve.reciprocal(G1[0][:, :], G1[0][:, :]))
                        tt(T1, top, wide(G1[0][:, :].unsqueeze(2)), ALU.mult).then_inc(s["gates"], 1)

                    def gate(e):
                        for h in range(2):
                            x = slice(h * TH, (h + 1) * TH)
                            dve.wait_ge(s["down"], dpe * (e + 1) if gated_out else dpe * (e + 1) - 1 + h)
                            if h == 0:
                                dve.wait_ge(s[f"g_loaded{e}"], 16)
                            if e >= 2:
                                dve.wait_ge(s["added"], 2 * (e - 2) + h + 1)
                            if e == 0:
                                dve.wait_ge(s["g_stored"], 16)
                            y = (PS[2 + e % 2] if gated_out else PS[3])[:, x]
                            o = (YG if e else ACC)[:, x]
                            if gated_out:
                                dve.scalar_tensor_tensor(o, y, col(f"b2_{l}", e), GB[:, e % 2, x], ALU.add, ALU.mult)\
                                   .then_inc(s["y_used"], 1)
                            else:
                                dve.tensor_tensor(o, y, GB[:, e % 2, x], ALU.mult).then_inc(s["y_used"], 1)
                            if e == NE - 1:
                                dve.wait_ge(s["y_used"], 2 * e + h + 1)
                                dve.wait_ge(s["added"], 2 * (e - 1) - 1 + h)
                                dve.tensor_tensor(ACC[:, x], ACC[:, x], o, ALU.add).then_inc(s["summed"], 1)

                    if gated_out:
                        for k in range(units):
                            for h in range(2):
                                u = k % 2 * 2 + h
                                dve.wait_ge(s["h_hi"], 2 * k + h + 1)
                                if k >= 2:
                                    dve.wait_ge(s["down"], k - 1)
                                dve.tensor_tensor(f32r(HLO[:, u, :]), HF[:, u, :], HHI[:, u, :], ALU.subtract)\
                                   .then_inc(s["h_made"], 1)
                            if k % nch == 0 and k > 0:
                                gate(k // nch - 1)
                            if l == 0 and k % nch == 1 and k < units - nch:
                                inputs(k // nch + 1)
                        gate(NE - 1)
                    else:
                        for k in range(units):
                            z = sizes[k % dpe // 2]
                            if prep == 2 and k in PREP_UNITS:
                                c = PREP_UNITS.index(k) + 2
                                prep_vector(dve, s, c, banks(c)[0], parts_of_keys)
                            dve.wait_ge(s["acted"], k + 1)
                            if k >= 3:
                                dve.wait_ge(s["down"], k - 2)
                            full = HF[0:z, k % 3, :]
                            dve.tensor_tensor(full, PS[k % 3][0:z, 512:1024], HG[0:z, k % 2, :],
                                              ALU.mult).then_inc(s["h_full"], 1)
                            dve.wait_ge(s["h_full"], k + 1)
                            dve.tensor_copy(f32r(HHI[0:z, k % 3, :]), full).then_inc(s["h_hi"], 1)
                            dve.wait_ge(s["h_hi"], k + 1)
                            dve.tensor_tensor(f32r(HLO[0:z, k % 3, :]), full, HHI[0:z, k % 3, :], ALU.subtract)\
                               .then_inc(s["h_made"], 1)
                            if k % dpe == 0 and k > 0:
                                gate(k // dpe - 1)
                        gate(NE - 1)
                    dst = XN if final else X
                    if l == 1:
                        dve.wait_ge(s["biased"], 1)
                    for h, tiles in enumerate(HALVES):
                        dve.wait_ge(s["back"], h + 1)
                        o = dst[:, 4 * h:4 * h + 4, :]
                        chain(dve.tensor_tensor(o, PS[0][:, h * TH:(h + 1) * TH].rearrange("p (t e) -> p t e", t=4),
                                                o, ALU.add))
                        norm_stats(dve, s, dst, EPS, tiles, chain)
                    for part, tiles in enumerate(HALVES):
                        norm_scale(dve, s, dst, tiles, part)
                        if final:
                            x = XN[:, 4 * part:4 * part + 4, :]
                            dve.wait_ge(s["norm_rows"], 4 * (part + 1))
                            chain(dve.tensor_tensor(x, x, row("ln2_g").unsqueeze(1).to_broadcast([P, 4, P]), ALU.mult))
                            dve.wait_ge(s["biased"], 1)
                            dve.tensor_tensor(x, x, X[:, 4 * part:4 * part + 4, :], ALU.add).then_inc(s["acc"], 1)

                @block.scalar
                def _(act):
                    for h in range(2):
                        act.wait_ge(s["turned"], h + 1)
                        act.activation(XNT[:, h * TH:(h + 1) * TH], PS[0][:, h * TH:(h + 1) * TH], ACT.Copy)\
                           .then_inc(s["kept"], 1)
                    if not final:
                        prep_scalar(act, s, prep, 0, *banks(0), parts_of_keys)
                        prep_scalar(act, s, prep, 1, *banks(1), parts_of_keys)
                        prep_middle(act, s, 0, parts_of_keys)
                        prep_middle(act, s, 1, parts_of_keys)
                    act.wait_ge(s["sub"], 1)
                    act.activation(GA[3][:, :, :], GA[0][:, :, :], ACT.Exp).then_inc(s["ex"], 1)
                    if l == 2:
                        act.wait_ge(s["sub"], 2)
                        act.activation(GA[5][:, :, :], GA[7][:, :, :], ACT.Exp).then_inc(s["ex"], 1)

                    def keep_keys(k):
                        if not final and k in PREP_UNITS:
                            c = PREP_UNITS.index(k) + 2
                            prep_scalar(act, s, prep, c, *banks(c), parts_of_keys)
                            prep_middle(act, s, c, parts_of_keys)

                    def keep_gates():
                        for h in range(2):
                            act.wait_ge(s["g_turned"], h + 1)
                            act.activation(GT[:, h * TH:(h + 1) * TH], GBANK[0:NE, h * TH:(h + 1) * TH], ACT.Copy)\
                               .then_inc(s["g_kept"], 1)
                        act.wait_ge(s["g_kept"], 2)
                        act.dma_start(g_rows, GT[:, :]).then_inc(s["g_stored"], 16)

                    def loads(k):
                        e, u = k // (units // NE), k % (units // NE)
                        if u == 1 and e + 1 < NE:
                            weights_hi(lambda o, i: act.activation(o, i, ACT.Copy), act, e + 1)
                        if u == 2 and e + 2 < NE:
                            act.wait_ge(s["w_first" if e == 0 else "w_made"], max(e, 1))
                            act.dma_start(W[:, e % 2, 0:EW[l]], d[f"we{l}"][e + 2]).then_inc(s[f"w_loaded{e % 2}"], 16)
                        if k == 4:
                            act.wait_ge(s["g_stored"], 16)
                        if (k == 4) or (u == 1 and e >= (2 if units // NE == 4 else 1)):
                            for i in ((0, 1) if k == 4 and units // NE == 4 else (k // (units // NE),)):
                                if i >= 2:
                                    act.wait_ge(s["y_used"], 2 * (i - 1))
                                act.dma_start(GB[:, i % 2, :], g_rows[i].partition_broadcast(P))\
                                   .then_inc(s[f"g_loaded{i}"], 16)
                    if gated_out:
                        for k in range(units):
                            if k == 2:
                                keep_gates()
                            keep_keys(k)
                            loads(k)
                            if k >= 2:
                                act.wait_ge(s["down"], k - 1)
                                act.wait_ge(s["h_made"], 2 * (k - 1))
                            for h in range(2):
                                act.wait_ge(s["up"], 2 * k + h + 1)
                                act.activation(HF[:, k % 2 * 2 + h, :], PS[k % 2][:, h * TH:(h + 1) * TH],
                                               ACT.Gelu if l == 0 else ACT.Relu, bias=col(f"b1_{l}", k))\
                                   .then_inc(s["acted"], 1)
                            for h in range(2):
                                act.wait_ge(s["acted"], 2 * k + h + 1)
                                act.activation(f32r(HHI[:, k % 2 * 2 + h, :]), HF[:, k % 2 * 2 + h, :], ACT.Copy)\
                                   .then_inc(s["h_hi"], 1)
                    else:
                        for k in range(units):
                            z = sizes[k % (2 * nch) // 2]
                            if k == 2:
                                keep_gates()
                            keep_keys(k)
                            loads(k)
                            act.wait_ge(s["up"], k + 1)
                            if k >= 2:
                                act.wait_ge(s["h_full"], k - 1)
                            act.activation(HG[0:z, k % 2, :], PS[k % 3][0:z, 0:512],
                                           ACT.Gelu if l == 1 else ACT.Silu).then_inc(s["acted"], 1)

                @block.tensor
                def _(pe):
                    turn_rows(pe, s, XN, PS[0], "turned", s["affine"] if final else None)
                    if not final:
                        prep_tensor(pe, s, prep, CTX, 0, *banks(0))
                        prep_tensor(pe, s, prep, CTX, 1, *banks(1))
                    src = XNT
                    pe.wait_ge(s["kept"], 2)
                    if l == 0:
                        pe.wait_ge(s["scaled_r"], 1)
                        src = YG
                    for t in range(NT):
                        ins = pe.matmul(PS[1][:, t * NE:(t + 1) * NE], src[:, t * P:(t + 1) * P], WR[:, l, :],
                                        start=True, stop=True)
                    ins.then_inc(s["routed"], 1)

                    def make_keys(k):
                        if not final and k in PREP_UNITS:
                            c = PREP_UNITS.index(k) + 2
                            if gated_out:
                                pe.wait_ge(s["g_kept"], 2)
                                pe.wait_ge(s["k_kept"], c)
                                pe.wait_ge(s["v_kept"], c)
                            else:
                                pe.wait_ge(s["h_full"], k - 2)
                            prep_tensor(pe, s, prep, CTX, c, *banks(c))

                    def turn_gates():
                        if not final:
                            pe.wait_ge(s["k_kept"], 2)
                            pe.wait_ge(s["v_kept"], 2)
                        pe.wait_ge(s["gates"], 1)
                        for t in range(NT):
                            ins = pe.transpose(GBANK[0:NE, t * P:(t + 1) * P], GA[6][:, t, :], IDF[:, :])
                            if t % 4 == 3:
                                ins.then_inc(s["g_turned"], 1)

                    def operands(e):
                        pe.wait_ge(s["w_made" if e else "w_first"], max(e, 1))
                        pe.wait_ge(s["x_made"], e + 1 if l == 0 else 1)

                    if gated_out:
                        def up(k):
                            e, c = k // nch, k % nch
                            if c == 0:
                                operands(e)
                            if k == 1:
                                pe.wait_ge(s["lg_read"], 1)
                            if k >= 2:
                                pe.wait_ge(s["acted"], 2 * (k - 1))
                            i, w = e % 2 if l == 0 else 0, slice(c * P, (c + 1) * P)
                            for h in range(2):
                                x = slice(h * TH, (h + 1) * TH)
                                product(pe, PS[k % 2][:, x], WHI[:, e % 3, w], WLO[:, e % 3, w],
                                        XHI[:, i, x], XLO[:, i, x], True, True).then_inc(s["up"], 1)

                        def down(k):
                            e, c = k // nch, k % nch
                            if c == 0 and e < 2 and not final:
                                pe.wait_ge(s["k_kept"], 2 * (e + 1))
                                pe.wait_ge(s["v_kept"], 2 * (e + 1))
                            if c == 0 and e == 1:
                                pe.wait_ge(s["g_kept"], 2)
                            if c == 0 and e >= 2:
                                pe.wait_ge(s["y_used"], 2 * (e - 1))
                            w = slice((nch + c) * P, (nch + c + 1) * P)
                            for h in range(2):
                                u = k % 2 * 2 + h
                                pe.wait_ge(s["h_made"], 2 * k + h + 1)
                                ins = product(pe, PS[2 + e % 2][:, h * TH:(h + 1) * TH], WHI[:, e % 3, w],
                                              WLO[:, e % 3, w], HHI[:, u, :], HLO[:, u, :], c == 0, c == nch - 1)
                            ins.then_inc(s["down"], 1)
                        up(0)
                        for k in range(units):
                            if k + 1 < units:
                                up(k + 1)
                            down(k)
                            if k == 0:
                                turn_gates()
                            make_keys(k + 2)
                    else:
                        def up(k):
                            e, c, h = k // (2 * nch), k % (2 * nch) // 2, k % 2
                            z = sizes[c]
                            if k % (2 * nch) == 0:
                                operands(e)
                            if k == 1:
                                pe.wait_ge(s["lg_read"], 1)
                            if k == 2:
                                turn_gates()
                                pe.wait_ge(s["g_kept"], 2)
                            if k == 2 or k in PREP_UNITS:
                                n = 2 if k == 2 else PREP_UNITS.index(k) + 3
                                pe.wait_ge(s["k_kept"], n)
                                pe.wait_ge(s["v_kept"], n)
                            if k >= 3:
                                pe.wait_ge(s["h_full"], k - 2)
                            x = slice(h * TH, (h + 1) * TH)
                            for i in range(2):
                                w = slice(i * hid + c * P, i * hid + c * P + z)
                                ins = product(pe, PS[k % 3][0:z, i * 512:(i + 1) * 512], WHI[:, e % 3, w],
                                              WLO[:, e % 3, w], XHI[:, 0, x], XLO[:, 0, x], True, True)
                            ins.then_inc(s["up"], 1)

                        def down(k):
                            e, c, h = k // (2 * nch), k % (2 * nch) // 2, k % 2
                            z = sizes[c]
                            pe.wait_ge(s["h_made"], k + 1)
                            if c == 0 and e >= 1:
                                pe.wait_ge(s["y_used"], 2 * (e - 1) + h + 1)
                            w = slice(2 * hid + c * P, 2 * hid + (c + 1) * P)
                            product(pe, PS[3][:, h * TH:(h + 1) * TH], WHI[0:z, e % 3, w], WLO[0:z, e % 3, w],
                                    HHI[0:z, k % 3, :], HLO[0:z, k % 3, :], c == 0, c == nch - 1)\
                                .then_inc(s["down"], 1)
                        up(0)
                        up(1)
                        for k in range(units):
                            make_keys(k + 2)
                            if k + 2 in PREP_UNITS:
                                down(k)
                                up(k + 2)
                            else:
                                if k + 2 < units:
                                    up(k + 2)
                                down(k)
                    for t in range(NT):
                        if t % 4 == 0:
                            pe.wait_ge(s["summed"], t // 4 + 1)
                        ins = pe.transpose(PS[0][:, t * P:(t + 1) * P], ACC[:, t * P:(t + 1) * P], IDF[:, :])
                        if t % 4 == 3:
                            ins.then_inc(s["back"], 1)
            mem.close()


        def convolution():
            s = signals(nc, "conv", "turned padded border made kept back rows", before)
            own_tensor, mem = phase_memory("conv")
            XPAD = own_tensor("XPAD", [P, B, SQ + 2])
            with nc.Block() as block:
                @block.gpsimd
                def _(pool):
                    for i in (0, SQ + 1):
                        pool.memset(XPAD[:, :, i:i + 1], 0.0).then_inc(s["border"], 1)

                @block.vector
                def _(dve):
                    for h in range(2):
                        dve.wait_ge(s["back"], h + 1)
                        dve.tensor_copy(XN[:, 4 * h:4 * h + 4, :],
                                        PS[0][:, h * TH:(h + 1) * TH].rearrange("p (t e) -> p t e", t=4))\
                           .then_inc(s["rows"], 1)

                @block.scalar
                def _(act):
                    for h in range(2):
                        act.wait_ge(s["turned"], h + 1)
                        act.activation(XPAD[:, 2 * h:2 * h + 2, 1:SQ + 1],
                                       PS[0][:, h * TH:(h + 1) * TH].rearrange("p (b n) -> p b n", b=2), ACT.Copy)\
                           .then_inc(s["padded"], 1)
                    for h in range(2):
                        act.wait_ge(s["made"], h + 1)
                        act.activation(XNT[:, h * TH:(h + 1) * TH], PS[1][:, h * TH:(h + 1) * TH], ACT.Identity,
                                       bias=col("conv_b")).then_inc(s["kept"], 1)

                @block.tensor
                def _(pe):
                    turn_rows(pe, s, XN, PS[0], "turned")
                    pe.wait_ge(s["border"], 2)
                    for h in range(2):
                        pe.wait_ge(s["padded"], h + 1)
                        for i in range(3):
                            ins = pe.matmul(PS[1][:, h * TH:(h + 1) * TH], WCONV[:, i, :],
                                            XPAD[:, 2 * h:2 * h + 2, i:i + SQ], start=(i == 0), stop=(i == 2))
                        ins.then_inc(s["made"], 1)
                    for h in range(2):
                        pe.wait_ge(s["kept"], h + 1)
                        for t in range(4 * h, 4 * h + 4):
                            ins = pe.transpose(PS[0][:, t * P:(t + 1) * P], XNT[:, t * P:(t + 1) * P], IDF[:, :])
                        ins.then_inc(s["back"], 1)
            mem.close()

        for l in range(4):
            attention(l)
            if l == 3:
                convolution()
                attention(4)
            experts(l)



def kernel(**inputs):
    import concourse.bacc as _bacc
    from concourse.bass_utils import run_bass_kernel_spmd as _run

    x = {k: np.asarray(v) for k, v in inputs.items()}
    f32 = np.float32
    zeros = np.zeros(P, f32)
    order = np.array([(2 * p + m) * DH + e for m in range(2) for e in range(DH) for p in range(NP)])
    wqkv, bqkv = x["L3_ffn_wqkv"], x["L3_ffn_bqkv"]
    w = [[x["L0_xattn_Wq"].T, x["L0_xattn_Wk"].T, x["L0_xattn_Wv"].T, x["L0_xattn_Wo"].T],
         [x["L1_xattn_Wq"].T, x["L1_xattn_Wk"].T, x["L1_xattn_Wv"].T, x["L1_xattn_Wo"].T],
         [x["L2_xattn_Wq"], x["L2_xattn_Wk"], x["L2_xattn_Wv"], x["L2_xattn_Wo"]],
         [x["L3_xattn_wq_w"].T, x["L3_xattn_wk_w"].T, x["L3_xattn_wv_w"].T, x["L3_xattn_proj_w"].T],
         [wqkv[0:P].T, wqkv[P:2 * P].T, wqkv[2 * P:].T, x["L3_ffn_wo"].T]]
    bq = [zeros, x["L1_xattn_bq"], zeros, x["L3_xattn_wq_b"], bqkv[0:P]]
    bk = [zeros, x["L1_xattn_bk"], zeros, x["L3_xattn_wk_b"], bqkv[P:2 * P]]
    bv = [zeros, x["L1_xattn_bv"], zeros, x["L3_xattn_wv_b"], bqkv[2 * P:]]
    bo = [zeros, x["L1_xattn_bo"], x["L2_xattn_bo"], x["L3_xattn_proj_b"], x["L3_ffn_bo"]]
    wattn = np.stack([np.stack([q[:, order], k[:, order], v, o], 1) for q, k, v, o in w], 1)
    cols = [b[order] for b in bq] + [b[order] for b in bk] + bv
    cols += [x["L3_ffn_conv_b"], x["L0_ffn_router_ln_scale"], x["L0_ffn_router_ln_bias"]]
    cols += list(x["L0_ffn_expert_ln_scale"]) + list(x["L0_ffn_expert_ln_bias"])
    cols += list(x["L0_ffn_b1"].reshape(-1, P)) + list(x["L3_ffn_b1"].reshape(-1, P))
    cols += list(x["L0_ffn_b2"]) + list(x["L3_ffn_b2"])
    rows = bo + [x["L1_ffn_bias"], x["L0_ffn_router_b"], x["L3_ffn_gate_b"], x["L3_ffn_ln1_g"], x["L3_ffn_ln1_b"],
                 x["L3_ffn_ln2_g"], x["L3_ffn_ln2_b"]]

    def tiles(a):
        n = -(-a.shape[1] // P)
        full = np.zeros((a.shape[0], n * P, a.shape[2]), a.dtype)
        full[:, 0:a.shape[1]] = a
        return full.reshape(a.shape[0], n, P, -1).transpose(0, 2, 1, 3).reshape(a.shape[0], P, -1)

    t = (0, 2, 1)
    we = [np.concatenate([x["L0_ffn_w1"].transpose(t), tiles(x["L0_ffn_w2"].transpose(t))], 2),
          np.concatenate([x["L1_ffn_w1"], x["L1_ffn_v1"], tiles(x["L1_ffn_w2"])], 2),
          np.concatenate([x["L2_ffn_w_gate"].transpose(t), x["L2_ffn_w_up"].transpose(t),
                          tiles(x["L2_ffn_w_down"].transpose(t))], 2),
          np.concatenate([x["L3_ffn_w1"], tiles(x["L3_ffn_w2"])], 2)]
    data = {
        "x": x["x"].reshape(T, P),
        "ctxT": x["ctx_1024"].reshape(TK, P).T,
        "mask0": x["mask_Bx1x1xS2_bf1"].reshape(1, TK),
        "mask_keys": x["mask_BxS2_bk0"].reshape(TK),
        "mask2": x["mask_SxS2_bk1"],
        "mask2T": x["mask_SxS2_bk1"].T,
        "wattn": wattn,
        "cols": np.stack(cols, 1),
        "rows": np.concatenate(rows),
        "wconv": x["L3_ffn_conv_w"].transpose(1, 2, 0),
        "wrouter": np.stack([x["L0_ffn_router_w"].T, x["L1_ffn_router_w"], x["L2_ffn_router_w"].T,
                             x["L3_ffn_gate_w"]], 1),
        "we0": we[0], "we1": we[1], "we2": we[2], "we3": we[3],
    }
    nc = _bacc.Bacc("TRN2", target_bir_lowering=False, num_devices=1)
    arrays, args = {}, {}
    for name, a in data.items():
        a = np.ascontiguousarray(a)
        arrays[f"in_{name}"] = a
        args[name] = nc.dram_tensor(f"in_{name}", a.shape, mybir.dt.from_np(a.dtype), kind="ExternalInput").ap()
    out = nc.dram_tensor("out", (T, P), F32, kind="ExternalOutput").ap()
    build(nc, args, out)
    r = _run(nc, [arrays], core_ids=[0])
    return r.results[0]["out"].reshape(B, SQ, P)
```
